# Optimizing a Trainium2 kernel written in Bass

```python
import numpy as np
import jax
import jax.numpy as jnp

def _softmax(x, axis=-1):
    return jax.nn.softmax(x, axis=axis)

def _gelu(x):
    return jax.nn.gelu(x, approximate=True)

def _silu(x):
    return jax.nn.silu(x)

def _sigmoid(x):
    return jax.nn.sigmoid(x)

def _layernorm(x, axis=-1, eps=1e-05):
    m = jnp.mean(x, axis=axis, keepdims=True)
    v = jnp.var(x, axis=axis, keepdims=True)
    return (x - m) / jnp.sqrt(v + eps)

def _scatter_add(tgt, idx, src, axis=0):
    return tgt.at[idx].add(src)

def _segment_sum(src, seg, n):
    return jax.ops.segment_sum(src, seg, n)
kernel_name = 'mk_sandwich_d1_jaxref_r8_62fee7'

def setup_inputs(seed: int=0):
    np.random.seed(seed)
    _w = jnp.asarray

    def _L0_attn_setup():
        import jax, jax.numpy as jnp
        import numpy as np
        N_EMBD = 128
        N_HEAD = 16
        HEAD_DIM = 64
        KERNEL = 4
        B, T = (2, 256)
        EPS = 1e-06

        def group_rmsnorm(x, weight, num_groups, eps=EPS):
            shp = x.shape
            gs = shp[-1] // num_groups
            xg = x.reshape(shp[:-1] + (num_groups, gs))
            rms = jnp.sqrt(jnp.mean(jnp.square(xg.astype(jnp.float32)), axis=-1, keepdims=True) + eps)
            return (xg / rms).reshape(shp) * weight

        def short_conv(x, w):
            C = x.shape[-1]
            K = w.shape[-1]
            xt = jnp.transpose(x, (0, 2, 1))
            out = jax.lax.conv_general_dilated(xt, w[:, None, :], window_strides=(1,), padding=[(K - 1, 0)], feature_group_count=C)
            out = jax.nn.silu(out)
            return jnp.transpose(out, (0, 2, 1))
        key = jax.random.key(seed)
        ks = jax.random.split(key, 12)
        s = 0.02
        D = N_EMBD
        QD = N_HEAD * HEAD_DIM
        return {'x': jax.random.normal(ks[0], (B, T, D), dtype=jnp.float32), 'Wq': jax.random.normal(ks[1], (D, QD), dtype=jnp.float32) * s, 'Wk': jax.random.normal(ks[2], (D, QD), dtype=jnp.float32) * s, 'Wv': jax.random.normal(ks[3], (D, QD), dtype=jnp.float32) * s, 'Wo': jax.random.normal(ks[4], (QD, D), dtype=jnp.float32) * s, 'Wf': jax.random.normal(ks[5], (D, N_HEAD), dtype=jnp.float32) * s, 'bf': jnp.full((N_HEAD,), 2.0, dtype=jnp.float32), 'Wg': jax.random.normal(ks[6], (D, QD), dtype=jnp.float32) * s, 'qnw': jnp.ones((QD,), dtype=jnp.float32), 'knw': jnp.ones((QD,), dtype=jnp.float32), 'onw': jnp.ones((HEAD_DIM,), dtype=jnp.float32), 'kconv_w': jax.random.normal(ks[7], (QD, KERNEL), dtype=jnp.float32) * (1.0 / np.sqrt(KERNEL)), 'vconv_w': jax.random.normal(ks[8], (QD, KERNEL), dtype=jnp.float32) * (1.0 / np.sqrt(KERNEL))}
    _L0_attn_in = _L0_attn_setup()

    def _L0_ffn_setup():
        import jax, jax.numpy as jnp
        import numpy as np
        DIM = 128
        HEADS = 16
        HD = DIM // HEADS
        M = 32
        E = 4
        K = 2
        HID = 256
        MID = 256
        LB = 0.01
        EPS = 1.1920929e-07

        def _rms(x, w):
            return x * jax.lax.rsqrt(jnp.mean(x * x, axis=-1, keepdims=True) + EPS) * w

        def _gelu(x):
            return jax.nn.gelu(x, approximate=False)
        key = jax.random.key(seed)
        ks = jax.random.split(key, 20)
        d = DIM
        w = lambda k, s: jax.random.normal(k, s, jnp.float32) * 0.02
        return {'x': jax.random.normal(ks[0], (4, 128, d), jnp.float32), 'n1_w': jnp.ones((d,), jnp.float32), 'n2_w': jnp.ones((d,), jnp.float32), 'wq': w(ks[1], (d, d)), 'wk': w(ks[2], (d, d)), 'wv': w(ks[3], (d, d)), 'wo': w(ks[4], (d, d)), 'qn_w': jnp.ones((HD,), jnp.float32), 'kn_w': jnp.ones((HD,), jnp.float32), 'gate_w': w(ks[5], (E, d)), 'e0_up': w(ks[6], (HID, d)), 'e0_down': w(ks[7], (d, HID)), 'e1_w1': w(ks[8], (HID, d)), 'e1_w2': w(ks[9], (HID, d)), 'e1_down': w(ks[10], (d, HID)), 'e2_l1': w(ks[11], (MID, d)), 'e2_l2': w(ks[12], (HID, MID)), 'e2_l3': w(ks[13], (MID, HID)), 'e2_l4': w(ks[14], (d, MID)), 'e3_down': w(ks[15], (d, d)), 'e3_up': w(ks[16], (HID, d)), 'e3_out': w(ks[17], (d, HID))}
    _L0_ffn_in = _L0_ffn_setup()
    _d = {'L0_attn_x': _L0_attn_in['x'], 'L0_attn_Wq': _L0_attn_in['Wq'], 'L0_attn_Wk': _L0_attn_in['Wk'], 'L0_attn_Wv': _L0_attn_in['Wv'], 'L0_attn_Wo': _L0_attn_in['Wo'], 'L0_attn_Wf': _L0_attn_in['Wf'], 'L0_attn_bf': _L0_attn_in['bf'], 'L0_attn_Wg': _L0_attn_in['Wg'], 'L0_attn_qnw': _L0_attn_in['qnw'], 'L0_attn_knw': _L0_attn_in['knw'], 'L0_attn_onw': _L0_attn_in['onw'], 'L0_attn_kconv_w': _L0_attn_in['kconv_w'], 'L0_attn_vconv_w': _L0_attn_in['vconv_w'], 'L0_ffn_n1_w': _L0_ffn_in['n1_w'], 'L0_ffn_n2_w': _L0_ffn_in['n2_w'], 'L0_ffn_wq': _L0_ffn_in['wq'], 'L0_ffn_wk': _L0_ffn_in['wk'], 'L0_ffn_wv': _L0_ffn_in['wv'], 'L0_ffn_wo': _L0_ffn_in['wo'], 'L0_ffn_qn_w': _L0_ffn_in['qn_w'], 'L0_ffn_kn_w': _L0_ffn_in['kn_w'], 'L0_ffn_gate_w': _L0_ffn_in['gate_w'], 'L0_ffn_e0_up': _L0_ffn_in['e0_up'], 'L0_ffn_e0_down': _L0_ffn_in['e0_down'], 'L0_ffn_e1_w1': _L0_ffn_in['e1_w1'], 'L0_ffn_e1_w2': _L0_ffn_in['e1_w2'], 'L0_ffn_e1_down': _L0_ffn_in['e1_down'], 'L0_ffn_e2_l1': _L0_ffn_in['e2_l1'], 'L0_ffn_e2_l2': _L0_ffn_in['e2_l2'], 'L0_ffn_e2_l3': _L0_ffn_in['e2_l3'], 'L0_ffn_e2_l4': _L0_ffn_in['e2_l4'], 'L0_ffn_e3_down': _L0_ffn_in['e3_down'], 'L0_ffn_e3_up': _L0_ffn_in['e3_up'], 'L0_ffn_e3_out': _L0_ffn_in['e3_out']}
    _x0 = _d['L0_attn_x']
    _d['L0_attn_x'] = jax.random.normal(jax.random.fold_in(jax.random.key(seed), 1), (32, 256, 128), dtype=_x0.dtype)
    del _x0
    return _d

def reference(L0_attn_x, L0_attn_Wq, L0_attn_Wk, L0_attn_Wv, L0_attn_Wo, L0_attn_Wf, L0_attn_bf, L0_attn_Wg, L0_attn_qnw, L0_attn_knw, L0_attn_onw, L0_attn_kconv_w, L0_attn_vconv_w, L0_ffn_n1_w, L0_ffn_n2_w, L0_ffn_wq, L0_ffn_wk, L0_ffn_wv, L0_ffn_wo, L0_ffn_qn_w, L0_ffn_kn_w, L0_ffn_gate_w, L0_ffn_e0_up, L0_ffn_e0_down, L0_ffn_e1_w1, L0_ffn_e1_w2, L0_ffn_e1_down, L0_ffn_e2_l1, L0_ffn_e2_l2, L0_ffn_e2_l3, L0_ffn_e2_l4, L0_ffn_e3_down, L0_ffn_e3_up, L0_ffn_e3_out):

    def _L0_attn_ref(x, Wq, Wk, Wv, Wo, Wf, bf, Wg, qnw, knw, onw, kconv_w, vconv_w):
        import jax, jax.numpy as jnp
        import numpy as np
        N_EMBD = 128
        N_HEAD = 16
        HEAD_DIM = 64
        KERNEL = 4
        B, T = (2, 256)
        EPS = 1e-06

        def group_rmsnorm(x, weight, num_groups, eps=EPS):
            shp = x.shape
            gs = shp[-1] // num_groups
            xg = x.reshape(shp[:-1] + (num_groups, gs))
            rms = jnp.sqrt(jnp.mean(jnp.square(xg.astype(jnp.float32)), axis=-1, keepdims=True) + eps)
            return (xg / rms).reshape(shp) * weight

        def short_conv(x, w):
            C = x.shape[-1]
            K = w.shape[-1]
            xt = jnp.transpose(x, (0, 2, 1))
            out = jax.lax.conv_general_dilated(xt, w[:, None, :], window_strides=(1,), padding=[(K - 1, 0)], feature_group_count=C)
            out = jax.nn.silu(out)
            return jnp.transpose(out, (0, 2, 1))
        Bx, Tx, C = x.shape
        H, Dh = (N_HEAD, HEAD_DIM)
        scale = 1.0 / np.sqrt(Dh)
        q = x @ Wq
        k = x @ Wk
        v = x @ Wv
        k = short_conv(k, kconv_w)
        v = short_conv(v, vconv_w)
        q = group_rmsnorm(q, qnw, H)
        k = group_rmsnorm(k, knw, H)
        fgate_logits = x @ Wf + bf
        log_fgate = jax.nn.log_sigmoid(fgate_logits)
        cum = jnp.cumsum(log_fgate, axis=1)
        cum = jnp.transpose(cum, (0, 2, 1))
        qh = jnp.transpose(q.reshape(Bx, Tx, H, Dh), (0, 2, 1, 3))
        kh = jnp.transpose(k.reshape(Bx, Tx, H, Dh), (0, 2, 1, 3))
        vh = jnp.transpose(v.reshape(Bx, Tx, H, Dh), (0, 2, 1, 3))
        scores = jnp.einsum('bhtd,bhsd->bhts', qh, kh) * scale
        decay = cum[:, :, :, None] - cum[:, :, None, :]
        scores = scores + decay
        causal = jnp.tril(jnp.ones((Tx, Tx), dtype=bool))
        scores = jnp.where(causal, scores, -jnp.inf)
        attn = jax.nn.softmax(scores, axis=-1)
        out = jnp.einsum('bhts,bhsd->bhtd', attn, vh)
        out = jnp.transpose(out, (0, 2, 1, 3))
        g = (x @ Wg).reshape(Bx, Tx, H, Dh)
        rms = jnp.sqrt(jnp.mean(jnp.square(out.astype(jnp.float32)), axis=-1, keepdims=True) + EPS)
        out = out / rms * onw * (g * jax.nn.sigmoid(g))
        out = out.reshape(Bx, Tx, H * Dh) @ Wo
        return out

    def _L0_ffn_ref(x, n1_w, n2_w, wq, wk, wv, wo, qn_w, kn_w, gate_w, e0_up, e0_down, e1_w1, e1_w2, e1_down, e2_l1, e2_l2, e2_l3, e2_l4, e3_down, e3_up, e3_out):
        import jax, jax.numpy as jnp
        import numpy as np
        DIM = 128
        HEADS = 16
        HD = DIM // HEADS
        M = 32
        E = 4
        K = 2
        HID = 256
        MID = 256
        LB = 0.01
        EPS = 1.1920929e-07

        def _rms(x, w):
            return x * jax.lax.rsqrt(jnp.mean(x * x, axis=-1, keepdims=True) + EPS) * w

        def _gelu(x):
            return jax.nn.gelu(x, approximate=False)
        B, T, C = x.shape
        h = _rms(x, n1_w)
        heads = lambda w_: (h @ w_.T).reshape(B, T, HEADS, HD).transpose(0, 2, 1, 3)
        q = _rms(heads(wq), qn_w)
        k = _rms(heads(wk), kn_w)
        v = heads(wv)
        scores = jnp.einsum('bhqd,bhkd->bhqk', q, k) * HD ** (-0.5)
        causal = jnp.tril(jnp.ones((T, T), bool))
        scores = jnp.where(causal[None, None], scores, -jnp.inf)
        attn = jax.nn.softmax(scores, axis=-1)
        ao = jnp.einsum('bhqk,bhkd->bhqd', attn, v).transpose(0, 2, 1, 3).reshape(B, T, C) @ wo.T
        ao = ao.at[:, :, :M].set(0.0)
        x = x + ao
        xf = _rms(x, n2_w).reshape(-1, C)
        N = xf.shape[0]
        logits = jnp.nan_to_num(xf @ gate_w.T)
        probs = jax.nn.softmax(logits, axis=-1)
        topv, topi = jax.lax.top_k(probs, K)
        topv = topv / (topv.sum(-1, keepdims=True) + 1e-08)
        wts = jnp.zeros((N, E), x.dtype).at[jnp.arange(N)[:, None], topi].add(topv)
        o0 = _gelu(xf @ e0_up.T) @ e0_down.T
        o1 = jax.nn.silu(xf @ e1_w1.T) * (xf @ e1_w2.T) @ e1_down.T
        o2 = _gelu(_gelu(_gelu(xf @ e2_l1.T) @ e2_l2.T) @ e2_l3.T) @ e2_l4.T
        o3 = _gelu(_gelu(xf @ e3_down.T) @ e3_up.T) @ e3_out.T
        moe = wts[:, 0:1] * o0 + wts[:, 1:2] * o1 + wts[:, 2:3] * o2 + wts[:, 3:4] * o3
        moe = moe.reshape(B, T, C).at[:, :, :M].set(0.0)
        return x + moe
    x = L0_attn_x
    x = x + _layernorm(_L0_attn_ref(_layernorm(x, axis=-1), L0_attn_Wq, L0_attn_Wk, L0_attn_Wv, L0_attn_Wo, L0_attn_Wf, L0_attn_bf, L0_attn_Wg, L0_attn_qnw, L0_attn_knw, L0_attn_onw, L0_attn_kconv_w, L0_attn_vconv_w), axis=-1)
    x = x + _layernorm(_L0_ffn_ref(_layernorm(x, axis=-1), L0_ffn_n1_w, L0_ffn_n2_w, L0_ffn_wq, L0_ffn_wk, L0_ffn_wv, L0_ffn_wo, L0_ffn_qn_w, L0_ffn_kn_w, L0_ffn_gate_w, L0_ffn_e0_up, L0_ffn_e0_down, L0_ffn_e1_w1, L0_ffn_e1_w2, L0_ffn_e1_down, L0_ffn_e2_l1, L0_ffn_e2_l2, L0_ffn_e2_l3, L0_ffn_e2_l4, L0_ffn_e3_down, L0_ffn_e3_up, L0_ffn_e3_out), axis=-1)
    return x

_drawn_inputs = setup_inputs


def setup_inputs(seed=0):
    import zlib

    import numpy as np

    out = dict(_drawn_inputs(seed))
    spreads = {'L0_attn_bf': (2.0, 0.2),
     'L0_attn_qnw': (1.0, 0.2),
     'L0_attn_knw': (1.0, 0.2),
     'L0_attn_onw': (1.0, 0.2),
     'L0_ffn_n1_w': (1.0, 0.6),
     'L0_ffn_n2_w': (1.0, 0.6),
     'L0_ffn_qn_w': (1.0, 0.6),
     'L0_ffn_kn_w': (1.0, 0.6)}
    factors = {'L0_ffn_wq': 8.0,
     'L0_ffn_wk': 8.0,
     'L0_ffn_wv': 8.0,
     'L0_ffn_wo': 8.0,
     'L0_ffn_gate_w': 8.0,
     'L0_ffn_e0_up': 8.0,
     'L0_ffn_e0_down': 8.0,
     'L0_ffn_e1_w1': 8.0,
     'L0_ffn_e1_w2': 8.0,
     'L0_ffn_e1_down': 8.0,
     'L0_ffn_e2_l1': 8.0,
     'L0_ffn_e2_l2': 8.0,
     'L0_ffn_e2_l3': 8.0,
     'L0_ffn_e2_l4': 8.0,
     'L0_ffn_e3_down': 8.0,
     'L0_ffn_e3_up': 8.0,
     'L0_ffn_e3_out': 8.0}
    for name, (base, spread) in spreads.items():
        noise = np.random.default_rng([zlib.crc32(name.encode()), seed]).standard_normal(out[name].shape)
        drawn = base * np.exp(spread * noise) if base else spread * noise
        out[name] = jnp.asarray(drawn.astype(out[name].dtype))
    for name, factor in factors.items():
        out[name] = (out[name] * factor).astype(out[name].dtype)
    return out
```

```python
from contextlib import ExitStack

import numpy as np

import concourse.bass as bass
from concourse import mybir

F32 = mybir.dt.float32
F16 = mybir.dt.float16
BF16 = mybir.dt.bfloat16
ALU = mybir.AluOpType
ACT = mybir.ActivationFunctionType
X = mybir.AxisListType.X

P = 128
D = 128
T = 256
TT = T // P
H, DH = 16, 64
C = H * DH
CT = C // P
TAPS = 4
HB, DB = 16, 8
SLOT = 32
NE = 4
HID = 256
MUTE = 32
PAIRS = H // 2
HALF = 512
MASKED = -1.0e30
LN_EPS = 1e-5
EPS_A = 1e-6
EPS_B = 1.1920929e-07
SERIES = [1.0 / (2 * k + 1) for k in range(8, 0, -1)]

WORK_A = (["xT", "gate_logits"] + [f"{m}0{h}" for m in "kvqg" for h in range(2)]
          + ["cum"] + [f"{m}1{h}" for m in "kvqg" for h in range(2)]
          + [f"kT{u}" for u in range(4)] + [f"qT{u}" for u in range(4)]
          + [f"yT{u}" for u in range(4)] + ["attn_out"])
WORK_B = (["hT", "qkv0", "qkv1", "qpT", "kpT", "aT", "wo0", "wo1", "xfT", "route",
           "e0", "e1a", "e1b", "e2a", "e3a", "e2b", "e3b", "e2c", "down0", "down1"])


class Segment:

    def __init__(self, name, reg, offset):
        self.name, self.reg, self.offset = name, reg, offset

    def scaled(self, per, const):
        return const if self.reg is None else self.reg * per + const

    def of(self, signal, n):
        return self.scaled(signal.per, self.offset[signal.block] * signal.per + n)


class Signal:

    def __init__(self, sem, block, per):
        self.sem, self.block, self.per = sem, block, per


class Ring:

    def __init__(self, size, uses_a, uses_b, trips):
        both = uses_b + uses_a
        assert len(both) % size == 0
        self.size, self.order = size, {"first": uses_a, "second": both, "loop": both, "last": uses_b}
        self.base = {"first": 0, "second": len(uses_a), "loop": len(uses_a), "last": len(uses_a) + (trips + 1) * len(both)}
        self.step = len(both) // size

    def place(self, seg, name):
        n = self.base[seg.name] + self.order[seg.name].index(name)
        return n % self.size, seg.scaled(self.step, n // self.size)


def build(nc, x_in, w, out):
    NB = x_in.shape[0]
    trips = NB - 2
    with ExitStack() as ctx:
        def sb(name, shape, dt=F32):
            return ctx.enter_context(nc.sbuf_tensor(name, shape, dt))

        def psum(name, shape, dt=F32):
            return ctx.enter_context(nc.psum_tensor(name, shape, dt))

        def sem(name):
            return ctx.enter_context(nc.semaphore(name))

        def signal(name, block, per):
            return Signal(sem(name), block, per)

        work_banks = [psum(f"work{i}", [P, HALF]) for i in range(2)]
        score_banks = [psum(f"scores{i}", [P, 2, HALF]) for i in range(2)]
        out_banks = [psum(f"pv{i}", [P, HALF]) for i in range(2)]

        ident = sb("ident", [P, P])
        ident16 = sb("ident16", [P, P], F16)
        identb = sb("identb", [P, P], BF16)
        mask = sb("mask", [P, P], BF16)
        tri = sb("tri", [P, T])
        before = sb("before", [P, TT, NE, NE])
        mhalf = sb("mhalf", [P, 64])
        eps = {n: sb(f"eps_{n}", [P, 64]) for n in ("ln", "k", "q", "z", "qk_b", "xf")}
        eps_value = {"ln": LN_EPS, "k": 4 * DH * EPS_A, "q": DH * EPS_A, "z": EPS_B, "qk_b": DB * EPS_B,
                     "xf": D * EPS_B}
        mark = sb("mark", [P, 1])
        bf_rows = sb("bf_rows", [P, H])
        wqk = sb("wqk", [P, CT])
        w8 = sb("w8", [P, HB, DB])

        proj = {m: sb(f"w_{m}", [P, 2, TAPS if m in "kv" else 1, C], F16) for m in "kvqg"}
        wf = sb("wf", [P, 2, H], F16)
        wo_a = sb("wo_a", [P, CT, D])
        wqkv = sb("wqkv", [P, 3 * D])
        wo_b = sb("wo_b", [P, D])
        gate_w = sb("gate_wT", [P, NE])
        up0, up1, up2, l1 = (sb(n, [P, HID]) for n in ("e0_upT", "e1_w1T", "e1_w2T", "e2_l1T"))
        l2, l3 = (sb(n, [P, 2, HID]) for n in ("e2_l2T", "e2_l3T"))
        e3d = sb("e3_downT", [P, D])
        e3u = sb("e3_upT", [P, HID])
        downs = [sb(f"down{e}T", [P, 2, D]) for e in range(NE)]

        arena = sb("arena", [P, 6 * 2048])
        o_sb = sb("o_sb", [P, TT, H, DH + 1])

        def region(i):
            return arena[:, i * 2048:(i + 1) * 2048]

        def tokens(ap, c=C):
            return ap.rearrange("p (t c) -> p t c", t=TT)

        def channels(ap):
            return ap.rearrange("p (c t) -> p c t", c=CT)

        ks, qs, gs = tokens(region(0)), tokens(region(1)), tokens(region(2))
        ksq, qsq = tokens(o_sb[:].rearrange("p t h d -> p (t h d)")[:, 0:TT * C]), tokens(region(3))
        qT, kT = channels(region(4)), channels(region(5))
        y, osq, yT = ks, qs, kT
        x_load = sb("x_load", [P, TT, D])
        x_keep = sb("x_keep", [P, TT, D])
        xn = sb("xn", [P, TT, D])
        xh = sb("xh", [P, TAPS - 1 + T], F16)
        xl = sb("xl", [P, TAPS - 1 + T], F16)
        tanh_a = sb("tanh_a", [P, 2, HALF])
        vs = sb("vs", [P, TT, H, DH + 1])
        probs = [sb(f"probs{i}", [P, 2, 3 * P]) for i in range(2)]
        fz, fneg, fe, fd, fr, fw, fw2, fq, fmin, fl = (sb(f"f{i}", [P, TT, H]) for i in range(10))
        c_res = sb("c_res", [H, T])
        c_res2 = sb("c_res2", [H, T])
        c_parts = sb("c_parts", [H, 3, T], BF16)
        dec_k = sb("dec_k", [6, H, T], BF16)
        dec_q = sb("dec_q", [6, H, T], BF16)
        c_dram = nc.dram_tensor("c_scratch", (2, H, 3, T), BF16, kind="Internal").ap()
        stats_a = sb("stats_a", [P, TT, 6])
        mv_a = sb("mv_a", [P, TT, 2])
        rs_a = sb("rs_a", [P, TT])
        t_a = sb("t_a", [P, TT])
        stats_o = sb("stats_o", [P, TT, 6])
        mv_o = sb("mv_o", [P, TT, 2])
        rs_o = sb("rs_o", [P, TT])
        t_o = sb("t_o", [P, TT])
        ssk, ssq, tk, tq, rk, rq, sso, den2, to, ro = (sb(f"n{i}", [P, TT, H]) for i in range(10))
        o_ln = xn
        x1 = sb("x1", [P, TT, D])

        x1_keep = sb("x1_keep", [P, TT, D])
        stats_b = sb("stats_b", [P, TT, 6])
        mv_b = sb("mv_b", [P, TT, 2])
        rs_b, t_b, v_b, u_b, r2_b, rz_b = (sb(f"b{i}", [P, TT]) for i in range(6))
        z = sb("z", [P, TT, D])
        h = sb("h", [P, TT, D])
        hT = sb("hT", [P, T])
        qk = sb("qk", [P, TT, 2, HB, DB])
        qk_sq = sb("qk_sq", [P, TT, 2, HB, DB])
        ss_b, ts_b, rr_b = (sb(f"bn{i}", [P, TT, 2 * HB]) for i in range(3))
        vb = sb("vb", [P, TT, HB, DB + 1])
        q_pad = sb("q_pad", [P, TT * HB, SLOT], F16)
        k_pad = sb("k_pad", [P, TT * HB, SLOT], F16)
        qTb = sb("qTb", [P, 4, T], F16)
        kTb = sb("kTb", [P, 4, T], F16)
        rden = sb("rden", [P, TT, HB])
        ao = sb("ao", [P, TT, HB, DB])
        aT = sb("aT", [P, T])
        x2 = sb("x2", [P, TT, D])
        ss_f, t_f, rs_f = (sb(f"xf{i}", [P, TT]) for i in range(3))
        xf = sb("xf", [P, TT, D])
        x2_sq = ex_out = xf
        xfT = sb("xfT", [P, T])
        lg, ls, ex, pr, sel, top = (sb(f"g{i}", [P, TT, NE]) for i in range(6))
        mx, es, er, tsum, trec = (sb(f"gs{i}", [P, TT]) for i in range(5))
        gt, ge, cnt = (sb(f"gg{i}", [P, TT, NE, NE]) for i in range(3))
        rank = sb("rank", [P, TT, NE])
        wts = sb("wts", [P, TT, NE])
        tanh_b = sb("tanh_b", [P, 2 * T])
        h0, h1, h2a, h2b, h3b = (sb(f"hid{i}", [P, 2, T]) for i in range(5))
        h2c = h2a
        h3a = sb("h3a", [P, T])
        stats_f = sb("stats_f", [P, TT, 6])
        mv_f = sb("mv_f", [P, TT, 2])
        rs_x, t_x = (sb(f"fx{i}", [P, TT]) for i in range(2))
        o_fin = sb("o_fin", [P, TT, D])

        s_load = sem("weights_loaded")
        s_const = sem("constants_made")
        s_tr = sem("weights_transposed")
        s_trc = sem("transposed_copied")
        s_init = sem("buffers_cleared")
        pool_init = sem("pool_setup_step")
        dve_init = sem("dve_setup_step")

        x_loaded = signal("x_loaded", "A", 16)
        x_copied = signal("x_kept", "A", 16)
        a_stats = signal("a_stats", "A", 4)
        a_rstd = signal("a_rstd", "A", 2)
        xn_ready = signal("xn_ready", "A", TT)
        xh_ready = signal("xh_ready", "A", 1)
        gate_abs = signal("gate_abs", "A", 3)
        gate_exp = signal("gate_exp", "A", 1)
        gate_log = signal("gate_log", "A", 5 + len(SERIES) + 1)
        cum_split = signal("cum_split", "A", 5)
        cum_stored = signal("cum_stored", "A", 16)
        decay_loaded = signal("decay_loaded", "A", 32)
        tanh_a_ready = signal("tanh_a_ready", "A", 12)
        q_copied = signal("q_copied", "A", 4)
        k_squared = signal("k_squared", "A", 4)
        q_summed = signal("q_summed", "A", 4)
        k_summed = signal("k_summed", "A", 4)
        qk_scale = signal("qk_scale", "A", 4)
        k_normed = signal("k_normed", "A", 1)
        q_normed = signal("q_normed", "A", 1)
        o_squared = signal("o_squared", "A", 1)
        o_summed = signal("o_summed", "A", 1)
        o_scale = signal("o_scale", "A", 4)
        o_normed = signal("o_normed", "A", 1)
        y_ready = signal("y_ready", "A", 1)
        o_stats = signal("o_stats", "A", 4)
        o_rstd = signal("o_rstd", "A", 2)
        o_ln_ready = signal("o_ln_ready", "A", 1)
        x1_ready = signal("x1_ready", "A", 1)

        x1_copied = signal("x1_copied", "B", 1)
        b_stats = signal("b_stats", "B", 4)
        b_rstd = signal("b_rstd", "B", 7)
        z_ready = signal("z_ready", "B", TT)
        h_ready = signal("h_ready", "B", TT)
        qk_copied = signal("qk_copied", "B", TT)
        qk_squared = signal("qk_squared", "B", 1)
        qk_summed = signal("qk_summed", "B", 1)
        b_scale = signal("b_scale", "B", 2)
        qk_normed = signal("qk_normed", "B", 1)
        q_weighted = signal("q_weighted", "B", 1)
        k_hi, k_lo = signal("k_hi", "B", 2), signal("k_lo", "B", 1)
        q_hi, q_lo = signal("q_hi", "B", 2), signal("q_lo", "B", 1)
        pads_T = signal("pads_T", "B", 2)
        den_ready = signal("den_ready", "B", TT)
        x2_head = signal("x2_head", "B", 1)
        x2_squared = signal("x2_squared", "B", 1)
        x2_summed = signal("x2_summed", "B", 1)
        x2_rms = signal("x2_rms", "B", 2)
        xf_ready = signal("xf_ready", "B", TT)
        route_max = signal("route_max", "B", 2)
        route_shift = signal("route_shift", "B", 1)
        route_exp = signal("route_exp", "B", 1)
        route_dve = signal("route_dve", "B", 5)
        route_cmp = signal("route_cmp", "B", 4)
        route_sel = signal("route_sel", "B", 1)
        route_recip = signal("route_recip", "B", 2)
        wts_ready = signal("wts_ready", "B", 1)
        tanh_b_ready = signal("tanh_b_ready", "B", 1)
        mixed = signal("mixed", "B", TT * (NE - 1))
        f_stats = signal("f_stats", "B", 4)
        f_rstd = signal("f_rstd", "B", 2)
        f_norm = signal("f_norm", "B", TT)
        out_ready = signal("out_ready", "B", 1)
        out_stored = signal("out_stored", "B", 16)

        A_PAIRS = [f"A{p}" for p in range(PAIRS)]
        B_PAIRS = [f"B{p}" for p in range(PAIRS)]
        work = Ring(2, WORK_A, WORK_B, trips)
        work_filled = [sem(f"work_filled{i}") for i in range(2)]
        work_freed = [sem(f"work_freed{i}") for i in range(2)]
        pair_ring = Ring(2, A_PAIRS, B_PAIRS, trips)
        scores_ready = [sem(f"scores_ready{i}") for i in range(2)]
        probs_ready = [sem(f"probs_ready{i}") for i in range(2)]
        probs_used = [sem(f"probs_used{i}") for i in range(2)]
        B_OUT = [f"B{t}" for t in range(TT)]
        out_ring = Ring(2, A_PAIRS, B_OUT, trips)
        pv_freed = [sem(f"pv_freed{i}") for i in range(2)]

        def work_of(seg, name):
            slot, before_it = work.place(seg, name)
            return work_banks[slot], slot, before_it

        def used(seg, name):
            slot, before_it = work.place(seg, name)
            return work_freed[slot], before_it + 1

        def wait_used(eng, seg, names):
            latest = {}
            for name in names:
                latest[work.place(seg, name)[0]] = name
            for name in latest.values():
                eng.wait_ge(*used(seg, name))

        def multiplied(seg, pair):
            slot, before_it = pair_ring.place(seg, pair)
            return probs_used[slot], before_it + 1

        def run(engine, *stages):
            def play(seg):
                for block, stage in stages:
                    if block in seg.offset:
                        stage(seg)

            play(Segment("first", None, {"A": 0}))
            play(Segment("second", None, {"A": 1, "B": 0}))
            with engine.Fori(1, trips + 1) as i:
                play(Segment("loop", i, {"A": 1, "B": 0}))
            play(Segment("last", None, {"B": NB - 1}))

        spares = [a[:].rearrange("p t h d -> p (t h d)") for a in (o_sb, vs)]
        stage_conv = {"k": arena[:, 0:4096], "v": arena[:, 4096:8192]}
        stage_proj = {m: arena[:, 8192 + i * C:8192 + (i + 1) * C] for i, m in enumerate("kvqg")}
        fold = tanh_a[:].rearrange("p a c -> p (a c)")
        n1 = sb("n1w_col", [P, 1])
        n2 = sb("n2w_col", [P, 1])
        onw2 = sb("onw2", [P, 1])
        q_w, k_w = sb("q_w", [P, CT]), sb("k_w", [P, CT])
        q8, k8 = sb("q8", [P, DB]), sb("k8", [P, DB])
        wf_raw = sb("wf_raw", [P, H])
        small = sb("small", [P, DB])

        flips, at = [], [0]

        def source(name, rows, cols):
            n = -(-rows // P) * cols
            lo = at[0]
            at[0] += n
            ap = spares[lo // 2048][:, lo % 2048:lo % 2048 + n]
            return name, rows, cols, ap.rearrange("p (r c) -> p r c", c=cols)

        groups = [([source("wq", D, D), source("wk", D, D), source("wv", D, D)], n1, wqkv[:]),
                  ([source("wo", D, D)], None, wo_b[:]),
                  ([source("e0_up", HID, D)], n2, up0[:]),
                  ([source("e1_w1", HID, D)], n2, up1[:]),
                  ([source("e1_w2", HID, D)], n2, up2[:]),
                  ([source("e2_l1", HID, D)], n2, l1[:]),
                  ([source("e3_down", D, D)], n2, e3d[:]),
                  ([source("e3_up", HID, D)], None, e3u[:]),
                  ([source("gate_w", NE, D)], n2, gate_w[:])]
        at[0] = max(at[0], 2048)
        groups += [([source("e2_l2", HID, HID)], None, l2[:]),
                   ([source("e2_l3", HID, HID)], None, l3[:]),
                   ([source("e0_down", D, HID)], None, downs[0][:]),
                   ([source("e1_down", D, HID)], 0.5, downs[1][:]),
                   ([source("e2_l4", D, HID)], None, downs[2][:]),
                   ([source("e3_out", D, HID)], None, downs[3][:])]
        sources = [s for g in groups for s in g[0]]
        n_loads = [0]

        block = ctx.enter_context(nc.Block())

        def row(ap):
            return ap.rearrange("(o n) -> o n", o=1)

        setup_loads = (
            [(stage_proj[m], w[f"W{m}"]) for m in "kvqg"]
            + [(stage_conv[m], w[f"{m}conv_w"].rearrange("(o c) j -> o (c j)", o=1).partition_broadcast(P)) for m in "kv"]
            + [(wf_raw[:], w["Wf"]), (bf_rows[:], w["bf"].partition_broadcast(P)),
               (q_w[:], w["qnw"].rearrange("(c p) -> p c", p=P)), (k_w[:], w["knw"].rearrange("(c p) -> p c", p=P)),
               (q8[:], w["qn_w"].partition_broadcast(P)), (k8[:], w["kn_w"].partition_broadcast(P)),
               (n1[:], w["n1_w"].rearrange("(p o) -> p o", o=1)), (n2[:], w["n2_w"].rearrange("(p o) -> p o", o=1)),
               (onw2[0:DH, :], w["onw"].rearrange("(p o) -> p o", o=1)),
               (onw2[DH:P, :], w["onw"].rearrange("(p o) -> p o", o=1)),
               (wo_a[:], w["Wo"].rearrange("(c p) d -> p c d", p=P))]
            + [(ap if rows % P == 0 else ap[0:rows], w[name].rearrange("(r p) c -> p r c", p=min(P, rows)))
               for name, rows, cols, ap in sources])
        loads_total = 16 * len(setup_loads)

        @block.sync
        def _(sp):
            for dst, src in setup_loads:
                sp.dma_start(dst, src, allow_slow_non_contiguous=True).then_inc(s_load, 16)

            def batch(seg, block):
                b = seg.scaled(1, seg.offset[block])
                return b if seg.reg is None else sp.snap(b)

            def tokens_of(ap, b):
                ap = ap[b] if isinstance(b, int) else ap[bass.ds(b, 1)].rearrange("o t d -> (o t) d")
                return ap.rearrange("(t p) d -> p t d", p=P)

            def load_x(seg):
                b = batch(seg, "A")
                sp.wait_ge(xn_ready.sem, seg.of(xn_ready, 0))
                sp.dma_start(x_load[:], tokens_of(x_in, b)).then_inc(x_loaded.sem, 16)
                sp.wait_ge(x1_ready.sem, seg.of(x1_ready, 0))
                sp.dma_start(x_keep[:], tokens_of(x_in, b)).then_inc(x_copied.sem, 16)

            def move_cum(seg):
                sp.wait_ge(cum_split.sem, seg.of(cum_split, 5))
                sp.dma_start(c_dram[0], c_parts[:]).then_inc(cum_stored.sem, 16)
                sp.wait_ge(cum_stored.sem, seg.of(cum_stored, 16))
                for pair in ("A0", "A1"):
                    slot, n = pair_ring.place(seg, pair)
                    sp.wait_ge(probs_used[slot], n)
                if seg.name == "first":
                    sp.wait_ge(s_init, 1)
                src = c_dram[0].rearrange("h p t -> p h t")
                sp.dma_start(dec_q[0:3], src).then_inc(decay_loaded.sem, 16)
                sp.dma_start(dec_k[3:6], src).then_inc(decay_loaded.sem, 16)

            def store(seg):
                b = batch(seg, "B")
                sp.wait_ge(out_ready.sem, seg.of(out_ready, 1))
                sp.dma_start(tokens_of(out, b), o_fin[:]).then_inc(out_stored.sem, 16)

            run(sp, ("A", load_x), ("B", store), ("A", move_cum))
            sp.wait_ge(out_stored.sem, 16 * NB)

        @block.gpsimd
        def _(pool):
            steps = [0]

            def step(ins):
                steps[0] += 1
                ins.then_inc(pool_init, 1)
                pool.wait_ge(pool_init, steps[0])

            step(pool.memset(ident[:], 1.0))
            step(pool.affine_select(out=ident[:], in_=ident[:], compare_op=ALU.is_equal, fill=0.0, base=0,
                                    pattern=[[-1, P]], channel_multiplier=1))
            step(pool.tensor_copy(ident16[:], ident[:]))
            step(pool.tensor_copy(identb[:], ident[:]))
            step(pool.memset(tri[:], 1.0))
            step(pool.affine_select(out=tri[:], in_=tri[:], compare_op=ALU.is_ge, fill=0.0, base=0,
                                    pattern=[[1, T]], channel_multiplier=-1))
            step(pool.memset(mask[:], 0.0))
            step(pool.affine_select(out=mask[:], in_=mask[:], compare_op=ALU.is_ge, fill=MASKED, base=0,
                                    pattern=[[1, P]], channel_multiplier=-1))
            step(pool.memset(before[:], 1.0))
            step(pool.affine_select(out=before[:], in_=before[:], compare_op=ALU.is_gt, fill=0.0, base=0,
                                    pattern=[[0, TT], [1, NE], [-1, NE]], channel_multiplier=0))
            for name, tile in eps.items():
                step(pool.memset(tile[:], eps_value[name]))
            pool.memset(mhalf[:], -0.5).then_inc(s_const, 1)
            step(pool.memset(dec_k[:], 1.0))
            step(pool.memset(dec_q[:], -1.0))
            step(pool.memset(xh[:, 0:TAPS - 1], 0.0))
            step(pool.memset(xl[:, 0:TAPS - 1], 0.0))
            step(pool.memset(q_pad[:], 0.0))
            step(pool.memset(k_pad[:], 0.0))
            step(pool.memset(vb[:, :, :, DB], 1.0))
            pool.wait_ge(s_trc, len(groups))
            pool.memset(vs[:, :, :, DH], 1.0).then_inc(s_init, 1)
            pool.wait_ge(s_init, 1)

            def flat(ap):
                return ap.rearrange("p t h -> p (t h)")

            def rsqrt(seg, done, n, dst, src, name, tmp):
                cols = src.shape[-1]
                pool.tensor_tensor(tmp, src, eps[name][:, 0:cols], ALU.add).then_inc(done.sem, 1)
                pool.wait_ge(done.sem, seg.of(done, n))
                pool.tensor_tensor(dst, tmp, mhalf[:, 0:cols], ALU.pow).then_inc(done.sem, 1)

            def rstd_a(seg):
                pool.wait_ge(a_stats.sem, seg.of(a_stats, 4))
                rsqrt(seg, a_rstd, 1, rs_a[:], mv_a[:, :, 1], "ln", t_a[:])

            def square_k(seg):
                for n in range(4):
                    t, half = n // 2, n % 2
                    lo = half * HALF
                    pool.wait_ge(*used(seg, f"k{t}{half}"))
                    pool.tensor_tensor(ksq[:, t, lo:lo + HALF], ks[:, t, lo:lo + HALF], ks[:, t, lo:lo + HALF],
                                       ALU.mult).then_inc(k_squared.sem, 1)

            def heads(ap):
                return ap.rearrange("p t (h d) -> p (t h) d", d=DH)

            def spread(ap, n):
                return ap.rearrange("p t h -> p (t h)").unsqueeze(2).broadcast_to([P, TT * H, n])

            def norm_qk(seg):
                pool.wait_ge(k_summed.sem, seg.of(k_summed, 4))
                rsqrt(seg, qk_scale, 1, flat(rk[:]), flat(ssk[:]), "k", flat(tk[:]))
                pool.wait_ge(qk_scale.sem, seg.of(qk_scale, 2))
                pool.tensor_tensor(heads(ks), heads(ks), spread(rk[:], DH), ALU.mult).then_inc(k_normed.sem, 1)
                pool.wait_ge(q_copied.sem, seg.of(q_copied, 4))
                pool.wait_ge(q_summed.sem, seg.of(q_summed, 4))
                rsqrt(seg, qk_scale, 3, flat(rq[:]), flat(ssq[:]), "q", flat(tq[:]))
                pool.wait_ge(qk_scale.sem, seg.of(qk_scale, 4))
                pool.tensor_tensor(heads(qs), heads(qs), spread(rq[:], DH), ALU.mult).then_inc(q_normed.sem, 1)

            def norm_o(seg):
                num = o_sb[:].rearrange("p t h d -> p (t h) d")[:, :, 0:DH]
                den = o_sb[:].rearrange("p t h d -> p (t h) d")[:, :, DH]
                pool.wait_ge(*used(seg, "qT3"))
                for p in (PAIRS - 2, PAIRS - 1):
                    slot, n = out_ring.place(seg, f"A{p}")
                    pool.wait_ge(pv_freed[slot], n + 1)
                pool.tensor_tensor(heads(osq), num, num, ALU.mult).then_inc(o_squared.sem, 1)
                pool.tensor_tensor(flat(den2[:]), den, den, ALU.mult).then_inc(o_scale.sem, 1)
                pool.wait_ge(o_scale.sem, seg.of(o_scale, 1))
                pool.tensor_tensor(flat(den2[:]), flat(den2[:]), eps["k"][:, 0:TT * H], ALU.mult)\
                    .then_inc(o_scale.sem, 1)
                pool.wait_ge(o_scale.sem, seg.of(o_scale, 2))
                pool.wait_ge(o_summed.sem, seg.of(o_summed, 1))
                pool.tensor_tensor(to[:], den2[:], sso[:], ALU.add).then_inc(o_scale.sem, 1)
                pool.wait_ge(o_scale.sem, seg.of(o_scale, 3))
                pool.tensor_tensor(flat(ro[:]), flat(to[:]), mhalf[:, 0:TT * H], ALU.pow).then_inc(o_scale.sem, 1)
                pool.wait_ge(o_scale.sem, seg.of(o_scale, 4))
                pool.tensor_tensor(heads(y), num, spread(ro[:], DH), ALU.mult).then_inc(o_normed.sem, 1)

            def rstd_o(seg):
                pool.wait_ge(o_stats.sem, seg.of(o_stats, 4))
                rsqrt(seg, o_rstd, 1, rs_o[:], mv_o[:, :, 1], "ln", t_o[:])

            def rstd_b(seg):
                def link(n, ins):
                    ins.then_inc(b_rstd.sem, 1)
                    pool.wait_ge(b_rstd.sem, seg.of(b_rstd, n))

                pool.wait_ge(b_stats.sem, seg.of(b_stats, 4))
                link(1, pool.tensor_tensor(t_b[:], mv_b[:, :, 1], eps["ln"][:, 0:TT], ALU.add))
                link(2, pool.tensor_tensor(rs_b[:], t_b[:], mhalf[:, 0:TT], ALU.pow))
                link(3, pool.tensor_tensor(v_b[:], mv_b[:, :, 1], rs_b[:], ALU.mult))
                link(4, pool.tensor_tensor(u_b[:], v_b[:], rs_b[:], ALU.mult))
                link(5, pool.tensor_tensor(u_b[:], u_b[:], eps["z"][:, 0:TT], ALU.add))
                link(6, pool.tensor_tensor(r2_b[:], u_b[:], mhalf[:, 0:TT], ALU.pow))
                pool.tensor_tensor(rz_b[:], rs_b[:], r2_b[:], ALU.mult).then_inc(b_rstd.sem, 1)

            def norm_b(seg):
                f = "p t a h d -> p (t a h) d"
                pool.wait_ge(qk_copied.sem, seg.of(qk_copied, TT))
                pool.tensor_tensor(qk_sq[:], qk[:], qk[:], ALU.mult).then_inc(qk_squared.sem, 1)
                pool.wait_ge(qk_summed.sem, seg.of(qk_summed, 1))
                rsqrt(seg, b_scale, 1, flat(rr_b[:]), flat(ss_b[:]), "qk_b", flat(ts_b[:]))
                pool.wait_ge(b_scale.sem, seg.of(b_scale, 2))
                r = rr_b[:].rearrange("p t h -> p (t h)").unsqueeze(2).broadcast_to([P, TT * 2 * HB, DB])
                pool.tensor_tensor(qk[:].rearrange(f), qk[:].rearrange(f), r, ALU.mult).then_inc(qk_normed.sem, 1)
                pool.wait_ge(qk_normed.sem, seg.of(qk_normed, 1))
                wb = w8[:].rearrange("p h d -> p (h d)").unsqueeze(1).broadcast_to([P, TT, HB * DB])
                qq = qk[:].rearrange("p t a h d -> p t a (h d)")[:, :, 0, :]
                pool.tensor_tensor(qq, qq, wb, ALU.mult).then_inc(q_weighted.sem, 1)

            def square_x2(seg):
                wait_used(pool, seg, [f"wo{t}" for t in range(TT)])
                pool.wait_ge(x2_head.sem, seg.of(x2_head, 1))
                pool.tensor_tensor(x2_sq[:], x2[:], x2[:], ALU.mult).then_inc(x2_squared.sem, 1)
                pool.wait_ge(x2_summed.sem, seg.of(x2_summed, 1))
                rsqrt(seg, x2_rms, 1, rs_f[:], ss_f[:], "xf", t_f[:])

            def route(seg):
                pool.wait_ge(route_max.sem, seg.of(route_max, 2))
                pool.tensor_tensor(ls[:], lg[:], mx[:].unsqueeze(2).broadcast_to([P, TT, NE]),
                                   ALU.subtract).then_inc(route_shift.sem, 1)
                pool.wait_ge(route_cmp.sem, seg.of(route_cmp, 2))
                pool.tensor_tensor(ge[:], ge[:], before[:], ALU.mult).then_inc(route_cmp.sem, 1)
                pool.wait_ge(route_cmp.sem, seg.of(route_cmp, 3))
                pool.tensor_tensor(cnt[:], gt[:], ge[:], ALU.add).then_inc(route_cmp.sem, 1)

            def rstd_f(seg):
                pool.wait_ge(f_stats.sem, seg.of(f_stats, 4))
                rsqrt(seg, f_rstd, 1, rs_x[:], mv_f[:, :, 1], "ln", t_x[:])

            run(pool, ("B", rstd_b), ("B", norm_b), ("B", square_x2), ("B", route), ("B", rstd_f), ("A", rstd_a),
                ("A", square_k), ("A", norm_qk), ("A", norm_o), ("A", rstd_o))

        @block.scalar
        def _(act):
            act.wait_ge(s_init, 1)

            def filled(seg, name):
                bank, slot, n = work_of(seg, name)
                act.wait_ge(work_filled[slot], n + 1)
                return bank, slot

            tanh_units = [f"{m}{t}{half}" for t in range(TT) for m in "kvg" for half in range(2)]

            def copy_xT(seg):
                bank, _ = filled(seg, "xT")
                act.activation(xh[:, TAPS - 1:], bank[:, 0:T], ACT.Copy).then_inc(xh_ready.sem, 1)

            def gate(seg):
                act.wait_ge(gate_abs.sem, seg.of(gate_abs, 3))
                act.activation(fe[:], fneg[:], ACT.Exp).then_inc(gate_exp.sem, 1)

            def projected(seg):
                n = 0
                for t in range(TT):
                    for m in "kvqg":
                        for half in range(2):
                            bank, slot = filled(seg, f"{m}{t}{half}")
                            lo = half * HALF
                            if m == "q":
                                act.activation(qs[:, t, lo:lo + HALF], bank[:], ACT.Copy).then_inc(q_copied.sem, 1)
                                act.activation(qsq[:, t, lo:lo + HALF], bank[:], ACT.Square)\
                                   .then_inc(work_freed[slot], 1)
                            else:
                                if n >= 2:
                                    act.wait_ge(*used(seg, tanh_units[n - 2]))
                                act.activation(tanh_a[:, n % 2, :], bank[:], ACT.Tanh, scale=0.5)\
                                   .then_inc(tanh_a_ready.sem, 1)
                                n += 1

            def copy_kT(seg):
                for u in range(4):
                    bank, slot = filled(seg, f"kT{u}")
                    act.activation(kT[:, 2 * u:2 * u + 2, :].rearrange("p c t -> p (c t)"), bank[:], ACT.Copy)\
                       .then_inc(work_freed[slot], 1)

            def exps(seg, block):
                for p in range(PAIRS):
                    slot, n = pair_ring.place(seg, f"{block}{p}")
                    act.wait_ge(scores_ready[slot], n + 1)
                    act.wait_ge(probs_used[slot], n)
                    act.activation(probs[slot][:], score_banks[slot][:, :, 0:3 * P], ACT.Exp)\
                       .then_inc(probs_ready[slot], 1)

            def copy_yT(seg):
                for u in range(4):
                    bank, slot = filled(seg, f"yT{u}")
                    act.activation(yT[:, 2 * u:2 * u + 2, :].rearrange("p c t -> p (c t)"), bank[:], ACT.Copy)\
                       .then_inc(work_freed[slot], 1)

            def keep(seg):
                act.wait_ge(out_ready.sem, seg.of(out_ready, 0))
                act.wait_ge(x1_ready.sem, seg.scaled(1, seg.offset["B"] + 1))
                act.activation(x1_keep[:], x1[:], ACT.Copy).then_inc(x1_copied.sem, 1)
                act.wait_ge(z_ready.sem, seg.of(z_ready, TT))
                act.wait_ge(f_norm.sem, seg.of(f_norm, 0))
                act.activation(x2[:, :, 0:MUTE], z[:, :, 0:MUTE], ACT.Copy).then_inc(x2_head.sem, 1)

            def copy_hT(seg):
                bank, slot = filled(seg, "hT")
                act.activation(hT[:], bank[:, 0:T], ACT.Copy).then_inc(work_freed[slot], 1)

            def copy_qkv(seg):
                for t in range(TT):
                    bank, slot = filled(seg, f"qkv{t}")
                    if t == 0:
                        act.wait_ge(k_lo.sem, seg.of(k_lo, 0))
                        act.wait_ge(q_lo.sem, seg.of(q_lo, 0))
                    act.activation(qk[:, t].rearrange("p a h d -> p (a h d)"), bank[:, 0:2 * D], ACT.Copy)\
                       .then_inc(qk_copied.sem, 1)
                    act.activation(vb[:, t, :, 0:DB], bank[:, 2 * D:3 * D].rearrange("p (h d) -> p h d", d=DB),
                                   ACT.Copy).then_inc(work_freed[slot], 1)

            def copy_pads(seg):
                for name, dst in (("qpT", qTb), ("kpT", kTb)):
                    bank, slot = filled(seg, name)
                    act.activation(dst[:].rearrange("p j t -> p (j t)"), bank[:].bitcast(F16), ACT.Copy)\
                       .then_inc(work_freed[slot], 1)

            def copy_aT(seg):
                bank, slot = filled(seg, "aT")
                act.activation(aT[:], bank[:, 0:T], ACT.Copy).then_inc(work_freed[slot], 1)

            def copy_xfT(seg):
                bank, slot = filled(seg, "xfT")
                act.activation(xfT[:], bank[:, 0:T], ACT.Copy).then_inc(work_freed[slot], 1)

            def route(seg):
                act.wait_ge(route_shift.sem, seg.of(route_shift, 1))
                act.activation(ex[:], ls[:], ACT.Exp).then_inc(route_exp.sem, 1)

            def flat(ap):
                return ap.rearrange("p c t -> p (c t)")

            def experts(seg):
                def gelu(name, dst, cols=2 * T):
                    bank, slot = filled(seg, name)
                    act.activation(dst, bank[:, 0:cols], ACT.Gelu).then_inc(work_freed[slot], 1)

                bank, slot = filled(seg, "e0")
                act.activation(flat(h0[:]), bank[:], ACT.Gelu).then_inc(work_freed[slot], 1)
                bank, slot = filled(seg, "e1a")
                act.activation(tanh_b[:], bank[:], ACT.Tanh, scale=0.5).then_inc(tanh_b_ready.sem, 1)
                gelu("e2a", flat(h2a[:]))
                gelu("e3a", h3a[:], T)
                gelu("e2b", flat(h2b[:]))
                gelu("e3b", flat(h3b[:]))
                gelu("e2c", flat(h2c[:]))

            run(act, ("B", keep), ("B", copy_hT), ("B", copy_qkv), ("B", copy_pads), ("B", lambda s: exps(s, "B")),
                ("B", copy_aT), ("B", copy_xfT), ("B", route), ("B", experts), ("A", copy_xT), ("A", gate),
                ("A", projected), ("A", copy_kT), ("A", lambda s: exps(s, "A")), ("A", copy_yT))

        @block.vector
        def _(dve):
            dve.wait_ge(s_load, loads_total)
            steps = [0]

            def step(ins):
                steps[0] += 1
                ins.then_inc(dve_init, 1)
                dve.wait_ge(dve_init, steps[0])

            def split(src, hi, lo):
                step(dve.tensor_copy(hi, src))
                step(dve.tensor_tensor(lo, src, hi, ALU.subtract))

            for m in "kv":
                for j in range(TAPS):
                    taps = stage_conv[m].rearrange("p (c j) -> p c j", j=TAPS)[:, :, j]
                    step(dve.tensor_tensor(fold, stage_proj[m], taps, ALU.mult))
                    split(fold, proj[m][:, 0, j, :], proj[m][:, 1, j, :])
            for m in "qg":
                split(stage_proj[m], proj[m][:, 0, 0, :], proj[m][:, 1, 0, :])
            split(wf_raw[:], wf[:, 0, :], wf[:, 1, :])
            step(dve.tensor_scalar(wo_a[:], wo_a[:], onw2[:, 0:1], 0.5 * DH ** 0.5, ALU.mult, ALU.mult))
            step(dve.tensor_scalar(n2[:], n2[:], float(D) ** 0.5, None, ALU.mult))
            step(dve.tensor_tensor(wqk[:], q_w[:], k_w[:], ALU.mult))
            step(dve.tensor_scalar(wqk[:], wqk[:], float(DH) * DH ** -0.5, None, ALU.mult))
            step(dve.tensor_tensor(small[:], q8[:], k8[:], ALU.mult))
            step(dve.tensor_scalar(w8[:], small[:].unsqueeze(1).broadcast_to([P, HB, DB]), float(DB) * DB ** -0.5, None,
                                   ALU.mult))
            for n, (srcs, scale, dst) in enumerate(groups):
                cols = sum(-(-r // P) * c if r >= P else r for _, r, c, _ in srcs)
                bank = work_banks[n % 2][:, 0:cols]
                dst = dst if len(dst.shape) == 2 else dst.rearrange("p a b -> p (a b)")
                dve.wait_ge(s_tr, n + 1)
                s = 1.0 if scale is None else scale if isinstance(scale, float) else scale[:, 0:1]
                dve.tensor_scalar(dst, bank, s, None, ALU.mult).then_inc(s_trc, 1)
            dve.wait_ge(s_init, 1)

            def filled(seg, name):
                bank, slot, n = work_of(seg, name)
                dve.wait_ge(work_filled[slot], n + 1)
                return bank, slot

            def stats(seg, done, src, st, mv):
                for t in range(TT):
                    dve.bn_stats(st[:, t, :], src(t)).then_inc(done.sem, 1)
                dve.wait_ge(done.sem, seg.of(done, TT))
                dve.memset(mark[:], 0.0)
                for t in range(TT):
                    dve.bn_aggr(mv[:, t, :], st[:, t, :]).then_inc(done.sem, 1)

            def layernorm_x(seg):
                dve.wait_ge(x_loaded.sem, seg.of(x_loaded, 16))
                stats(seg, a_stats, lambda t: x_load[:, t, :], stats_a, mv_a)
                dve.wait_ge(a_rstd.sem, seg.of(a_rstd, 2))
                dve.wait_ge(a_stats.sem, seg.of(a_stats, 4))
                for t in range(TT):
                    dve.tensor_scalar(xn[:, t, :], x_load[:, t, :], mv_a[:, t, 0:1], rs_a[:, t:t + 1],
                                      ALU.subtract, ALU.mult).then_inc(xn_ready.sem, 1)
                bank, slot = filled(seg, "xT")
                dve.wait_ge(xh_ready.sem, seg.of(xh_ready, 1))
                dve.tensor_tensor(xl[:, TAPS - 1:], bank[:, 0:T], xh[:, TAPS - 1:], ALU.subtract)\
                   .then_inc(work_freed[slot], 1)

            def gates(seg):
                def link(n, ins):
                    ins.then_inc(gate_log.sem, 1)
                    dve.wait_ge(gate_log.sem, seg.of(gate_log, n))

                bank, slot = filled(seg, "gate_logits")
                dve.tensor_tensor(fz[:], bank[:, 0:TT * H].rearrange("p (t h) -> p t h", t=TT),
                                  bf_rows[:].unsqueeze(1).broadcast_to([P, TT, H]), ALU.add)\
                   .then_inc(work_freed[slot], 1)
                dve.wait_ge(work_freed[slot], work_of(seg, "gate_logits")[2] + 1)
                dve.tensor_scalar(fneg[:], fz[:], -1.0, None, ALU.mult).then_inc(gate_abs.sem, 1)
                dve.tensor_scalar(fmin[:], fz[:], 0.0, None, ALU.min).then_inc(gate_abs.sem, 1)
                dve.wait_ge(gate_abs.sem, seg.of(gate_abs, 2))
                dve.tensor_tensor(fneg[:], fneg[:], fz[:], ALU.min).then_inc(gate_abs.sem, 1)
                dve.wait_ge(gate_exp.sem, seg.of(gate_exp, 1))
                link(1, dve.tensor_scalar(fd[:], fe[:], 2.0, None, ALU.add))
                link(2, dve.reciprocal(fr[:], fd[:]))
                link(3, dve.tensor_tensor(fw[:], fe[:], fr[:], ALU.mult))
                link(4, dve.tensor_tensor(fw2[:], fw[:], fw[:], ALU.mult))
                link(5, dve.tensor_scalar(fq[:], fw2[:], SERIES[0], None, ALU.mult))
                n = 5
                for c in SERIES[1:]:
                    n += 1
                    link(n, dve.scalar_tensor_tensor(out=fq[:], in0=fq[:], scalar=c, in1=fw2[:], op0=ALU.add,
                                                     op1=ALU.mult))
                link(n + 1, dve.scalar_tensor_tensor(out=fq[:], in0=fq[:], scalar=1.0, in1=fw[:], op0=ALU.add,
                                                     op1=ALU.mult))
                dve.scalar_tensor_tensor(out=fl[:], in0=fq[:], scalar=-2.0, in1=fmin[:], op0=ALU.mult,
                                         op1=ALU.add).then_inc(gate_log.sem, 1)

            def split_cum(seg):
                bank, slot = filled(seg, "cum")
                cum = bank[0:H, 0:T]
                dve.wait_ge(cum_stored.sem, seg.of(cum_stored, 0))
                dve.tensor_copy(c_parts[:, 0, :], cum).then_inc(cum_split.sem, 1)
                dve.wait_ge(cum_split.sem, seg.of(cum_split, 1))
                dve.tensor_tensor(c_res[:], cum, c_parts[:, 0, :], ALU.subtract).then_inc(work_freed[slot], 1)
                dve.wait_ge(work_freed[slot], work_of(seg, "cum")[2] + 1)
                dve.tensor_copy(c_parts[:, 1, :], c_res[:]).then_inc(cum_split.sem, 1)
                dve.wait_ge(cum_split.sem, seg.of(cum_split, 2))
                dve.tensor_tensor(c_res2[:], c_res[:], c_parts[:, 1, :], ALU.subtract).then_inc(cum_split.sem, 1)
                dve.wait_ge(cum_split.sem, seg.of(cum_split, 3))
                dve.tensor_copy(c_parts[:, 2, :], c_res2[:]).then_inc(cum_split.sem, 2)

            def by_head(ap):
                return ap.rearrange("p (h d) -> p h d", d=DH)

            def projected(seg, t):
                n = 6 * t
                if True:
                    for m in "kvqg":
                        for half in range(2):
                            lo, hh = half * HALF, slice(half * 8, half * 8 + 8)
                            if m == "q":
                                continue
                            bank, slot = filled(seg, f"{m}{t}{half}")
                            dve.wait_ge(tanh_a_ready.sem, seg.of(tanh_a_ready, n + 1))
                            n += 1
                            th = tanh_a[:, (n - 1) % 2, :]
                            src = bank[:]
                            dst = {"k": ks[:, t, lo:lo + HALF], "g": gs[:, t, lo:lo + HALF],
                                   "v": vs[:, t, hh, 0:DH]}[m]
                            if m == "v":
                                th, src = by_head(th), by_head(src)
                            dve.scalar_tensor_tensor(out=dst, in0=th, scalar=1.0, in1=src, op0=ALU.add,
                                                     op1=ALU.mult).then_inc(work_freed[slot], 1)
                    for half in range(2):
                        lo, hh = half * HALF, slice(half * 8, half * 8 + 8)
                        dve.wait_ge(k_squared.sem, seg.of(k_squared, 2 * t + half + 1))
                        dve.tensor_reduce(ssk[:, t, hh], by_head(ksq[:, t, lo:lo + HALF]), X, ALU.add)\
                           .then_inc(k_summed.sem, 1)
                        _, slot, before_it = work_of(seg, f"q{t}{half}")
                        dve.wait_ge(work_freed[slot], before_it + 1)
                        dve.tensor_reduce(ssq[:, t, hh], by_head(qsq[:, t, lo:lo + HALF]), X, ALU.add)\
                           .then_inc(q_summed.sem, 1)

            def copy_qT(seg):
                for u in range(4):
                    bank, slot = filled(seg, f"qT{u}")
                    dve.tensor_tensor(qT[:, 2 * u:2 * u + 2, :], bank[:].rearrange("p (c t) -> p c t", c=2),
                                      wqk[:, 2 * u:2 * u + 2].unsqueeze(2).broadcast_to([P, 2, T]), ALU.mult)\
                       .then_inc(work_freed[slot], 1)

            def copy_o(seg):
                for p in range(PAIRS):
                    slot, _ = out_ring.place(seg, f"A{p}")
                    dve.wait_ge(*multiplied(seg, f"A{p}"))
                    src = out_banks[slot][:, 0:4 * (DH + 1)].rearrange("p (t h d) -> p t (h d)", t=TT, h=2)
                    dst = o_sb[:, :, 2 * p:2 * p + 2, :].rearrange("p t h d -> p t (h d)")
                    if p == 0:
                        dve.wait_ge(o_normed.sem, seg.of(o_normed, 0))
                    dve.tensor_copy(dst, src).then_inc(pv_freed[slot], 1)

            def finish_o(seg):
                dve.wait_ge(o_squared.sem, seg.of(o_squared, 1))
                dve.tensor_reduce(sso[:].rearrange("p t h -> p (t h)"),
                                  osq.rearrange("p t (h d) -> p (t h) d", d=DH), X, ALU.add)\
                   .then_inc(o_summed.sem, 1)
                dve.wait_ge(o_normed.sem, seg.of(o_normed, 1))
                dve.wait_ge(*used(seg, "g11"))
                dve.tensor_tensor(y, y, gs, ALU.mult).then_inc(y_ready.sem, 1)

            def layernorm_o(seg):
                bank, slot = filled(seg, "attn_out")
                stats(seg, o_stats, lambda t: bank[:, t * D:(t + 1) * D], stats_o, mv_o)
                dve.wait_ge(o_rstd.sem, seg.of(o_rstd, 2))
                dve.wait_ge(o_stats.sem, seg.of(o_stats, 4))
                for t, done in enumerate((o_ln_ready.sem, work_freed[slot])):
                    dve.tensor_scalar(o_ln[:, t, :], bank[:, t * D:(t + 1) * D], mv_o[:, t, 0:1], rs_o[:, t:t + 1],
                                      ALU.subtract, ALU.mult).then_inc(done, 1)
                dve.wait_ge(o_ln_ready.sem, seg.of(o_ln_ready, 1))
                dve.wait_ge(*used(seg, "attn_out"))
                dve.wait_ge(x_copied.sem, seg.of(x_copied, 16))
                dve.wait_ge(x1_copied.sem, seg.scaled(1, seg.offset["A"]))
                dve.wait_ge(h_ready.sem, seg.scaled(TT, TT * seg.offset["A"]))
                dve.tensor_tensor(x1[:], x_keep[:], o_ln[:], ALU.add).then_inc(x1_ready.sem, 1)

            def layernorm_b(seg):
                dve.wait_ge(x1_ready.sem, seg.scaled(1, seg.offset["B"] + 1))
                stats(seg, b_stats, lambda t: x1[:, t, :], stats_b, mv_b)
                dve.wait_ge(b_rstd.sem, seg.of(b_rstd, 7))
                dve.wait_ge(b_stats.sem, seg.of(b_stats, 4))
                dve.wait_ge(x2_head.sem, seg.of(x2_head, 0))
                for t in range(TT):
                    dve.tensor_scalar(h[:, t, :], x1[:, t, :], mv_b[:, t, 0:1], rz_b[:, t:t + 1],
                                      ALU.subtract, ALU.mult).then_inc(h_ready.sem, 1)
                    dve.tensor_scalar(z[:, t, :], x1[:, t, :], mv_b[:, t, 0:1], rs_b[:, t:t + 1],
                                      ALU.subtract, ALU.mult).then_inc(z_ready.sem, 1)

            def pads(seg):
                dve.wait_ge(qk_squared.sem, seg.of(qk_squared, 1))
                dve.tensor_reduce(ss_b[:].rearrange("p t h -> p (t h)"),
                                  qk_sq[:].rearrange("p t a h d -> p (t a h) d"), X, ALU.add)\
                   .then_inc(qk_summed.sem, 1)

                def head_rows(a):
                    return qk[:, :, a].rearrange("p t h d -> p t h d")

                def pad(ap, part):
                    return ap[:].rearrange("p (t h) s -> p t h s", t=TT)[:, :, :, part * DB:(part + 1) * DB]

                dve.wait_ge(qk_normed.sem, seg.of(qk_normed, 1))
                dve.tensor_copy(pad(k_pad, 0), head_rows(1)).then_inc(k_hi.sem, 1)
                dve.tensor_copy(pad(k_pad, 2), head_rows(1)).then_inc(k_hi.sem, 1)
                dve.wait_ge(k_hi.sem, seg.of(k_hi, 1))
                dve.tensor_tensor(pad(k_pad, 1), head_rows(1), pad(k_pad, 0), ALU.subtract).then_inc(k_lo.sem, 1)
                dve.wait_ge(q_weighted.sem, seg.of(q_weighted, 1))
                dve.tensor_copy(pad(q_pad, 0), head_rows(0)).then_inc(q_hi.sem, 1)
                dve.tensor_copy(pad(q_pad, 1), head_rows(0)).then_inc(q_hi.sem, 1)
                dve.wait_ge(q_hi.sem, seg.of(q_hi, 1))
                dve.tensor_tensor(pad(q_pad, 2), head_rows(0), pad(q_pad, 0), ALU.subtract).then_inc(q_lo.sem, 1)

            def outputs_b(seg):
                for t in range(TT):
                    slot, _ = out_ring.place(seg, f"B{t}")
                    dve.wait_ge(*multiplied(seg, f"B{PAIRS - 1}"))
                    o = out_banks[slot][:, 0:HB * (DB + 1)].rearrange("p (h d) -> p h d", h=HB)
                    dve.reciprocal(rden[:, t], o[:, :, DB]).then_inc(den_ready.sem, 1)
                    dve.wait_ge(den_ready.sem, seg.of(den_ready, t + 1))
                    dve.tensor_tensor(ao[:, t], o[:, :, 0:DB], rden[:, t].unsqueeze(2).broadcast_to([P, HB, DB]),
                                      ALU.mult).then_inc(pv_freed[slot], 1)

            def residual_b(seg):
                for t in range(TT):
                    bank, slot = filled(seg, f"wo{t}")
                    dve.wait_ge(f_norm.sem, seg.of(f_norm, 0))
                    dve.wait_ge(z_ready.sem, seg.of(z_ready, TT))
                    dve.tensor_tensor(x2[:, t, MUTE:], bank[:, 0:D - MUTE], z[:, t, MUTE:], ALU.add)\
                       .then_inc(work_freed[slot], 1)
                dve.wait_ge(x2_squared.sem, seg.of(x2_squared, 1))
                dve.tensor_reduce(ss_f[:], x2_sq[:], X, ALU.add).then_inc(x2_summed.sem, 1)
                dve.wait_ge(x2_rms.sem, seg.of(x2_rms, 2))
                for t in range(TT):
                    dve.tensor_scalar(xf[:, t, :], x2[:, t, :], rs_f[:, t:t + 1], None, ALU.mult)\
                       .then_inc(xf_ready.sem, 1)

            def route(seg):
                bank, slot = filled(seg, "route")
                big = float(np.finfo(np.float32).max)
                dve.tensor_scalar(lg[:], bank[:, 0:TT * NE].rearrange("p (t e) -> p t e", t=TT), -big, big,
                                  ALU.max, ALU.min).then_inc(work_freed[slot], 1)
                dve.wait_ge(work_freed[slot], work_of(seg, "route")[2] + 1)
                dve.tensor_reduce(mx[:], lg[:], X, ALU.max).then_inc(route_max.sem, 2)
                dve.wait_ge(route_exp.sem, seg.of(route_exp, 1))
                dve.tensor_reduce(es[:], ex[:], X, ALU.add).then_inc(route_dve.sem, 1)
                dve.wait_ge(route_dve.sem, seg.of(route_dve, 1))
                dve.reciprocal(er[:], es[:]).then_inc(route_dve.sem, 1)
                dve.wait_ge(route_dve.sem, seg.of(route_dve, 2))
                dve.tensor_tensor(pr[:], ex[:], er[:].unsqueeze(2).broadcast_to([P, TT, NE]), ALU.mult)\
                   .then_inc(route_dve.sem, 1)
                dve.wait_ge(route_dve.sem, seg.of(route_dve, 3))
                pj = pr[:].unsqueeze(2).broadcast_to([P, TT, NE, NE])
                pi = pr[:].unsqueeze(3).broadcast_to([P, TT, NE, NE])
                dve.tensor_tensor(gt[:], pj, pi, ALU.is_gt).then_inc(route_cmp.sem, 1)
                dve.tensor_tensor(ge[:], pj, pi, ALU.is_equal).then_inc(route_cmp.sem, 1)
                dve.wait_ge(route_cmp.sem, seg.of(route_cmp, 4))
                dve.tensor_reduce(rank[:], cnt[:], X, ALU.add).then_inc(route_dve.sem, 1)
                dve.wait_ge(route_dve.sem, seg.of(route_dve, 4))
                dve.scalar_tensor_tensor(out=top[:], in0=rank[:], scalar=1.5, in1=pr[:], op0=ALU.is_lt,
                                         op1=ALU.mult).then_inc(route_sel.sem, 1)
                dve.wait_ge(route_sel.sem, seg.of(route_sel, 1))
                dve.tensor_reduce(tsum[:], top[:], X, ALU.add).then_inc(route_dve.sem, 1)
                dve.wait_ge(route_dve.sem, seg.of(route_dve, 5))
                dve.tensor_scalar(trec[:], tsum[:], 1e-8, None, ALU.add).then_inc(route_recip.sem, 1)
                dve.wait_ge(route_recip.sem, seg.of(route_recip, 1))
                dve.reciprocal(tsum[:], trec[:]).then_inc(route_recip.sem, 1)
                dve.wait_ge(route_recip.sem, seg.of(route_recip, 2))
                dve.tensor_tensor(wts[:], top[:], tsum[:].unsqueeze(2).broadcast_to([P, TT, NE]), ALU.mult)\
                   .then_inc(wts_ready.sem, 1)

            def experts(seg):
                bank, slot = filled(seg, "e1a")
                dve.wait_ge(tanh_b_ready.sem, seg.of(tanh_b_ready, 1))
                hid = h1[:].rearrange("p c t -> p (c t)")
                dve.scalar_tensor_tensor(out=hid, in0=tanh_b[:], scalar=1.0, in1=bank[:], op0=ALU.add,
                                         op1=ALU.mult).then_inc(work_freed[slot], 1)
                bank, slot = filled(seg, "e1b")
                dve.wait_ge(*used(seg, "e1a"))
                dve.tensor_tensor(hid, hid, bank[:], ALU.mult).then_inc(work_freed[slot], 1)

            def mix(seg):
                dve.wait_ge(wts_ready.sem, seg.of(wts_ready, 1))
                for t in range(TT):
                    bank, slot = filled(seg, f"down{t}")
                    for e in range(NE):
                        acc = x2[:, t, MUTE:]
                        dve.scalar_tensor_tensor(out=acc, in0=bank[:, e * P:e * P + D - MUTE],
                                                 scalar=wts[:, t, e:e + 1], in1=acc, op0=ALU.mult,
                                                 op1=ALU.add)\
                           .then_inc(mixed.sem if e < NE - 1 else work_freed[slot], 1)
                        if e < NE - 1:
                            dve.wait_ge(mixed.sem, seg.of(mixed, t * (NE - 1) + e + 1))
                    dve.wait_ge(*used(seg, f"down{t}"))
                stats(seg, f_stats, lambda t: x2[:, t, :], stats_f, mv_f)
                dve.wait_ge(f_rstd.sem, seg.of(f_rstd, 2))
                dve.wait_ge(f_stats.sem, seg.of(f_stats, 4))
                dve.wait_ge(out_stored.sem, seg.of(out_stored, 0))
                for t in range(TT):
                    dve.tensor_scalar(ex_out[:, t, :], x2[:, t, :], mv_f[:, t, 0:1], rs_x[:, t:t + 1],
                                      ALU.subtract, ALU.mult).then_inc(f_norm.sem, 1)
                dve.wait_ge(f_norm.sem, seg.of(f_norm, TT))
                dve.wait_ge(x1_copied.sem, seg.of(x1_copied, 1))
                dve.tensor_tensor(o_fin[:], ex_out[:], x1_keep[:], ALU.add).then_inc(out_ready.sem, 1)

            run(dve, ("B", layernorm_b), ("B", pads), ("B", outputs_b), ("B", residual_b), ("B", route),
                ("B", experts), ("B", mix), ("A", layernorm_x), ("A", gates), ("A", lambda s: projected(s, 0)),
                ("A", split_cum), ("A", lambda s: projected(s, 1)), ("A", copy_qT), ("A", copy_o), ("A", finish_o),
                ("A", layernorm_o))

        @block.tensor
        def _(pe):
            pe.wait_ge(s_load, loads_total)
            pe.wait_ge(s_const, 1)
            for n, (srcs, _, _) in enumerate(groups):
                if n >= 2:
                    pe.wait_ge(s_trc, n - 1)
                bank, at_col = work_banks[n % 2], 0
                for _, rows, cols, src in srcs:
                    for c in range(cols // P):
                        for r in range(-(-rows // P)):
                            m = min(P, rows)
                            last = pe.transpose(bank[:, at_col:at_col + m], src[0:m, r, c * P:(c + 1) * P],
                                                ident[0:m, 0:m])
                            at_col += m
                last.then_inc(s_tr, 1)
            pe.wait_ge(s_init, 1)

            def take(seg, name):
                bank, slot, n = work_of(seg, name)
                pe.wait_ge(work_freed[slot], n)
                return bank, work_filled[slot]

            def turn(seg, name, src):
                bank, full = take(seg, name)
                for t in range(TT):
                    last = pe.transpose(bank[:, t * P:(t + 1) * P], src[:, t], ident[:])
                last.then_inc(full, 1)

            def turn_x(seg):
                pe.wait_ge(xn_ready.sem, seg.of(xn_ready, TT))
                turn(seg, "xT", xn)

            def three(out_ap, lhs, rhs, taps, start=True):
                n, total = 0, 3 * len(taps)
                for j in taps:
                    for a, b in ((0, 0), (0, 1), (1, 0)):
                        last = pe.matmul(out_ap, lhs(a, j), rhs(b, j), start=start and n == 0, stop=n == total - 1)
                        n += 1
                return last

            def x_cols(t, shift):
                return lambda a, j: (xh, xl)[a][:, t * P + shift + j:t * P + shift + j + P]

            def gate_logits(seg):
                bank, full = take(seg, "gate_logits")
                pe.wait_ge(xh_ready.sem, seg.of(xh_ready, 1))
                pe.wait_ge(*used(seg, "xT"))
                for t in range(TT):
                    last = three(bank[:, t * H:(t + 1) * H], x_cols(t, TAPS - 1), lambda b, j: wf[:, b, :], [0])
                last.then_inc(full, 1)

            def project(seg, t):
                for m in "kvqg":
                    for half in range(2):
                        bank, full = take(seg, f"{m}{t}{half}")
                        lo = half * HALF
                        taps = list(range(TAPS)) if m in "kv" else [0]
                        three(bank[:], x_cols(t, 0 if m in "kv" else TAPS - 1),
                              lambda b, j: proj[m][:, b, j, lo:lo + HALF], taps).then_inc(full, 1)

            def cumulate(seg):
                bank, full = take(seg, "cum")
                pe.wait_ge(gate_log.sem, seg.of(gate_log, gate_log.per))
                pe.matmul(bank[0:H, 0:T], fl[:, 0, :], tri[:], start=True, stop=False)
                pe.matmul(bank[0:H, P:T], fl[:, 1, :], tri[:, 0:P], start=False, stop=True).then_inc(full, 1)

            def turn_heads(seg, name, src):
                for u in range(4):
                    bank, full = take(seg, f"{name}{u}")
                    for i in range(2):
                        for t in range(TT):
                            c = 2 * u + i
                            last = pe.transpose(bank[:, i * T + t * P:i * T + (t + 1) * P],
                                                src[:, t, c * P:(c + 1) * P], ident[:])
                    last.then_inc(full, 1)

            def turn_qk(seg):
                pe.wait_ge(k_normed.sem, seg.of(k_normed, 1))
                turn_heads(seg, "kT", ks)
                pe.wait_ge(q_normed.sem, seg.of(q_normed, 1))
                turn_heads(seg, "qT", qs)

            BLOCKS = ((slice(0, T), 0, slice(0, T)), (slice(T, T + P), 1, slice(P, T)))

            def scores_a(seg, p):
                slot, n = pair_ring.place(seg, f"A{p}")
                pe.wait_ge(probs_ready[slot], n)
                for i in range(2):
                    head, rows = 2 * p + i, slice(i * DH, (i + 1) * DH)
                    for cols, s, toks in BLOCKS:
                        dst = score_banks[slot][:, i, cols]
                        keys = slice(s * P, (s + 1) * P)
                        pe.matmul(dst, dec_k[:, head, keys], dec_q[:, head, toks], start=True, stop=False)
                        pe.matmul(score_banks[slot][:, i, cols.start:cols.start + P], identb[:], mask[:],
                                  start=False, stop=False)
                        last = pe.matmul(dst, kT[rows, p, keys], qT[rows, p, toks], start=False, stop=True)
                return last.then_inc(scores_ready[slot], 1)

            def values(dst, pr, i, rhs, t):
                pe_last = pe.matmul(dst, pr[:, i, t * P:(t + 1) * P], rhs(0), start=True, stop=t == 0)
                if t == 1:
                    pe_last = pe.matmul(dst, pr[:, i, T:T + P], rhs(1), start=False, stop=True)
                return pe_last

            def values_a(seg, p):
                slot, n = pair_ring.place(seg, f"A{p}")
                o, m = out_ring.place(seg, f"A{p}")
                pe.wait_ge(probs_ready[slot], n + 1)
                pe.wait_ge(pv_freed[o], m)
                bank = out_banks[o][:, 0:4 * (DH + 1)].rearrange("p (t h d) -> p t h d", t=TT, h=2)
                for t in range(TT):
                    for i in range(2):
                        last = values(bank[:, t, i, :], probs[slot], i, lambda s: vs[:, s, 2 * p + i, :], t)
                last.then_inc(probs_used[slot], 1)

            def attention_a(seg):
                pe.wait_ge(decay_loaded.sem, seg.of(decay_loaded, 32))
                wait_used(pe, seg, [f"{m}T{u}" for m in "kq" for u in range(4)])
                for p in range(PAIRS + 1):
                    if p < PAIRS:
                        scores_a(seg, p)
                    if p >= 1:
                        values_a(seg, p - 1)

            def output_a(seg):
                pe.wait_ge(y_ready.sem, seg.of(y_ready, 1))
                turn_heads(seg, "yT", y)
                bank, full = take(seg, "attn_out")
                wait_used(pe, seg, [f"yT{u}" for u in range(4)])
                for t in range(TT):
                    for c in range(CT):
                        last = pe.matmul(bank[:, t * D:(t + 1) * D], yT[:, c, t * P:(t + 1) * P], wo_a[:, c, :],
                                         start=c == 0, stop=c == CT - 1)
                last.then_inc(full, 1)

            def qkv_b(seg):
                pe.wait_ge(h_ready.sem, seg.of(h_ready, TT))
                turn(seg, "hT", h)
                for t in range(TT):
                    bank, full = take(seg, f"qkv{t}")
                    pe.wait_ge(*used(seg, "hT"))
                    pe.matmul(bank[:, 0:3 * D], hT[:, t * P:(t + 1) * P], wqkv[:], start=True, stop=True)\
                      .then_inc(full, 1)

            def turn_pads(seg):
                for name, src, ready in (("qpT", q_pad, q_lo), ("kpT", k_pad, k_lo)):
                    pe.wait_ge(ready.sem, seg.of(ready, 1))
                    bank, full = take(seg, name)
                    dst = bank[:].bitcast(F16)
                    for j in range(4):
                        for t in range(TT):
                            lo = t * HB + 4 * j
                            last = pe.transpose(dst[:, j * T + t * P:j * T + (t + 1) * P],
                                                src[:, lo:lo + 4, :].rearrange("p h s -> p (h s)"), ident16[:])
                    last.then_inc(full, 1)

            def scores_b(seg, p):
                slot, n = pair_ring.place(seg, f"B{p}")
                pe.wait_ge(probs_ready[slot], n)
                for i in range(2):
                    j, r = divmod(2 * p + i, 4)
                    rows = slice(r * SLOT, r * SLOT + 3 * DB)
                    for cols, s, toks in BLOCKS:
                        pe.matmul(score_banks[slot][:, i, cols], kTb[rows, j, s * P:(s + 1) * P], qTb[rows, j, toks],
                                  start=True, stop=False)
                        last = pe.matmul(score_banks[slot][:, i, cols.start:cols.start + P], identb[:], mask[:],
                                         start=False, stop=True)
                last.then_inc(scores_ready[slot], 1)

            def values_b(seg, p):
                slot, n = pair_ring.place(seg, f"B{p}")
                pe.wait_ge(probs_ready[slot], n + 1)
                for t in range(TT):
                    o, m = out_ring.place(seg, f"B{t}")
                    if p == 0:
                        pe.wait_ge(pv_freed[o], m)
                    for i in range(2):
                        head = 2 * p + i
                        dst = out_banks[o][:, head * (DB + 1):(head + 1) * (DB + 1)]
                        last = values(dst, probs[slot], i, lambda s: vb[:, s, head, :], t)
                last.then_inc(probs_used[slot], 1)

            def attention_b(seg):
                wait_used(pe, seg, ["qpT", "kpT"])
                for p in range(PAIRS + 1):
                    if p < PAIRS:
                        scores_b(seg, p)
                    if p >= 1:
                        values_b(seg, p - 1)

            def output_b(seg):
                for t in range(TT):
                    o, m = out_ring.place(seg, f"B{t}")
                    pe.wait_ge(pv_freed[o], m + 1)
                turn(seg, "aT", ao[:].rearrange("p t h d -> p t (h d)"))
                for t in range(TT):
                    bank, full = take(seg, f"wo{t}")
                    pe.wait_ge(*used(seg, "aT"))
                    pe.matmul(bank[:, 0:D - MUTE], aT[:, t * P:(t + 1) * P], wo_b[:, MUTE:], start=True, stop=True)\
                      .then_inc(full, 1)

            def layer(seg, name, weights, inputs, cols=HID):
                bank, full = take(seg, name)
                for m in range(cols // P):
                    for k, (wt, src) in enumerate(zip(weights, inputs)):
                        last = pe.matmul(bank[:, m * T:(m + 1) * T], wt[:, m * P:(m + 1) * P], src,
                                         start=k == 0, stop=k == len(weights) - 1)
                last.then_inc(full, 1)

            def experts(seg):
                pe.wait_ge(xf_ready.sem, seg.of(xf_ready, TT))
                turn(seg, "xfT", xf)
                bank, full = take(seg, "route")
                pe.wait_ge(*used(seg, "xfT"))
                for t in range(TT):
                    last = pe.matmul(bank[:, t * NE:(t + 1) * NE], xfT[:, t * P:(t + 1) * P], gate_w[:],
                                     start=True, stop=True)
                last.then_inc(full, 1)
                layer(seg, "e0", [up0], [xfT[:]])
                layer(seg, "e1a", [up1], [xfT[:]])
                layer(seg, "e1b", [up2], [xfT[:]])
                layer(seg, "e2a", [l1], [xfT[:]])
                layer(seg, "e3a", [e3d], [xfT[:]], P)
                pe.wait_ge(*used(seg, "e2a"))
                layer(seg, "e2b", [l2[:, k, :] for k in range(2)], [h2a[:, k, :] for k in range(2)])
                pe.wait_ge(*used(seg, "e3a"))
                layer(seg, "e3b", [e3u], [h3a[:]])
                pe.wait_ge(*used(seg, "e2b"))
                layer(seg, "e2c", [l3[:, k, :] for k in range(2)], [h2b[:, k, :] for k in range(2)])
                wait_used(pe, seg, ["e0", "e1b", "e3b", "e2c"])
                for t in range(TT):
                    bank, full = take(seg, f"down{t}")
                    for e, hid in enumerate((h0, h1, h2c, h3b)):
                        for k in range(2):
                            last = pe.matmul(bank[:, e * P:e * P + D - MUTE], hid[:, k, t * P:(t + 1) * P],
                                             downs[e][:, k, MUTE:], start=k == 0, stop=k == 1)
                    last.then_inc(full, 1)

            run(pe, ("B", qkv_b), ("B", turn_pads), ("B", attention_b), ("B", output_b), ("B", experts),
                ("A", turn_x), ("A", gate_logits), ("A", lambda s: project(s, 0)), ("A", cumulate),
                ("A", lambda s: project(s, 1)), ("A", turn_qk), ("A", attention_a), ("A", output_a))


_NAMES = ["x", "Wq", "Wk", "Wv", "Wo", "Wf", "bf", "Wg", "qnw", "knw", "onw", "kconv_w", "vconv_w"]
_FFN = ["n1_w", "n2_w", "wq", "wk", "wv", "wo", "qn_w", "kn_w", "gate_w", "e0_up", "e0_down", "e1_w1", "e1_w2",
        "e1_down", "e2_l1", "e2_l2", "e2_l3", "e2_l4", "e3_down", "e3_up", "e3_out"]


def kernel(**inputs):
    import numpy as _np
    import concourse.bacc as _bacc
    from concourse import mybir as _mybir
    from concourse.bass_utils import run_bass_kernel_spmd as _run

    nc = _bacc.Bacc("TRN2", target_bir_lowering=False, num_devices=1)
    arrays, args = {}, {}
    for prefix, names in (("L0_attn_", _NAMES), ("L0_ffn_", _FFN)):
        for name in names:
            a = _np.ascontiguousarray(inputs[prefix + name])
            arrays[f"in_{prefix}{name}"] = a
            args[name] = nc.dram_tensor(f"in_{prefix}{name}", a.shape, _mybir.dt.from_np(a.dtype),
                                        kind="ExternalInput").ap()
    x = args.pop("x")
    out = nc.dram_tensor("out_0", tuple(x.shape), F32, kind="ExternalOutput").ap()
    build(nc, x, args, out)
    r = _run(nc, [arrays], core_ids=[0])
    return r.results[0]["out_0"]
```

```python
from contextlib import ExitStack

import numpy as np

import concourse.bass as bass
from concourse import mybir

F32 = mybir.dt.float32
F16 = mybir.dt.float16
I32 = mybir.dt.int32
BF16 = mybir.dt.bfloat16
ALU = mybir.AluOpType
ACT = mybir.ActivationFunctionType
X = mybir.AxisListType.X

P = 128
D = 128
T = 256
TT = T // P
H, DH = 16, 64
C = H * DH
CT = C // P
TAPS = 4
HB, DB = 16, 8
SLOT = 32
NE = 4
HID = 256
MUTE = 32
PAIRS = H // 2
HALF = 512
MASKED = -1.0e30
LN_EPS = 1e-5
EPS_A = 1e-6
EPS_B = 1.1920929e-07
ROOT_SEED = float(0x5F3759DF)
ROOT_ROUNDS = 3
SERIES = [1.0 / (2 * k + 1) for k in range(8, 0, -1)]

WORK = ([("A", f"{m}0{h}") for m in "kvqg" for h in range(2)]
        + [("B", "hT"), ("B", "qkv0"), ("B", "qkv1")]
        + [("A", f"{m}1{h}") for m in "kvqg" for h in range(2)]
        + [("B", "qpT"), ("B", "kpT"), ("X", "xT"), ("X", "gate_logits")]
        + [("A", f"{m}T{u}") for m in "kq" for u in range(4)]
        + [("B", "aT"), ("B", "wo0"), ("B", "wo1"), ("X", "cum"), ("B", "xfT")]
        + [("B", n) for n in ("route", "e0", "e1a", "e1b", "e2a", "e3a", "e2b", "e3b", "e2c", "down0", "down1")]
        + [("A", f"yT{u}") for u in range(4)] + [("A", "attn_out")])
ATTENTION = [("B", f"B{p}") for p in range(PAIRS)] + [("A", f"A{p}") for p in range(PAIRS)]
OUTPUTS = [("B", f"B{t}") for t in range(TT)] + [("A", f"A{p}") for p in range(PAIRS)]


class Segment:

    def __init__(self, name, reg, offset):
        self.name, self.reg, self.offset = name, reg, offset

    def scaled(self, per, const):
        return const if self.reg is None else self.reg * per + const

    def of(self, signal, n):
        return self.scaled(signal.per, self.offset[signal.block] * signal.per + n)


class Signal:

    def __init__(self, sem, block, per):
        self.sem, self.block, self.per = sem, block, per


class Ring:

    def __init__(self, size, uses, rounds):
        blocks = {"first": "X", "second": "XA", "third": "XAB", "loop": "XAB", "end": "AB", "last": "B"}
        self.order = {seg: [name for block, name in uses if block in blocks[seg]] for seg in blocks}
        self.size, both = size, len(uses)
        assert both % size == 0
        before = sum(len(self.order[seg]) for seg in ("first", "second"))
        self.base = {"first": 0, "second": len(self.order["first"]), "third": before, "loop": before,
                     "end": before + (rounds + 1) * both}
        self.base["last"] = self.base["end"] + len(self.order["end"])
        self.step = both // size

    def place(self, seg, name):
        n = self.base[seg.name] + self.order[seg.name].index(name)
        return n % self.size, seg.scaled(self.step, n // self.size)


def build(nc, x_in, w, out):
    NB = x_in.shape[0]
    rounds = NB - 3
    with ExitStack() as ctx:
        def sb(name, shape, dt=F32):
            return ctx.enter_context(nc.sbuf_tensor(name, shape, dt))

        def psum(name, shape, dt=F32):
            return ctx.enter_context(nc.psum_tensor(name, shape, dt))

        def sem(name):
            return ctx.enter_context(nc.semaphore(name))

        def signal(name, block, per):
            return Signal(sem(name), block, per)

        work_banks = [psum(f"work{i}", [P, HALF]) for i in range(2)]
        score_banks = [psum(f"scores{i}", [P, 2, HALF]) for i in range(2)]
        out_banks = [psum(f"pv{i}", [P, HALF]) for i in range(2)]

        ident = sb("ident", [P, P])
        ident16 = sb("ident16", [P, P], F16)
        identb = sb("identb", [P, P], BF16)
        mask = sb("mask", [P, P], BF16)
        tri = sb("tri", [P, T])
        before = sb("before", [P, TT, NE, NE])
        mhalf = sb("mhalf", [P, TT])
        eps = {n: sb(f"eps_{n}", [P, TT]) for n in ("ln", "z", "xf")}
        eps_value = {"ln": LN_EPS, "z": EPS_B, "xf": D * EPS_B}
        mark = sb("mark", [P, 1])
        bf_rows = sb("bf_rows", [P, H])
        w_row = sb("w_row", [P, C])
        w8 = sb("w8", [P, HB, DB])

        proj = {m: sb(f"w_{m}", [P, 2, TAPS if m in "kv" else 1, C], F16) for m in "kvqg"}
        wf = sb("wf", [P, 2, H], F16)
        wo_a = sb("wo_a", [P, 2, CT, D], F16)
        wqkv = sb("wqkv", [P, 2, 3 * D], F16)
        wo_b = sb("wo_b", [P, D])
        gate_w = sb("gate_wT", [P, 2, NE], F16)
        up0, up1, up2, l1 = (sb(n, [P, 2, HID], F16) for n in ("e0_upT", "e1_w1T", "e1_w2T", "e2_l1T"))
        l2, l3 = (sb(n, [P, 2, 2, HID], F16) for n in ("e2_l2T", "e2_l3T"))
        e3d = sb("e3_downT", [P, 2, D], F16)
        e3u = sb("e3_upT", [P, 2, HID], F16)
        downs = [sb(f"down{e}T", [P, 2, 2, D], F16) for e in range(NE)]

        arena = sb("arena", [P, 6 * 2048])
        o_sb = sb("o_sb", [P, TT, H, DH + 1])

        def region(i):
            return arena[:, i * 2048:(i + 1) * 2048]

        def tokens(ap, c=C):
            return ap.rearrange("p (t c) -> p t c", t=TT)

        def channels(ap):
            return ap.rearrange("p (c t) -> p c t", c=CT)

        ks, qs, gs = tokens(region(0)), tokens(region(1)), tokens(region(2))
        ksq, qsq = tokens(o_sb[:].rearrange("p t h d -> p (t h d)")[:, 0:TT * C]), tokens(region(3))

        def pair(ap):
            parts = ap.bitcast(F16).rearrange("p (a n) -> p a n", a=2)
            return [channels(parts[:, a, :]) for a in range(2)]

        qT, kT = pair(region(4)), pair(region(5))
        y, osq, yT = ks, qs, kT
        x_load = sb("x_load", [P, TT, D])
        x_keep = sb("x_keep", [P, TT, D])
        xn = sb("xn", [P, TT, D])
        xh = sb("xh", [P, TAPS - 1 + T], F16)
        xl = sb("xl", [P, TAPS - 1 + T], F16)
        tanh_a = sb("tanh_a", [P, 2, HALF])
        vs = sb("vs", [P, TT, H, DH + 1])
        probs = [sb(f"probs{i}", [P, 2, 3 * P]) for i in range(2)]
        fz, fneg, fe, fd, fr, fw, fw2, fq, fmin, fl = (sb(f"f{i}", [P, TT, H]) for i in range(10))
        c_res = sb("c_res", [H, T])
        c_res2 = sb("c_res2", [H, T])
        c_parts = sb("c_parts", [H, 3, T], BF16)
        dec_k = sb("dec_k", [6, H, T], BF16)
        dec_q = sb("dec_q", [6, H, T], BF16)
        c_dram = nc.dram_tensor("c_scratch", (2, H, 3, T), BF16, kind="Internal").ap()
        stats_a = sb("stats_a", [P, TT, 6])
        mv_a = sb("mv_a", [P, TT, 2])
        rs_a = sb("rs_a", [P, TT])
        t_a = sb("t_a", [P, TT])
        stats_o = sb("stats_o", [P, TT, 6])
        mv_o = sb("mv_o", [P, TT, 2])
        rs_o = sb("rs_o", [P, TT])
        t_o = sb("t_o", [P, TT])
        ss_qk, v_qk, a_qk, y_qk, r_qk = (sb(f"root_qk{i}", [P, 2, TT, H]) for i in range(5))
        sso, v_o, a_o, y_o, r_o = (sb(f"root_o{i}", [P, TT, H]) for i in range(5))
        x1 = sb("x1", [P, TT, D])

        x1_keep = sb("x1_keep", [P, TT, D])
        stats_b = sb("stats_b", [P, TT, 6])
        mv_b = sb("mv_b", [P, TT, 2])
        rs_b, t_b, v_b, u_b, r2_b, rz_b = (sb(f"b{i}", [P, TT]) for i in range(6))
        flow_b = sb("flow_b", [P, 4, TT * D])
        z, h = (flow_b[:, i].rearrange("p (t d) -> p t d", t=TT) for i in range(2))
        qk = flow_b[:, 2:4].rearrange("p t (a h d) -> p t a h d", a=2, h=HB)
        gelu32 = [flow_b[:, 2 * i:2 * i + 2].rearrange("p a n -> p (a n)") for i in range(2)]
        wo_raw = flow_b[:].rearrange("p a (b d) -> p (a b) d", d=D)
        hT = sb("hT", [P, 2, T], F16)
        tanh_b = sb("tanh_b", [P, 2 * T])
        qk_sq = tanh_b[:].rearrange("p (t a h d) -> p t a h d", t=TT, a=2, h=HB)
        ss_b, v_b2, a_b2, y_b2, rr_b = (sb(f"root_b{i}", [P, TT, 2 * HB]) for i in range(5))
        vb = sb("vb", [P, TT, HB, DB + 1])
        q_pad = sb("q_pad", [P, TT * HB, SLOT], F16)
        k_pad = sb("k_pad", [P, TT * HB, SLOT], F16)
        qTb = sb("qTb", [P, 4, T], F16)
        kTb = sb("kTb", [P, 4, T], F16)
        rden = sb("rden", [P, TT, HB])
        ao = sb("ao", [P, TT, HB, DB])
        aT = sb("aT", [P, T])
        x2 = sb("x2", [P, TT, D])
        ss_f, t_f, rs_f = (sb(f"xf{i}", [P, TT]) for i in range(3))
        xf = sb("xf", [P, TT, D])
        x2_sq = ex_out = xf
        xfT = sb("xfT", [P, 2, T], F16)
        lg, ls, ex, pr, sel, top = (sb(f"g{i}", [P, TT, NE]) for i in range(6))
        mx, es, er, tsum, trec = (sb(f"gs{i}", [P, TT]) for i in range(5))
        gt, ge, cnt = (sb(f"gg{i}", [P, TT, NE, NE]) for i in range(3))
        rank = sb("rank", [P, TT, NE])
        wts = sb("wts", [P, TT, NE])
        h0, h1, h2a, h2b, h3b = (sb(f"hid{i}", [P, 2, 2, T], F16) for i in range(5))
        h2c = h2a
        h3a = sb("h3a", [P, 2, 1, T], F16)
        stats_f = sb("stats_f", [P, TT, 6])
        mv_f = sb("mv_f", [P, TT, 2])
        rs_x, t_x = (sb(f"fx{i}", [P, TT]) for i in range(2))
        o_fin = sb("o_fin", [P, TT, D])

        s_load = sem("weights_loaded")
        s_const = sem("constants_made")
        s_tr = sem("weights_transposed")
        s_trc = sem("transposed_copied")
        s_init = sem("buffers_cleared")
        pool_init = sem("pool_setup_step")
        dve_init = sem("dve_setup_step")

        x_loaded = signal("x_loaded", "X", 16)
        x_copied = signal("x_kept", "A", 16)
        a_stats = signal("a_stats", "X", 4)
        a_rstd = signal("a_rstd", "X", 2)
        xn_ready = signal("xn_ready", "X", TT)
        xh_ready = signal("xh_ready", "X", 1)
        gate_abs = signal("gate_abs", "X", 3)
        gate_exp = signal("gate_exp", "X", 1)
        gate_log = signal("gate_log", "X", 5 + len(SERIES) + 1)
        cum_split = signal("cum_split", "X", 5)
        cum_stored = signal("cum_stored", "X", 16)
        decay_loaded = signal("decay_loaded", "X", 32)
        tanh_a_ready = signal("tanh_a_ready", "A", 12)
        q_squared = signal("q_squared", "A", 4)
        k_squared = signal("k_squared", "A", 4)
        q_summed = signal("q_summed", "A", 4)
        k_summed = signal("k_summed", "A", 4)
        qk_scale = signal("qk_scale", "A", 12)
        k_normed = signal("k_normed", "A", 1)
        q_normed = signal("q_normed", "A", 1)
        o_squared = signal("o_squared", "A", 2)
        o_summed = signal("o_summed", "A", 2)
        o_scale = signal("o_scale", "A", 12)
        o_normed = signal("o_normed", "A", TT)
        y_ready = signal("y_ready", "A", TT)
        o_stats = signal("o_stats", "A", 4)
        o_rstd = signal("o_rstd", "A", 2)
        o_ln_ready = signal("o_ln_ready", "A", 1)
        hi_a = signal("hi_a", "A", 12)
        x1_ready = signal("x1_ready", "A", 1)

        x1_copied = signal("x1_copied", "B", 1)
        b_stats = signal("b_stats", "B", 4)
        b_rstd = signal("b_rstd", "B", 7)
        z_ready = signal("z_ready", "B", TT)
        h_ready = signal("h_ready", "B", TT)
        hT_hi = signal("hT_hi", "B", 1)
        xfT_hi = signal("xfT_hi", "B", 1)
        hid_hi = signal("hid_hi", "B", 7)
        hid_lo = signal("hid_lo", "B", 7)
        qk_copied = signal("qk_copied", "B", TT)
        qk_squared = signal("qk_squared", "B", 1)
        qk_summed = signal("qk_summed", "B", 1)
        b_scale = signal("b_scale", "B", 11)
        qk_normed = signal("qk_normed", "B", 1)
        q_weighted = signal("q_weighted", "B", 1)
        k_hi, k_lo = signal("k_hi", "B", 2), signal("k_lo", "B", 1)
        q_hi, q_lo = signal("q_hi", "B", 2), signal("q_lo", "B", 1)
        pads_T = signal("pads_T", "B", 2)
        den_ready = signal("den_ready", "B", TT)
        x2_head = signal("x2_head", "B", 1)
        x2_squared = signal("x2_squared", "B", 1)
        x2_summed = signal("x2_summed", "B", 1)
        x2_rms = signal("x2_rms", "B", 2)
        xf_ready = signal("xf_ready", "B", TT)
        route_max = signal("route_max", "B", 2)
        route_shift = signal("route_shift", "B", 1)
        route_exp = signal("route_exp", "B", 1)
        route_dve = signal("route_dve", "B", 5)
        route_cmp = signal("route_cmp", "B", 4)
        route_sel = signal("route_sel", "B", 1)
        route_recip = signal("route_recip", "B", 2)
        wts_ready = signal("wts_ready", "B", 1)
        tanh_b_ready = signal("tanh_b_ready", "B", 1)
        mixed = signal("mixed", "B", TT * (NE - 1))
        f_stats = signal("f_stats", "B", 4)
        f_rstd = signal("f_rstd", "B", 2)
        f_norm = signal("f_norm", "B", TT)
        out_ready = signal("out_ready", "B", 1)
        out_stored = signal("out_stored", "B", 16)

        work = Ring(2, WORK, rounds)
        work_filled = [sem(f"work_filled{i}") for i in range(2)]
        work_freed = [sem(f"work_freed{i}") for i in range(2)]
        pair_ring = Ring(2, ATTENTION, rounds)
        scores_ready = [sem(f"scores_ready{i}") for i in range(2)]
        probs_ready = [sem(f"probs_ready{i}") for i in range(2)]
        probs_used = [sem(f"probs_used{i}") for i in range(2)]
        out_ring = Ring(2, OUTPUTS, rounds)
        pv_freed = [sem(f"pv_freed{i}") for i in range(2)]

        def work_of(seg, name):
            slot, before_it = work.place(seg, name)
            return work_banks[slot], slot, before_it

        def used(seg, name):
            slot, before_it = work.place(seg, name)
            return work_freed[slot], before_it + 1

        def wait_used(eng, seg, names):
            latest = {}
            for name in names:
                latest[work.place(seg, name)[0]] = name
            for name in latest.values():
                eng.wait_ge(*used(seg, name))

        def multiplied(seg, pair):
            slot, before_it = pair_ring.place(seg, pair)
            return probs_used[slot], before_it + 1

        def run(engine, *stages):
            def play(seg):
                for block, stage in stages:
                    if block in seg.offset:
                        stage(seg)

            play(Segment("first", None, {"X": 0}))
            play(Segment("second", None, {"X": 1, "A": 0}))
            play(Segment("third", None, {"X": 2, "A": 1, "B": 0}))
            with engine.Fori(1, rounds + 1) as i:
                play(Segment("loop", i, {"X": 2, "A": 1, "B": 0}))
            play(Segment("end", None, {"A": NB - 1, "B": NB - 2}))
            play(Segment("last", None, {"B": NB - 1}))

        spares = [a[:].rearrange("p t h d -> p (t h d)") for a in (o_sb, vs)]
        stage_conv = {"k": arena[:, 0:4096], "v": arena[:, 4096:8192]}
        stage_proj = {m: arena[:, 8192 + i * C:8192 + (i + 1) * C] for i, m in enumerate("kvqg")}
        fold = tanh_a[:].rearrange("p a c -> p (a c)")
        n1 = sb("n1w_col", [P, 1])
        n2 = sb("n2w_col", [P, 1])
        onw2 = sb("onw2", [P, 1])
        q8, k8 = sb("q8", [P, DB]), sb("k8", [P, DB])
        wf_raw = sb("wf_raw", [P, H])
        small = sb("small", [P, DB])

        flips, at = [], [0]

        def source(name, rows, cols):
            n = -(-rows // P) * cols
            lo = at[0]
            at[0] += n
            ap = spares[lo // 2048][:, lo % 2048:lo % 2048 + n]
            return name, rows, cols, ap.rearrange("p (r c) -> p r c", c=cols)

        groups = [([source("wq", D, D), source("wk", D, D), source("wv", D, D)], n1, wqkv[:]),
                  ([source("wo", D, D)], None, wo_b[:]),
                  ([source("e0_up", HID, D)], n2, up0[:]),
                  ([source("e1_w1", HID, D)], n2, up1[:]),
                  ([source("e1_w2", HID, D)], n2, up2[:]),
                  ([source("e2_l1", HID, D)], n2, l1[:]),
                  ([source("e3_down", D, D)], n2, e3d[:]),
                  ([source("e3_up", HID, D)], None, e3u[:]),
                  ([source("gate_w", NE, D)], n2, gate_w[:])]
        at[0] = max(at[0], 2048)
        groups += [([source("e2_l2", HID, HID)], None, l2[:]),
                   ([source("e2_l3", HID, HID)], None, l3[:]),
                   ([source("e0_down", D, HID)], None, downs[0][:]),
                   ([source("e1_down", D, HID)], 0.5, downs[1][:]),
                   ([source("e2_l4", D, HID)], None, downs[2][:]),
                   ([source("e3_out", D, HID)], None, downs[3][:])]
        sources = [s for g in groups for s in g[0]]
        n_loads = [0]

        block = ctx.enter_context(nc.Block())

        def row(ap):
            return ap.rearrange("(o n) -> o n", o=1)

        setup_loads = (
            [(stage_proj[m], w[f"W{m}"]) for m in "kvqg"]
            + [(stage_conv[m], w[f"{m}conv_w"].rearrange("(o c) j -> o (c j)", o=1).partition_broadcast(P)) for m in "kv"]
            + [(wf_raw[:], w["Wf"]), (bf_rows[:], w["bf"].partition_broadcast(P)),
               (w_row[:], w["qnw"].partition_broadcast(P)), (fold, w["knw"].partition_broadcast(P)),
               (q8[:], w["qn_w"].partition_broadcast(P)), (k8[:], w["kn_w"].partition_broadcast(P)),
               (n1[:], w["n1_w"].rearrange("(p o) -> p o", o=1)), (n2[:], w["n2_w"].rearrange("(p o) -> p o", o=1)),
               (onw2[0:DH, :], w["onw"].rearrange("(p o) -> p o", o=1)),
               (onw2[DH:P, :], w["onw"].rearrange("(p o) -> p o", o=1)),
               (wo_raw[:], w["Wo"].rearrange("(c p) d -> p c d", p=P))]
            + [(ap if rows % P == 0 else ap[0:rows], w[name].rearrange("(r p) c -> p r c", p=min(P, rows)))
               for name, rows, cols, ap in sources])
        loads_total = 16 * len(setup_loads)

        @block.sync
        def _(sp):
            for dst, src in setup_loads:
                sp.dma_start(dst, src, allow_slow_non_contiguous=True).then_inc(s_load, 16)

            def batch(seg, block):
                b = seg.scaled(1, seg.offset[block])
                return b if seg.reg is None else sp.snap(b)

            def tokens_of(ap, b):
                ap = ap[b] if isinstance(b, int) else ap[bass.ds(b, 1)].rearrange("o t d -> (o t) d")
                return ap.rearrange("(t p) d -> p t d", p=P)

            def load_x(seg):
                b = batch(seg, "X")
                sp.wait_ge(xn_ready.sem, seg.of(xn_ready, 0))
                sp.dma_start(x_load[:], tokens_of(x_in, b)).then_inc(x_loaded.sem, 16)

            def load_residual(seg):
                b = batch(seg, "A")
                sp.wait_ge(x1_ready.sem, seg.of(x1_ready, 0))
                sp.dma_start(x_keep[:], tokens_of(x_in, b)).then_inc(x_copied.sem, 16)

            def move_cum(seg):
                sp.wait_ge(decay_loaded.sem, seg.of(decay_loaded, 0))
                sp.wait_ge(cum_split.sem, seg.of(cum_split, 5))
                sp.dma_start(c_dram[0], c_parts[:]).then_inc(cum_stored.sem, 16)
                sp.wait_ge(cum_stored.sem, seg.of(cum_stored, 16))
                if "A" in seg.offset:
                    sp.wait_ge(*multiplied(seg, f"A{PAIRS - 1}"))
                else:
                    sp.wait_ge(s_init, 1)
                src = c_dram[0].rearrange("h p t -> p h t")
                sp.dma_start(dec_q[0:3], src).then_inc(decay_loaded.sem, 16)
                sp.dma_start(dec_k[3:6], src).then_inc(decay_loaded.sem, 16)

            def store(seg):
                b = batch(seg, "B")
                sp.wait_ge(out_ready.sem, seg.of(out_ready, 1))
                sp.dma_start(tokens_of(out, b), o_fin[:]).then_inc(out_stored.sem, 16)

            run(sp, ("X", load_x), ("A", load_residual), ("X", move_cum), ("B", store))
            sp.wait_ge(out_stored.sem, 16 * NB)

        LO_OF = [0, 1, 3, 4, 5, 6]

        @block.gpsimd
        def _(pool):
            steps = [0]

            def step(ins):
                steps[0] += 1
                ins.then_inc(pool_init, 1)
                pool.wait_ge(pool_init, steps[0])

            step(pool.memset(ident[:], 1.0))
            step(pool.affine_select(out=ident[:], in_=ident[:], compare_op=ALU.is_equal, fill=0.0, base=0,
                                    pattern=[[-1, P]], channel_multiplier=1))
            step(pool.tensor_copy(ident16[:], ident[:]))
            step(pool.tensor_copy(identb[:], ident[:]))
            step(pool.memset(tri[:], 1.0))
            step(pool.affine_select(out=tri[:], in_=tri[:], compare_op=ALU.is_ge, fill=0.0, base=0,
                                    pattern=[[1, T]], channel_multiplier=-1))
            step(pool.memset(mask[:], 0.0))
            step(pool.affine_select(out=mask[:], in_=mask[:], compare_op=ALU.is_ge, fill=MASKED, base=0,
                                    pattern=[[1, P]], channel_multiplier=-1))
            step(pool.memset(before[:], 1.0))
            step(pool.affine_select(out=before[:], in_=before[:], compare_op=ALU.is_gt, fill=0.0, base=0,
                                    pattern=[[0, TT], [1, NE], [-1, NE]], channel_multiplier=0))
            for name, tile in eps.items():
                step(pool.memset(tile[:], eps_value[name]))
            pool.memset(mhalf[:], -0.5).then_inc(s_const, 1)
            step(pool.memset(dec_k[:], 1.0))
            step(pool.memset(dec_q[:], -1.0))
            step(pool.memset(xh[:, 0:TAPS - 1], 0.0))
            step(pool.memset(xl[:, 0:TAPS - 1], 0.0))
            step(pool.memset(q_pad[:], 0.0))
            step(pool.memset(k_pad[:], 0.0))
            step(pool.memset(vb[:, :, :, DB], 1.0))
            pool.wait_ge(s_trc, len(groups))
            pool.memset(vs[:, :, :, DH], 1.0).then_inc(s_init, 1)
            pool.wait_ge(s_init, 1)

            def flat(ap):
                return ap.rearrange("p t h -> p (t h)")

            def rsqrt(seg, done, n, dst, src, name, tmp):
                cols = src.shape[-1]
                pool.tensor_tensor(tmp, src, eps[name][:, 0:cols], ALU.add).then_inc(done.sem, 1)
                pool.wait_ge(done.sem, seg.of(done, n))
                pool.tensor_tensor(dst, tmp, mhalf[:, 0:cols], ALU.pow).then_inc(done.sem, 1)

            def rstd_a(seg):
                pool.wait_ge(a_stats.sem, seg.of(a_stats, 4))
                rsqrt(seg, a_rstd, 1, rs_a[:], mv_a[:, :, 1], "ln", t_a[:])

            def square_k(seg, t):
                for half in range(2):
                    lo = half * HALF
                    pool.wait_ge(*used(seg, f"k{t}{half}"))
                    pool.tensor_tensor(ksq[:, t, lo:lo + HALF], ks[:, t, lo:lo + HALF], ks[:, t, lo:lo + HALF],
                                       ALU.mult).then_inc(k_squared.sem, 1)

            def heads(ap):
                return ap.rearrange("p t (h d) -> p (t h) d", d=DH)

            def spread(ap, n):
                return ap.rearrange("p t h -> p (t h)").unsqueeze(2).broadcast_to([P, TT * H, n])

            def norm_qk(seg):
                wait_used(pool, seg, [f"q1{half}" for half in range(2)])
                pool.wait_ge(qk_scale.sem, seg.of(qk_scale, 12))
                pool.tensor_tensor(heads(ks), heads(ks), spread(r_qk[:, 0], DH), ALU.mult).then_inc(k_normed.sem, 1)
                pool.tensor_tensor(heads(qs), heads(qs), spread(r_qk[:, 1], DH), ALU.mult).then_inc(q_normed.sem, 1)

            def square_o(seg, half):
                hh = slice(half * 8, half * 8 + 8)
                if half == 0:
                    pool.wait_ge(*used(seg, "qT3"))
                for p in (4 * half + 2, 4 * half + 3):
                    slot, n = out_ring.place(seg, f"A{p}")
                    pool.wait_ge(pv_freed[slot], n + 1)
                num = o_sb[:, :, hh, 0:DH]
                pool.tensor_tensor(osq.rearrange("p t (h d) -> p t h d", d=DH)[:, :, hh, :], num, num, ALU.mult)\
                    .then_inc(o_squared.sem, 1)

            def norm_o(seg):
                pool.wait_ge(o_scale.sem, seg.of(o_scale, 12))
                for t in range(TT):
                    pool.tensor_tensor(y[:, t].rearrange("p (h d) -> p h d", d=DH), o_sb[:, t, :, 0:DH],
                                       r_o[:, t].unsqueeze(2).broadcast_to([P, H, DH]), ALU.mult)\
                        .then_inc(o_normed.sem, 1)

            def rstd_o(seg):
                pool.wait_ge(o_stats.sem, seg.of(o_stats, 4))
                rsqrt(seg, o_rstd, 1, rs_o[:], mv_o[:, :, 1], "ln", t_o[:])

            def rstd_b(seg):
                def link(n, ins):
                    ins.then_inc(b_rstd.sem, 1)
                    pool.wait_ge(b_rstd.sem, seg.of(b_rstd, n))

                pool.wait_ge(b_stats.sem, seg.of(b_stats, 4))
                link(1, pool.tensor_tensor(t_b[:], mv_b[:, :, 1], eps["ln"][:, 0:TT], ALU.add))
                link(2, pool.tensor_tensor(rs_b[:], t_b[:], mhalf[:, 0:TT], ALU.pow))
                link(3, pool.tensor_tensor(v_b[:], mv_b[:, :, 1], rs_b[:], ALU.mult))
                link(4, pool.tensor_tensor(u_b[:], v_b[:], rs_b[:], ALU.mult))
                link(5, pool.tensor_tensor(u_b[:], u_b[:], eps["z"][:, 0:TT], ALU.add))
                link(6, pool.tensor_tensor(r2_b[:], u_b[:], mhalf[:, 0:TT], ALU.pow))
                pool.tensor_tensor(rz_b[:], rs_b[:], r2_b[:], ALU.mult).then_inc(b_rstd.sem, 1)

            def norm_b(seg):
                f = "p t a h d -> p (t a h) d"
                pool.wait_ge(qk_copied.sem, seg.of(qk_copied, TT))
                pool.tensor_tensor(qk_sq[:], qk[:], qk[:], ALU.mult).then_inc(qk_squared.sem, 1)
                pool.wait_ge(b_scale.sem, seg.of(b_scale, 11))
                r = rr_b[:].rearrange("p t h -> p (t h)").unsqueeze(2).broadcast_to([P, TT * 2 * HB, DB])
                pool.tensor_tensor(qk[:].rearrange(f), qk[:].rearrange(f), r, ALU.mult).then_inc(qk_normed.sem, 1)
                pool.wait_ge(qk_normed.sem, seg.of(qk_normed, 1))
                wb = w8[:].rearrange("p h d -> p (h d)").unsqueeze(1).broadcast_to([P, TT, HB * DB])
                qq = qk[:].rearrange("p t a h d -> p t a (h d)")[:, :, 0, :]
                pool.tensor_tensor(qq, qq, wb, ALU.mult).then_inc(q_weighted.sem, 1)

            def square_x2(seg):
                wait_used(pool, seg, [f"wo{t}" for t in range(TT)])
                pool.wait_ge(x2_head.sem, seg.of(x2_head, 1))
                pool.tensor_tensor(x2_sq[:], x2[:], x2[:], ALU.mult).then_inc(x2_squared.sem, 1)
                pool.wait_ge(x2_summed.sem, seg.of(x2_summed, 1))
                rsqrt(seg, x2_rms, 1, rs_f[:], ss_f[:], "xf", t_f[:])

            def route(seg):
                pool.wait_ge(route_max.sem, seg.of(route_max, 2))
                pool.tensor_tensor(ls[:], lg[:], mx[:].unsqueeze(2).broadcast_to([P, TT, NE]),
                                   ALU.subtract).then_inc(route_shift.sem, 1)
                pool.wait_ge(route_cmp.sem, seg.of(route_cmp, 2))
                pool.tensor_tensor(ge[:], ge[:], before[:], ALU.mult).then_inc(route_cmp.sem, 1)
                pool.wait_ge(route_cmp.sem, seg.of(route_cmp, 3))
                pool.tensor_tensor(cnt[:], gt[:], ge[:], ALU.add).then_inc(route_cmp.sem, 1)

            def rstd_f(seg):
                pool.wait_ge(f_stats.sem, seg.of(f_stats, 4))
                rsqrt(seg, f_rstd, 1, rs_x[:], mv_f[:, :, 1], "ln", t_x[:])

            run(pool, ("B", rstd_b), ("A", lambda s: square_k(s, 0)), ("B", norm_b), ("A", lambda s: square_k(s, 1)),
                ("X", rstd_a), ("A", norm_qk), ("A", lambda s: square_o(s, 0)), ("B", square_x2), ("B", route),
                ("A", lambda s: square_o(s, 1)), ("A", norm_o), ("B", rstd_f), ("A", rstd_o))

        @block.scalar
        def _(act):
            act.wait_ge(s_init, 1)

            def filled(seg, name):
                bank, slot, n = work_of(seg, name)
                act.wait_ge(work_filled[slot], n + 1)
                return bank, slot

            tanh_units = [f"{m}{t}{half}" for t in range(TT) for m in "kvg" for half in range(2)]

            def copy_xT(seg):
                bank, _ = filled(seg, "xT")
                act.activation(xh[:, TAPS - 1:], bank[:, 0:T], ACT.Copy).then_inc(xh_ready.sem, 1)

            def gate(seg):
                act.wait_ge(gate_abs.sem, seg.of(gate_abs, 3))
                act.activation(fe[:], fneg[:], ACT.Exp).then_inc(gate_exp.sem, 1)

            def projected(seg, t):
                n = 6 * t
                for m in "kvqg":
                    for half in range(2):
                        bank, slot = filled(seg, f"{m}{t}{half}")
                        lo = half * HALF
                        if m == "q":
                            act.activation(qsq[:, t, lo:lo + HALF], bank[:], ACT.Square).then_inc(q_squared.sem, 1)
                        else:
                            if n >= 2:
                                act.wait_ge(*used(seg, tanh_units[n - 2]))
                            act.activation(tanh_a[:, n % 2, :], bank[:], ACT.Tanh, scale=0.5)\
                               .then_inc(tanh_a_ready.sem, 1)
                            n += 1

            def turned(seg, name, dst):
                for u in range(4):
                    bank, slot = filled(seg, f"{name}{u}")
                    act.activation(dst[0][:, 2 * u:2 * u + 2, :].rearrange("p c t -> p (c t)"), bank[:], ACT.Copy)\
                       .then_inc(hi_a.sem, 1)

            def exps(seg, block, pairs):
                for p in pairs:
                    slot, n = pair_ring.place(seg, f"{block}{p}")
                    act.wait_ge(scores_ready[slot], n + 1)
                    act.wait_ge(probs_used[slot], n)
                    act.activation(probs[slot][:], score_banks[slot][:, :, 0:3 * P], ACT.Exp)\
                       .then_inc(probs_ready[slot], 1)

            def keep(seg):
                act.wait_ge(out_ready.sem, seg.of(out_ready, 0))
                act.wait_ge(x1_ready.sem, seg.scaled(1, seg.offset["B"] + 1))
                act.activation(x1_keep[:], x1[:], ACT.Copy).then_inc(x1_copied.sem, 1)
                act.wait_ge(z_ready.sem, seg.of(z_ready, TT))
                act.wait_ge(f_norm.sem, seg.of(f_norm, 0))
                act.activation(x2[:, :, 0:MUTE], z[:, :, 0:MUTE], ACT.Copy).then_inc(x2_head.sem, 1)

            def copy_hT(seg):
                bank, _ = filled(seg, "hT")
                act.activation(hT[:, 0], bank[:, 0:T], ACT.Copy).then_inc(hT_hi.sem, 1)

            def copy_qkv(seg):
                for t in range(TT):
                    bank, slot = filled(seg, f"qkv{t}")
                    if t == 0:
                        act.wait_ge(k_lo.sem, seg.of(k_lo, 0))
                        act.wait_ge(q_lo.sem, seg.of(q_lo, 0))
                    act.activation(qk[:, t].rearrange("p a h d -> p (a h d)"), bank[:, 0:2 * D], ACT.Copy)\
                       .then_inc(qk_copied.sem, 1)
                    act.activation(vb[:, t, :, 0:DB], bank[:, 2 * D:3 * D].rearrange("p (h d) -> p h d", d=DB),
                                   ACT.Copy).then_inc(work_freed[slot], 1)

            def copy_pads(seg):
                for name, dst in (("qpT", qTb), ("kpT", kTb)):
                    bank, slot = filled(seg, name)
                    act.activation(dst[:].rearrange("p j t -> p (j t)"), bank[:].bitcast(F16), ACT.Copy)\
                       .then_inc(work_freed[slot], 1)

            def copy_aT(seg):
                bank, slot = filled(seg, "aT")
                act.activation(aT[:], bank[:, 0:T], ACT.Copy).then_inc(work_freed[slot], 1)

            def copy_xfT(seg):
                bank, _ = filled(seg, "xfT")
                act.activation(xfT[:, 0], bank[:, 0:T], ACT.Copy).then_inc(xfT_hi.sem, 1)

            def route(seg):
                act.wait_ge(route_shift.sem, seg.of(route_shift, 1))
                act.activation(ex[:], ls[:], ACT.Exp).then_inc(route_exp.sem, 1)

            def experts(seg):
                n = [0]

                def gelu(name, dst):
                    cols = dst.shape[2] * T
                    bank, slot = filled(seg, name)
                    if n[0] >= 2:
                        act.wait_ge(hid_lo.sem, seg.of(hid_lo, LO_OF[n[0] - 2] + 1))
                    act.activation(gelu32[n[0] % 2][:, 0:cols], bank[:, 0:cols], ACT.Gelu).then_inc(hid_hi.sem, 1)
                    act.activation(dst[:, 0].rearrange("p c t -> p (c t)"), bank[:, 0:cols], ACT.Gelu)\
                       .then_inc(work_freed[slot], 1)
                    n[0] += 1

                gelu("e0", h0)
                bank, slot = filled(seg, "e1a")
                act.activation(tanh_b[:], bank[:], ACT.Tanh, scale=0.5).then_inc(tanh_b_ready.sem, 1)
                gelu("e2a", h2a)
                act.wait_ge(*used(seg, "e1b"))
                act.activation(h1[:, 0].rearrange("p c t -> p (c t)"), tanh_b[:], ACT.Copy).then_inc(hid_hi.sem, 1)
                gelu("e3a", h3a)
                gelu("e2b", h2b)
                gelu("e3b", h3b)
                gelu("e2c", h2c)

            run(act, ("A", lambda s: projected(s, 0)), ("B", keep), ("B", copy_hT), ("B", copy_qkv),
                ("A", lambda s: projected(s, 1)), ("B", copy_pads), ("X", copy_xT),
                ("B", lambda s: exps(s, "B", range(0, 4))), ("X", gate), ("B", lambda s: exps(s, "B", range(4, 8))),
                ("A", lambda s: turned(s, "kT", kT)), ("A", lambda s: turned(s, "qT", qT)),
                ("A", lambda s: exps(s, "A", range(0, 2))), ("B", copy_aT),
                ("A", lambda s: exps(s, "A", range(2, 6))), ("B", copy_xfT), ("A", lambda s: exps(s, "A", range(6, 8))),
                ("B", route), ("B", experts), ("A", lambda s: turned(s, "yT", yT)))

        @block.vector
        def _(dve):
            dve.wait_ge(s_load, loads_total)
            steps = [0]

            def step(ins):
                steps[0] += 1
                ins.then_inc(dve_init, 1)
                dve.wait_ge(dve_init, steps[0])

            def split(src, hi, lo):
                step(dve.tensor_copy(hi, src))
                step(dve.tensor_tensor(lo, src, hi, ALU.subtract))

            step(dve.scalar_tensor_tensor(out=w_row[:], in0=w_row[:], scalar=float(DH) * DH ** -0.5, in1=fold,
                                          op0=ALU.mult, op1=ALU.mult))
            for m in "kv":
                for j in range(TAPS):
                    taps = stage_conv[m].rearrange("p (c j) -> p c j", j=TAPS)[:, :, j]
                    step(dve.tensor_tensor(fold, stage_proj[m], taps, ALU.mult))
                    split(fold, proj[m][:, 0, j, :], proj[m][:, 1, j, :])
            for m in "qg":
                split(stage_proj[m], proj[m][:, 0, 0, :], proj[m][:, 1, 0, :])
            split(wf_raw[:], wf[:, 0, :], wf[:, 1, :])
            wo_flat = wo_raw[:].rearrange("p c d -> p (c d)")
            step(dve.tensor_scalar(wo_flat, wo_flat, onw2[:, 0:1], 0.5 * DH ** 0.5, ALU.mult, ALU.mult))
            split(wo_flat, wo_a[:, 0].rearrange("p c d -> p (c d)"), wo_a[:, 1].rearrange("p c d -> p (c d)"))
            step(dve.tensor_scalar(n2[:], n2[:], float(D) ** 0.5, None, ALU.mult))
            step(dve.tensor_tensor(small[:], q8[:], k8[:], ALU.mult))
            step(dve.tensor_scalar(w8[:], small[:].unsqueeze(1).broadcast_to([P, HB, DB]), float(DB) * DB ** -0.5, None,
                                   ALU.mult))
            for n, (srcs, scale, dst) in enumerate(groups):
                cols = sum(-(-r // P) * c if r >= P else r for _, r, c, _ in srcs)
                bank = work_banks[n % 2][:, 0:cols]
                dve.wait_ge(s_tr, n + 1)
                s = 1.0 if scale is None else scale if isinstance(scale, float) else scale[:, 0:1]
                if len(dst.shape) == 2:
                    dve.tensor_scalar(dst, bank, s, None, ALU.mult).then_inc(s_trc, 1)
                    continue
                hi, lo = (dst[:, a] if len(dst.shape) == 3 else dst[:, a].rearrange("p a b -> p (a b)")
                          for a in range(2))
                step(dve.tensor_scalar(hi, bank, s, None, ALU.mult))
                dve.scalar_tensor_tensor(out=lo, in0=bank, scalar=s, in1=hi, op0=ALU.mult, op1=ALU.subtract)\
                   .then_inc(s_trc, 1)
            dve.wait_ge(s_init, 1)

            def filled(seg, name):
                bank, slot, n = work_of(seg, name)
                dve.wait_ge(work_filled[slot], n + 1)
                return bank, slot

            def stats(seg, done, src, st, mv):
                for t in range(TT):
                    dve.bn_stats(st[:, t, :], src(t)).then_inc(done.sem, 1)
                dve.wait_ge(done.sem, seg.of(done, TT))
                dve.memset(mark[:], 0.0)
                for t in range(TT):
                    dve.bn_aggr(mv[:, t, :], st[:, t, :]).then_inc(done.sem, 1)

            def root(seg, done, n, dst, v, a, y):
                def link(ins, k, wait=True):
                    ins.then_inc(done.sem, 1)
                    if wait:
                        dve.wait_ge(done.sem, seg.of(done, k))

                dve.wait_ge(done.sem, seg.of(done, n))
                link(dve.tensor_scalar(y.bitcast(I32), v.bitcast(I32), -0.5, ROOT_SEED, ALU.mult, ALU.add), n + 1)
                for r in range(ROOT_ROUNDS):
                    k, last = n + 3 * r, r == ROOT_ROUNDS - 1
                    link(dve.tensor_tensor(a, y, y, ALU.mult), k + 2)
                    link(dve.scalar_tensor_tensor(out=a, in0=a, scalar=-0.5, in1=v, op0=ALU.mult, op1=ALU.mult), k + 3)
                    link(dve.scalar_tensor_tensor(out=dst if last else y, in0=a, scalar=1.5, in1=y, op0=ALU.add,
                                                  op1=ALU.mult), k + 4, not last)

            def stats_x(seg):
                dve.wait_ge(x_loaded.sem, seg.of(x_loaded, 16))
                stats(seg, a_stats, lambda t: x_load[:, t, :], stats_a, mv_a)

            def layernorm_x(seg):
                dve.wait_ge(a_rstd.sem, seg.of(a_rstd, 2))
                dve.wait_ge(a_stats.sem, seg.of(a_stats, 4))
                for t in range(TT):
                    dve.tensor_scalar(xn[:, t, :], x_load[:, t, :], mv_a[:, t, 0:1], rs_a[:, t:t + 1],
                                      ALU.subtract, ALU.mult).then_inc(xn_ready.sem, 1)

            def split_xT(seg):
                bank, slot = filled(seg, "xT")
                dve.wait_ge(xh_ready.sem, seg.of(xh_ready, 1))
                dve.tensor_tensor(xl[:, TAPS - 1:], bank[:, 0:T], xh[:, TAPS - 1:], ALU.subtract)\
                   .then_inc(work_freed[slot], 1)

            def gates(seg):
                bank, slot = filled(seg, "gate_logits")
                dve.tensor_tensor(fz[:], bank[:, 0:TT * H].rearrange("p (t h) -> p t h", t=TT),
                                  bf_rows[:].unsqueeze(1).broadcast_to([P, TT, H]), ALU.add)\
                   .then_inc(work_freed[slot], 1)
                dve.wait_ge(work_freed[slot], work_of(seg, "gate_logits")[2] + 1)
                dve.tensor_scalar(fneg[:], fz[:], -1.0, None, ALU.mult).then_inc(gate_abs.sem, 1)
                dve.tensor_scalar(fmin[:], fz[:], 0.0, None, ALU.min).then_inc(gate_abs.sem, 1)
                dve.wait_ge(gate_abs.sem, seg.of(gate_abs, 2))
                dve.tensor_tensor(fneg[:], fneg[:], fz[:], ALU.min).then_inc(gate_abs.sem, 1)

            def gates_log(seg):
                def link(n, ins):
                    ins.then_inc(gate_log.sem, 1)
                    dve.wait_ge(gate_log.sem, seg.of(gate_log, n))

                dve.wait_ge(gate_exp.sem, seg.of(gate_exp, 1))
                link(1, dve.tensor_scalar(fd[:], fe[:], 2.0, None, ALU.add))
                link(2, dve.reciprocal(fr[:], fd[:]))
                link(3, dve.tensor_tensor(fw[:], fe[:], fr[:], ALU.mult))
                link(4, dve.tensor_tensor(fw2[:], fw[:], fw[:], ALU.mult))
                link(5, dve.tensor_scalar(fq[:], fw2[:], SERIES[0], None, ALU.mult))
                n = 5
                for c in SERIES[1:]:
                    n += 1
                    link(n, dve.scalar_tensor_tensor(out=fq[:], in0=fq[:], scalar=c, in1=fw2[:], op0=ALU.add,
                                                     op1=ALU.mult))
                link(n + 1, dve.scalar_tensor_tensor(out=fq[:], in0=fq[:], scalar=1.0, in1=fw[:], op0=ALU.add,
                                                     op1=ALU.mult))
                dve.scalar_tensor_tensor(out=fl[:], in0=fq[:], scalar=-2.0, in1=fmin[:], op0=ALU.mult,
                                         op1=ALU.add).then_inc(gate_log.sem, 1)

            def split_cum(seg):
                bank, slot = filled(seg, "cum")
                cum = bank[0:H, 0:T]
                dve.wait_ge(cum_stored.sem, seg.of(cum_stored, 0))
                dve.tensor_copy(c_parts[:, 0, :], cum).then_inc(cum_split.sem, 1)
                dve.wait_ge(cum_split.sem, seg.of(cum_split, 1))
                dve.tensor_tensor(c_res[:], cum, c_parts[:, 0, :], ALU.subtract).then_inc(work_freed[slot], 1)
                dve.wait_ge(work_freed[slot], work_of(seg, "cum")[2] + 1)
                dve.tensor_copy(c_parts[:, 1, :], c_res[:]).then_inc(cum_split.sem, 1)
                dve.wait_ge(cum_split.sem, seg.of(cum_split, 2))
                dve.tensor_tensor(c_res2[:], c_res[:], c_parts[:, 1, :], ALU.subtract).then_inc(cum_split.sem, 1)
                dve.wait_ge(cum_split.sem, seg.of(cum_split, 3))
                dve.tensor_copy(c_parts[:, 2, :], c_res2[:]).then_inc(cum_split.sem, 2)

            def by_head(ap):
                return ap.rearrange("p (h d) -> p h d", d=DH)

            def projected(seg, t, kinds):
                for m in kinds:
                    for half in range(2):
                        lo, hh = half * HALF, slice(half * 8, half * 8 + 8)
                        bank, slot = filled(seg, f"{m}{t}{half}")
                        if m == "q":
                            dve.wait_ge(q_squared.sem, seg.of(q_squared, 2 * t + half + 1))
                            dve.tensor_tensor(qs[:, t, lo:lo + HALF], bank[:], w_row[:, lo:lo + HALF], ALU.mult)\
                               .then_inc(work_freed[slot], 1)
                            continue
                        n = 6 * t + 2 * "kvg".index(m) + half
                        dve.wait_ge(tanh_a_ready.sem, seg.of(tanh_a_ready, n + 1))
                        th, src = tanh_a[:, n % 2, :], bank[:]
                        dst = {"k": ks[:, t, lo:lo + HALF], "g": gs[:, t, lo:lo + HALF],
                               "v": vs[:, t, hh, 0:DH]}[m]
                        if m == "v":
                            th, src = by_head(th), by_head(src)
                        dve.scalar_tensor_tensor(out=dst, in0=th, scalar=1.0, in1=src, op0=ALU.add,
                                                 op1=ALU.mult).then_inc(work_freed[slot], 1)

            def sum_qk(seg, t, m):
                for half in range(2):
                    lo, hh = half * HALF, slice(half * 8, half * 8 + 8)
                    squared, src, at_row = {"k": (k_squared, ksq, 0), "q": (q_squared, qsq, 1)}[m]
                    dve.wait_ge(squared.sem, seg.of(squared, 2 * t + half + 1))
                    dve.tensor_reduce(ss_qk[:, at_row, t, hh], by_head(src[:, t, lo:lo + HALF]), X, ALU.add)\
                       .then_inc((k_summed, q_summed)[at_row].sem, 1)

            def root_qk(seg):
                for n, (summed, eps_of) in enumerate(((k_summed, 4 * DH * EPS_A), (q_summed, DH * EPS_A))):
                    dve.wait_ge(summed.sem, seg.of(summed, 4))
                    dve.tensor_scalar(v_qk[:, n], ss_qk[:, n], eps_of, None, ALU.add).then_inc(qk_scale.sem, 1)
                flat = [ap[:].rearrange("p a t h -> p (a t h)") for ap in (r_qk, v_qk, a_qk, y_qk)]
                root(seg, qk_scale, 2, *flat)

            def split_turned(seg, name, dst):
                first = {"kT": 0, "qT": 4, "yT": 8}[name]
                for u in range(4):
                    bank, slot = filled(seg, f"{name}{u}")
                    dve.wait_ge(hi_a.sem, seg.of(hi_a, first + u + 1))
                    hi, lo = (part[:, 2 * u:2 * u + 2, :].rearrange("p c t -> p (c t)") for part in dst)
                    dve.tensor_tensor(lo, bank[:], hi, ALU.subtract).then_inc(work_freed[slot], 1)

            def copy_o(seg, pairs):
                for p in pairs:
                    slot, _ = out_ring.place(seg, f"A{p}")
                    dve.wait_ge(*multiplied(seg, f"A{p}"))
                    src = out_banks[slot][:, 0:4 * (DH + 1)].rearrange("p (t h d) -> p t (h d)", t=TT, h=2)
                    dst = o_sb[:, :, 2 * p:2 * p + 2, :].rearrange("p t h d -> p t (h d)")
                    dve.tensor_copy(dst, src).then_inc(pv_freed[slot], 1)

            def sum_o(seg, half):
                hh = slice(half * 8, half * 8 + 8)
                dve.wait_ge(o_squared.sem, seg.of(o_squared, half + 1))
                for_heads = osq.rearrange("p t (h d) -> p t h d", d=DH)[:, :, hh, :]
                dve.tensor_reduce(sso[:, :, hh], for_heads, X, ALU.add).then_inc(o_summed.sem, 1)

            def root_o(seg):
                den = o_sb[:, :, :, DH]
                for p in (PAIRS - 2, PAIRS - 1):
                    slot, n = out_ring.place(seg, f"A{p}")
                    dve.wait_ge(pv_freed[slot], n + 1)
                dve.wait_ge(o_summed.sem, seg.of(o_summed, 2))
                dve.tensor_tensor(a_o[:], den, den, ALU.mult).then_inc(o_scale.sem, 1)
                dve.wait_ge(o_scale.sem, seg.of(o_scale, 1))
                dve.scalar_tensor_tensor(out=v_o[:], in0=a_o[:], scalar=4 * DH * EPS_A, in1=sso[:], op0=ALU.mult,
                                         op1=ALU.add).then_inc(o_scale.sem, 1)
                root(seg, o_scale, 2, *[ap[:].rearrange("p t h -> p (t h)") for ap in (r_o, v_o, a_o, y_o)])

            def gate_o(seg):
                wait_used(dve, seg, ["g10", "g11"])
                for t in range(TT):
                    dve.wait_ge(o_normed.sem, seg.of(o_normed, t + 1))
                    dve.tensor_tensor(y[:, t], y[:, t], gs[:, t], ALU.mult).then_inc(y_ready.sem, 1)

            def layernorm_o(seg):
                bank, slot = filled(seg, "attn_out")
                stats(seg, o_stats, lambda t: bank[:, t * D:(t + 1) * D], stats_o, mv_o)
                dve.wait_ge(o_rstd.sem, seg.of(o_rstd, 2))
                dve.wait_ge(o_stats.sem, seg.of(o_stats, 4))
                dve.wait_ge(x1_copied.sem, seg.scaled(1, seg.offset["A"]))
                for t, done in enumerate((o_ln_ready.sem, work_freed[slot])):
                    dve.tensor_scalar(x1[:, t, :], bank[:, t * D:(t + 1) * D], mv_o[:, t, 0:1], rs_o[:, t:t + 1],
                                      ALU.subtract, ALU.mult).then_inc(done, 1)
                dve.wait_ge(o_ln_ready.sem, seg.of(o_ln_ready, 1))
                dve.wait_ge(*used(seg, "attn_out"))
                dve.wait_ge(x_copied.sem, seg.of(x_copied, 16))
                dve.tensor_tensor(x1[:], x_keep[:], x1[:], ALU.add).then_inc(x1_ready.sem, 1)

            def stats_of_b(seg):
                dve.wait_ge(x1_ready.sem, seg.scaled(1, seg.offset["B"] + 1))
                stats(seg, b_stats, lambda t: x1[:, t, :], stats_b, mv_b)

            def layernorm_b(seg):
                dve.wait_ge(b_rstd.sem, seg.of(b_rstd, 7))
                dve.wait_ge(b_stats.sem, seg.of(b_stats, 4))
                dve.wait_ge(x2_head.sem, seg.of(x2_head, 0))
                for t in range(TT):
                    dve.tensor_scalar(h[:, t, :], x1[:, t, :], mv_b[:, t, 0:1], rz_b[:, t:t + 1],
                                      ALU.subtract, ALU.mult).then_inc(h_ready.sem, 1)
                    dve.tensor_scalar(z[:, t, :], x1[:, t, :], mv_b[:, t, 0:1], rs_b[:, t:t + 1],
                                      ALU.subtract, ALU.mult).then_inc(z_ready.sem, 1)

            def split_hT(seg):
                bank, slot = filled(seg, "hT")
                dve.wait_ge(hT_hi.sem, seg.of(hT_hi, 1))
                dve.tensor_tensor(hT[:, 1], bank[:, 0:T], hT[:, 0], ALU.subtract).then_inc(work_freed[slot], 1)

            def root_b(seg):
                dve.wait_ge(qk_squared.sem, seg.of(qk_squared, 1))
                dve.tensor_reduce(ss_b[:].rearrange("p t h -> p (t h)"),
                                  qk_sq[:].rearrange("p t a h d -> p (t a h) d"), X, ALU.add)\
                   .then_inc(qk_summed.sem, 1)
                dve.wait_ge(qk_summed.sem, seg.of(qk_summed, 1))
                dve.tensor_scalar(v_b2[:], ss_b[:], DB * EPS_B, None, ALU.add).then_inc(b_scale.sem, 1)
                root(seg, b_scale, 1, *[ap[:].rearrange("p t h -> p (t h)") for ap in (rr_b, v_b2, a_b2, y_b2)])

            def pads(seg):
                def head_rows(a):
                    return qk[:, :, a].rearrange("p t h d -> p t h d")

                def pad(ap, part):
                    return ap[:].rearrange("p (t h) s -> p t h s", t=TT)[:, :, :, part * DB:(part + 1) * DB]

                dve.wait_ge(qk_normed.sem, seg.of(qk_normed, 1))
                dve.tensor_copy(pad(k_pad, 0), head_rows(1)).then_inc(k_hi.sem, 1)
                dve.tensor_copy(pad(k_pad, 2), head_rows(1)).then_inc(k_hi.sem, 1)
                dve.wait_ge(k_hi.sem, seg.of(k_hi, 1))
                dve.tensor_tensor(pad(k_pad, 1), head_rows(1), pad(k_pad, 0), ALU.subtract).then_inc(k_lo.sem, 1)
                dve.wait_ge(q_weighted.sem, seg.of(q_weighted, 1))
                dve.tensor_copy(pad(q_pad, 0), head_rows(0)).then_inc(q_hi.sem, 1)
                dve.tensor_copy(pad(q_pad, 1), head_rows(0)).then_inc(q_hi.sem, 1)
                dve.wait_ge(q_hi.sem, seg.of(q_hi, 1))
                dve.tensor_tensor(pad(q_pad, 2), head_rows(0), pad(q_pad, 0), ALU.subtract).then_inc(q_lo.sem, 1)

            def outputs_b(seg):
                for t in range(TT):
                    slot, _ = out_ring.place(seg, f"B{t}")
                    dve.wait_ge(*multiplied(seg, f"B{PAIRS - 1}"))
                    o = out_banks[slot][:, 0:HB * (DB + 1)].rearrange("p (h d) -> p h d", h=HB)
                    dve.reciprocal(rden[:, t], o[:, :, DB]).then_inc(den_ready.sem, 1)
                    dve.wait_ge(den_ready.sem, seg.of(den_ready, t + 1))
                    dve.tensor_tensor(ao[:, t], o[:, :, 0:DB], rden[:, t].unsqueeze(2).broadcast_to([P, HB, DB]),
                                      ALU.mult).then_inc(pv_freed[slot], 1)

            def residual_b(seg):
                for t in range(TT):
                    bank, slot = filled(seg, f"wo{t}")
                    dve.wait_ge(f_norm.sem, seg.of(f_norm, 0))
                    dve.wait_ge(z_ready.sem, seg.of(z_ready, TT))
                    dve.tensor_tensor(x2[:, t, MUTE:], bank[:, 0:D - MUTE], z[:, t, MUTE:], ALU.add)\
                       .then_inc(work_freed[slot], 1)

            def normalize_b(seg):
                dve.wait_ge(x2_squared.sem, seg.of(x2_squared, 1))
                dve.tensor_reduce(ss_f[:], x2_sq[:], X, ALU.add).then_inc(x2_summed.sem, 1)
                dve.wait_ge(x2_rms.sem, seg.of(x2_rms, 2))
                for t in range(TT):
                    dve.tensor_scalar(xf[:, t, :], x2[:, t, :], rs_f[:, t:t + 1], None, ALU.mult)\
                       .then_inc(xf_ready.sem, 1)

            def split_xfT(seg):
                bank, slot = filled(seg, "xfT")
                dve.wait_ge(xfT_hi.sem, seg.of(xfT_hi, 1))
                dve.tensor_tensor(xfT[:, 1], bank[:, 0:T], xfT[:, 0], ALU.subtract).then_inc(work_freed[slot], 1)

            def route(seg):
                bank, slot = filled(seg, "route")
                big = float(np.finfo(np.float32).max)
                dve.tensor_scalar(lg[:], bank[:, 0:TT * NE].rearrange("p (t e) -> p t e", t=TT), -big, big,
                                  ALU.max, ALU.min).then_inc(work_freed[slot], 1)
                dve.wait_ge(work_freed[slot], work_of(seg, "route")[2] + 1)
                dve.tensor_reduce(mx[:], lg[:], X, ALU.max).then_inc(route_max.sem, 2)

            def route_weights(seg):
                dve.wait_ge(route_exp.sem, seg.of(route_exp, 1))
                dve.tensor_reduce(es[:], ex[:], X, ALU.add).then_inc(route_dve.sem, 1)
                dve.wait_ge(route_dve.sem, seg.of(route_dve, 1))
                dve.reciprocal(er[:], es[:]).then_inc(route_dve.sem, 1)
                dve.wait_ge(route_dve.sem, seg.of(route_dve, 2))
                dve.tensor_tensor(pr[:], ex[:], er[:].unsqueeze(2).broadcast_to([P, TT, NE]), ALU.mult)\
                   .then_inc(route_dve.sem, 1)
                dve.wait_ge(route_dve.sem, seg.of(route_dve, 3))
                pj = pr[:].unsqueeze(2).broadcast_to([P, TT, NE, NE])
                pi = pr[:].unsqueeze(3).broadcast_to([P, TT, NE, NE])
                dve.tensor_tensor(gt[:], pj, pi, ALU.is_gt).then_inc(route_cmp.sem, 1)
                dve.tensor_tensor(ge[:], pj, pi, ALU.is_equal).then_inc(route_cmp.sem, 1)
                dve.wait_ge(route_cmp.sem, seg.of(route_cmp, 4))
                dve.tensor_reduce(rank[:], cnt[:], X, ALU.add).then_inc(route_dve.sem, 1)
                dve.wait_ge(route_dve.sem, seg.of(route_dve, 4))
                dve.scalar_tensor_tensor(out=top[:], in0=rank[:], scalar=1.5, in1=pr[:], op0=ALU.is_lt,
                                         op1=ALU.mult).then_inc(route_sel.sem, 1)
                dve.wait_ge(route_sel.sem, seg.of(route_sel, 1))
                dve.tensor_reduce(tsum[:], top[:], X, ALU.add).then_inc(route_dve.sem, 1)
                dve.wait_ge(route_dve.sem, seg.of(route_dve, 5))
                dve.tensor_scalar(trec[:], tsum[:], 1e-8, None, ALU.add).then_inc(route_recip.sem, 1)
                dve.wait_ge(route_recip.sem, seg.of(route_recip, 1))
                dve.reciprocal(tsum[:], trec[:]).then_inc(route_recip.sem, 1)
                dve.wait_ge(route_recip.sem, seg.of(route_recip, 2))
                dve.tensor_tensor(wts[:], top[:], tsum[:].unsqueeze(2).broadcast_to([P, TT, NE]), ALU.mult)\
                   .then_inc(wts_ready.sem, 1)

            def experts(seg):
                gelus = [0]

                def lo_part(dst, src, hi_ready):
                    cols = dst.shape[2] * T
                    dve.wait_ge(*hi_ready)
                    dve.tensor_tensor(dst[:, 1].rearrange("p c t -> p (c t)"), src[:, 0:cols],
                                      dst[:, 0].rearrange("p c t -> p (c t)"), ALU.subtract).then_inc(hid_lo.sem, 1)

                def gelu_lo(name, dst):
                    lo_part(dst, gelu32[gelus[0] % 2], used(seg, name))
                    gelus[0] += 1

                gelu_lo("e0", h0)
                bank, slot = filled(seg, "e1a")
                dve.wait_ge(tanh_b_ready.sem, seg.of(tanh_b_ready, 1))
                dve.scalar_tensor_tensor(out=tanh_b[:], in0=tanh_b[:], scalar=1.0, in1=bank[:], op0=ALU.add,
                                         op1=ALU.mult).then_inc(work_freed[slot], 1)
                bank, slot = filled(seg, "e1b")
                dve.wait_ge(*used(seg, "e1a"))
                dve.tensor_tensor(tanh_b[:], tanh_b[:], bank[:], ALU.mult).then_inc(work_freed[slot], 1)
                dve.wait_ge(*used(seg, "e1b"))
                gelu_lo("e2a", h2a)
                lo_part(h1, tanh_b, (hid_hi.sem, seg.of(hid_hi, 3)))
                gelu_lo("e3a", h3a)
                gelu_lo("e2b", h2b)
                gelu_lo("e3b", h3b)
                gelu_lo("e2c", h2c)

            def mix(seg):
                dve.wait_ge(wts_ready.sem, seg.of(wts_ready, 1))
                for t in range(TT):
                    bank, slot = filled(seg, f"down{t}")
                    for e in range(NE):
                        acc = x2[:, t, MUTE:]
                        dve.scalar_tensor_tensor(out=acc, in0=bank[:, e * P:e * P + D - MUTE],
                                                 scalar=wts[:, t, e:e + 1], in1=acc, op0=ALU.mult,
                                                 op1=ALU.add)\
                           .then_inc(mixed.sem if e < NE - 1 else work_freed[slot], 1)
                        if e < NE - 1:
                            dve.wait_ge(mixed.sem, seg.of(mixed, t * (NE - 1) + e + 1))
                    dve.wait_ge(*used(seg, f"down{t}"))
                stats(seg, f_stats, lambda t: x2[:, t, :], stats_f, mv_f)
                dve.wait_ge(f_rstd.sem, seg.of(f_rstd, 2))
                dve.wait_ge(f_stats.sem, seg.of(f_stats, 4))
                dve.wait_ge(out_stored.sem, seg.of(out_stored, 0))
                for t in range(TT):
                    dve.tensor_scalar(ex_out[:, t, :], x2[:, t, :], mv_f[:, t, 0:1], rs_x[:, t:t + 1],
                                      ALU.subtract, ALU.mult).then_inc(f_norm.sem, 1)
                dve.wait_ge(f_norm.sem, seg.of(f_norm, TT))
                dve.wait_ge(x1_copied.sem, seg.of(x1_copied, 1))
                dve.tensor_tensor(o_fin[:], ex_out[:], x1_keep[:], ALU.add).then_inc(out_ready.sem, 1)

            run(dve, ("B", stats_of_b), ("A", lambda s: projected(s, 0, "k")), ("B", layernorm_b),
                ("A", lambda s: projected(s, 0, "vqg")), ("B", split_hT), ("A", lambda s: sum_qk(s, 0, "k")),
                ("A", lambda s: sum_qk(s, 0, "q")), ("X", stats_x), ("A", lambda s: projected(s, 1, "k")),
                ("B", root_b), ("A", lambda s: projected(s, 1, "v")), ("A", lambda s: sum_qk(s, 1, "k")),
                ("B", pads), ("A", lambda s: projected(s, 1, "qg")), ("A", lambda s: sum_qk(s, 1, "q")),
                ("A", root_qk), ("X", layernorm_x), ("X", split_xT), ("X", gates), ("X", gates_log),
                ("A", lambda s: split_turned(s, "kT", kT)), ("B", outputs_b),
                ("A", lambda s: split_turned(s, "qT", qT)),
                ("A", lambda s: copy_o(s, range(0, 2))), ("B", residual_b),
                ("X", split_cum), ("A", lambda s: copy_o(s, range(2, 4))), ("B", normalize_b),
                ("A", lambda s: copy_o(s, range(4, 6))), ("B", split_xfT), ("A", lambda s: sum_o(s, 0)),
                ("A", lambda s: copy_o(s, range(6, 8))), ("B", route), ("B", route_weights),
                ("A", lambda s: sum_o(s, 1)), ("A", root_o), ("B", experts), ("A", gate_o), ("B", mix),
                ("A", lambda s: split_turned(s, "yT", yT)), ("A", layernorm_o))

        @block.tensor
        def _(pe):
            pe.wait_ge(s_load, loads_total)
            pe.wait_ge(s_const, 1)
            for n, (srcs, _, _) in enumerate(groups):
                if n >= 2:
                    pe.wait_ge(s_trc, n - 1)
                bank, at_col = work_banks[n % 2], 0
                for _, rows, cols, src in srcs:
                    for c in range(cols // P):
                        for r in range(-(-rows // P)):
                            m = min(P, rows)
                            last = pe.transpose(bank[:, at_col:at_col + m], src[0:m, r, c * P:(c + 1) * P],
                                                ident[0:m, 0:m])
                            at_col += m
                last.then_inc(s_tr, 1)
            pe.wait_ge(s_init, 1)
            taken = {}

            def take(seg, name):
                order, n = work.order[seg.name], taken.get(seg.name, 0)
                assert order[n] == name, (seg.name, name, order[n])
                taken[seg.name] = n + 1
                bank, slot, n = work_of(seg, name)
                pe.wait_ge(work_freed[slot], n)
                return bank, work_filled[slot]

            def turn(seg, name, src):
                bank, full = take(seg, name)
                for t in range(TT):
                    last = pe.transpose(bank[:, t * P:(t + 1) * P], src[:, t], ident[:])
                last.then_inc(full, 1)

            def turn_x(seg):
                pe.wait_ge(xn_ready.sem, seg.of(xn_ready, TT))
                turn(seg, "xT", xn)

            def three(out_ap, lhs, rhs, taps, start=True):
                n, total = 0, 3 * len(taps)
                for j in taps:
                    for a, b in ((0, 0), (0, 1), (1, 0)):
                        last = pe.matmul(out_ap, lhs(a, j), rhs(b, j), start=start and n == 0, stop=n == total - 1)
                        n += 1
                return last

            def x_cols(t, shift):
                return lambda a, j: (xh, xl)[a][:, t * P + shift + j:t * P + shift + j + P]

            def gate_logits(seg):
                bank, full = take(seg, "gate_logits")
                pe.wait_ge(xh_ready.sem, seg.of(xh_ready, 1))
                pe.wait_ge(*used(seg, "xT"))
                for t in range(TT):
                    last = three(bank[:, t * H:(t + 1) * H], x_cols(t, TAPS - 1), lambda b, j: wf[:, b, :], [0])
                last.then_inc(full, 1)

            def project(seg, t):
                for m in "kvqg":
                    for half in range(2):
                        bank, full = take(seg, f"{m}{t}{half}")
                        lo = half * HALF
                        taps = list(range(TAPS)) if m in "kv" else [0]
                        three(bank[:], x_cols(t, 0 if m in "kv" else TAPS - 1),
                              lambda b, j: proj[m][:, b, j, lo:lo + HALF], taps).then_inc(full, 1)

            PARTS = ((0, 0), (1, 0), (0, 1))

            def cumulate(seg):
                bank, full = take(seg, "cum")
                pe.wait_ge(gate_log.sem, seg.of(gate_log, gate_log.per))
                pe.matmul(bank[0:H, 0:T], fl[:, 0, :], tri[:], start=True, stop=False)
                pe.matmul(bank[0:H, P:T], fl[:, 1, :], tri[:, 0:P], start=False, stop=True).then_inc(full, 1)

            def turn_heads(seg, name, src):
                for u in range(4):
                    bank, full = take(seg, f"{name}{u}")
                    for i in range(2):
                        for t in range(TT):
                            c = 2 * u + i
                            last = pe.transpose(bank[:, i * T + t * P:i * T + (t + 1) * P],
                                                src[:, t, c * P:(c + 1) * P], ident[:])
                    last.then_inc(full, 1)

            def turn_k(seg):
                pe.wait_ge(k_normed.sem, seg.of(k_normed, 1))
                turn_heads(seg, "kT", ks)

            def turn_q(seg):
                pe.wait_ge(q_normed.sem, seg.of(q_normed, 1))
                turn_heads(seg, "qT", qs)

            BLOCKS = ((slice(0, T), 0, slice(0, T)), (slice(T, T + P), 1, slice(P, T)))

            def scores_a(seg, p):
                slot, n = pair_ring.place(seg, f"A{p}")
                pe.wait_ge(probs_ready[slot], n)
                for i in range(2):
                    head, rows = 2 * p + i, slice(i * DH, (i + 1) * DH)
                    for cols, s, toks in BLOCKS:
                        dst = score_banks[slot][:, i, cols]
                        keys = slice(s * P, (s + 1) * P)
                        pe.matmul(dst, dec_k[:, head, keys], dec_q[:, head, toks], start=True, stop=False)
                        pe.matmul(score_banks[slot][:, i, cols.start:cols.start + P], identb[:], mask[:],
                                  start=False, stop=False)
                        for a, b in PARTS:
                            last = pe.matmul(dst, kT[a][rows, p, keys], qT[b][rows, p, toks], start=False,
                                             stop=(a, b) == PARTS[-1])
                return last.then_inc(scores_ready[slot], 1)

            def values(dst, pr, i, rhs, t):
                pe_last = pe.matmul(dst, pr[:, i, t * P:(t + 1) * P], rhs(0), start=True, stop=t == 0)
                if t == 1:
                    pe_last = pe.matmul(dst, pr[:, i, T:T + P], rhs(1), start=False, stop=True)
                return pe_last

            def values_a(seg, p):
                slot, n = pair_ring.place(seg, f"A{p}")
                o, m = out_ring.place(seg, f"A{p}")
                pe.wait_ge(probs_ready[slot], n + 1)
                pe.wait_ge(pv_freed[o], m)
                bank = out_banks[o][:, 0:4 * (DH + 1)].rearrange("p (t h d) -> p t h d", t=TT, h=2)
                for t in range(TT):
                    for i in range(2):
                        last = values(bank[:, t, i, :], probs[slot], i, lambda s: vs[:, s, 2 * p + i, :], t)
                last.then_inc(probs_used[slot], 1)

            def attention_a(seg, steps):
                if steps[0] == 0:
                    pe.wait_ge(decay_loaded.sem, seg.scaled(32, 32 * (seg.offset["A"] + 1)))
                    wait_used(pe, seg, [f"{m}T{u}" for m in "kq" for u in range(4)])
                for p in steps:
                    if p < PAIRS:
                        scores_a(seg, p)
                    if p >= 1:
                        values_a(seg, p - 1)

            def output_a(seg):
                pe.wait_ge(y_ready.sem, seg.of(y_ready, TT))
                turn_heads(seg, "yT", y)
                bank, full = take(seg, "attn_out")
                wait_used(pe, seg, [f"yT{u}" for u in range(4)])
                for t in range(TT):
                    for c in range(CT):
                        for a, b in PARTS:
                            last = pe.matmul(bank[:, t * D:(t + 1) * D], yT[a][:, c, t * P:(t + 1) * P],
                                             wo_a[:, b, c, :], start=c == 0 and (a, b) == PARTS[0],
                                             stop=c == CT - 1 and (a, b) == PARTS[-1])
                last.then_inc(full, 1)

            def qkv_b(seg):
                pe.wait_ge(h_ready.sem, seg.of(h_ready, TT))
                turn(seg, "hT", h)
                for t in range(TT):
                    bank, full = take(seg, f"qkv{t}")
                    pe.wait_ge(*used(seg, "hT"))
                    for a, b in PARTS:
                        last = pe.matmul(bank[:, 0:3 * D], hT[:, a, t * P:(t + 1) * P], wqkv[:, b],
                                         start=(a, b) == PARTS[0], stop=(a, b) == PARTS[-1])
                    last.then_inc(full, 1)

            def turn_pads(seg):
                for name, src, ready in (("qpT", q_pad, q_lo), ("kpT", k_pad, k_lo)):
                    pe.wait_ge(ready.sem, seg.of(ready, 1))
                    bank, full = take(seg, name)
                    dst = bank[:].bitcast(F16)
                    for j in range(4):
                        for t in range(TT):
                            lo = t * HB + 4 * j
                            last = pe.transpose(dst[:, j * T + t * P:j * T + (t + 1) * P],
                                                src[:, lo:lo + 4, :].rearrange("p h s -> p (h s)"), ident16[:])
                    last.then_inc(full, 1)

            def scores_b(seg, p):
                slot, n = pair_ring.place(seg, f"B{p}")
                pe.wait_ge(probs_ready[slot], n)
                for i in range(2):
                    j, r = divmod(2 * p + i, 4)
                    rows = slice(r * SLOT, r * SLOT + 3 * DB)
                    for cols, s, toks in BLOCKS:
                        pe.matmul(score_banks[slot][:, i, cols], kTb[rows, j, s * P:(s + 1) * P], qTb[rows, j, toks],
                                  start=True, stop=False)
                        last = pe.matmul(score_banks[slot][:, i, cols.start:cols.start + P], identb[:], mask[:],
                                         start=False, stop=True)
                last.then_inc(scores_ready[slot], 1)

            def values_b(seg, p):
                slot, n = pair_ring.place(seg, f"B{p}")
                pe.wait_ge(probs_ready[slot], n + 1)
                for t in range(TT):
                    o, m = out_ring.place(seg, f"B{t}")
                    if p == 0:
                        pe.wait_ge(pv_freed[o], m)
                    for i in range(2):
                        head = 2 * p + i
                        dst = out_banks[o][:, head * (DB + 1):(head + 1) * (DB + 1)]
                        last = values(dst, probs[slot], i, lambda s: vb[:, s, head, :], t)
                last.then_inc(probs_used[slot], 1)

            def attention_b(seg, steps):
                if steps[0] == 0:
                    wait_used(pe, seg, ["qpT", "kpT"])
                for p in steps:
                    if p < PAIRS:
                        scores_b(seg, p)
                    if p >= 1:
                        values_b(seg, p - 1)

            def turn_out(seg):
                for t in range(TT):
                    o, m = out_ring.place(seg, f"B{t}")
                    pe.wait_ge(pv_freed[o], m + 1)
                turn(seg, "aT", ao[:].rearrange("p t h d -> p t (h d)"))

            def output_b(seg):
                for t in range(TT):
                    bank, full = take(seg, f"wo{t}")
                    pe.wait_ge(*used(seg, "aT"))
                    pe.matmul(bank[:, 0:D - MUTE], aT[:, t * P:(t + 1) * P], wo_b[:, MUTE:], start=True, stop=True)\
                      .then_inc(full, 1)

            def layer(seg, name, weights, inputs, cols=HID):
                bank, full = take(seg, name)
                steps = [(k, a, b) for k in range(len(weights)) for a, b in PARTS]
                for m in range(cols // P):
                    for k, a, b in steps:
                        last = pe.matmul(bank[:, m * T:(m + 1) * T], weights[k][a][:, m * P:(m + 1) * P],
                                         inputs[k][b], start=(k, a, b) == steps[0], stop=(k, a, b) == steps[-1])
                last.then_inc(full, 1)

            def flat_pair(wt):
                return [[wt[:, 0], wt[:, 1]]]

            def tiled_pair(wt):
                return [[wt[:, a, k] for a in range(2)] for k in range(wt.shape[2])]

            def turn_xf(seg):
                pe.wait_ge(xf_ready.sem, seg.of(xf_ready, TT))
                turn(seg, "xfT", xf)

            def experts(seg):
                bank, full = take(seg, "route")
                pe.wait_ge(*used(seg, "xfT"))
                for t in range(TT):
                    for a, b in PARTS:
                        last = pe.matmul(bank[:, t * NE:(t + 1) * NE], xfT[:, a, t * P:(t + 1) * P], gate_w[:, b],
                                         start=(a, b) == PARTS[0], stop=(a, b) == PARTS[-1])
                last.then_inc(full, 1)
                x_pair = flat_pair(xfT)
                layer(seg, "e0", flat_pair(up0), x_pair)
                layer(seg, "e1a", flat_pair(up1), x_pair)
                layer(seg, "e1b", flat_pair(up2), x_pair)
                layer(seg, "e2a", flat_pair(l1), x_pair)
                layer(seg, "e3a", flat_pair(e3d), x_pair, P)
                pe.wait_ge(hid_lo.sem, seg.of(hid_lo, 2))
                layer(seg, "e2b", tiled_pair(l2), tiled_pair(h2a))
                pe.wait_ge(hid_lo.sem, seg.of(hid_lo, 4))
                layer(seg, "e3b", flat_pair(e3u), tiled_pair(h3a))
                pe.wait_ge(hid_lo.sem, seg.of(hid_lo, 5))
                layer(seg, "e2c", tiled_pair(l3), tiled_pair(h2b))
                pe.wait_ge(hid_lo.sem, seg.of(hid_lo, 7))
                steps = [(k, a, b) for k in range(2) for a, b in PARTS]
                for t in range(TT):
                    bank, full = take(seg, f"down{t}")
                    for e, hid in enumerate((h0, h1, h2c, h3b)):
                        for k, a, b in steps:
                            last = pe.matmul(bank[:, e * P:e * P + D - MUTE], hid[:, a, k, t * P:(t + 1) * P],
                                             downs[e][:, b, k, MUTE:], start=(k, a, b) == steps[0],
                                             stop=(k, a, b) == steps[-1])
                    last.then_inc(full, 1)

            run(pe, ("A", lambda s: project(s, 0)), ("B", qkv_b), ("A", lambda s: project(s, 1)), ("B", turn_pads),
                ("X", turn_x), ("B", lambda s: attention_b(s, range(0, 4))), ("X", gate_logits),
                ("B", lambda s: attention_b(s, range(4, PAIRS + 1))), ("A", turn_k), ("A", turn_q),
                ("A", lambda s: attention_a(s, range(0, 2))), ("B", turn_out),
                ("A", lambda s: attention_a(s, range(2, 4))), ("B", output_b), ("X", cumulate),
                ("A", lambda s: attention_a(s, range(4, 6))), ("B", turn_xf),
                ("A", lambda s: attention_a(s, range(6, PAIRS + 1))), ("B", experts), ("A", output_a))


_NAMES = ["x", "Wq", "Wk", "Wv", "Wo", "Wf", "bf", "Wg", "qnw", "knw", "onw", "kconv_w", "vconv_w"]
_FFN = ["n1_w", "n2_w", "wq", "wk", "wv", "wo", "qn_w", "kn_w", "gate_w", "e0_up", "e0_down", "e1_w1", "e1_w2",
        "e1_down", "e2_l1", "e2_l2", "e2_l3", "e2_l4", "e3_down", "e3_up", "e3_out"]


def kernel(**inputs):
    import numpy as _np
    import concourse.bacc as _bacc
    from concourse import mybir as _mybir
    from concourse.bass_utils import run_bass_kernel_spmd as _run

    nc = _bacc.Bacc("TRN2", target_bir_lowering=False, num_devices=1)
    arrays, args = {}, {}
    for prefix, names in (("L0_attn_", _NAMES), ("L0_ffn_", _FFN)):
        for name in names:
            a = _np.ascontiguousarray(inputs[prefix + name])
            arrays[f"in_{prefix}{name}"] = a
            args[name] = nc.dram_tensor(f"in_{prefix}{name}", a.shape, _mybir.dt.from_np(a.dtype),
                                        kind="ExternalInput").ap()
    x = args.pop("x")
    out = nc.dram_tensor("out_0", tuple(x.shape), F32, kind="ExternalOutput").ap()
    build(nc, x, args, out)
    r = _run(nc, [arrays], core_ids=[0])
    return r.results[0]["out_0"]
```

```python
from contextlib import ExitStack

import numpy as np

import concourse.bass as bass
from concourse import mybir

F32 = mybir.dt.float32
F16 = mybir.dt.float16
I32 = mybir.dt.int32
BF16 = mybir.dt.bfloat16
ALU = mybir.AluOpType
ACT = mybir.ActivationFunctionType
X = mybir.AxisListType.X

P = 128
D = 128
T = 256
TT = T // P
H, DH = 16, 64
C = H * DH
CT = C // P
TAPS = 4
HB, DB = 16, 8
SLOT = 32
NE = 4
HID = 256
MUTE = 32
PAIRS = H // 2
HALF = 512
MASKED = -1.0e30
LN_EPS = 1e-5
EPS_A = 1e-6
EPS_B = 1.1920929e-07
ROOT_SEED = float(0x5F3759DF)
ROOT_ROUNDS = 3
SERIES = [1.0 / (2 * k + 1) for k in range(8, 0, -1)]

WORK = ([("A", "k00"), ("A", "k01"), ("B", "qkv0"), ("B", "qkv1"), ("A", "k10"), ("A", "k11"),
         ("A", "v11"), ("B", "kpT"), ("B", "qpT"), ("X", "xT"),
         ("X", "gate_logits")]
        + [("A", f"kT{u}") for u in range(4)] + [("A", "qT0"), ("A", "qT1"), ("B", "oB0"), ("B", "oB1")]
        + [("A", "qT2"), ("B", "aT"), ("A", "qT3"), ("B", "wo0"), ("B", "wo1"), ("X", "cum"), ("B", "xfT")]
        + [("B", "route"), ("B", "e2a"), ("B", "e3a"), ("B", "e0"), ("B", "e2b"),
           ("B", "e1a"), ("B", "e1b"), ("B", "e3b"), ("B", "down0"),
           ("B", "down1")])
SPARE = ([("A", "q00"), ("B", "hT"), ("A", "q01"), ("A", "g00"), ("A", "g01")]
         + [("A", n) for n in ("q10", "q11", "g10", "g11")]
         + [("X", "v00"), ("X", "v01"), ("X", "v10"), ("B", "e2c")]
         + [("A", f"yT{u}") for u in range(4)] + [("A", "attn_out")])
ATTENTION = [("B", f"B{p}") for p in range(PAIRS)] + [("A", f"A{p}") for p in range(PAIRS)]


class Segment:

    def __init__(self, name, reg, offset):
        self.name, self.reg, self.offset = name, reg, offset

    def scaled(self, per, const):
        return const if self.reg is None else self.reg * per + const

    def of(self, signal, n):
        return self.scaled(signal.per, self.offset[signal.block] * signal.per + n)


class Signal:

    def __init__(self, sem, block, per):
        self.sem, self.block, self.per = sem, block, per


class Ring:

    def __init__(self, size, uses, rounds):
        blocks = {"first": "X", "second": "XA", "third": "XAB", "loop": "XAB", "end": "AB", "last": "B"}
        self.order = {seg: [name for block, name in uses if block in blocks[seg]] for seg in blocks}
        self.size, both = size, len(uses)
        assert both % size == 0
        before = sum(len(self.order[seg]) for seg in ("first", "second"))
        self.base = {"first": 0, "second": len(self.order["first"]), "third": before, "loop": before,
                     "end": before + (rounds + 1) * both}
        self.base["last"] = self.base["end"] + len(self.order["end"])
        self.step = both // size

    def place(self, seg, name):
        n = self.base[seg.name] + self.order[seg.name].index(name)
        return n % self.size, seg.scaled(self.step, n // self.size)


def build(nc, x_in, w, out):
    NB = x_in.shape[0]
    rounds = NB - 3
    with ExitStack() as ctx:
        def sb(name, shape, dt=F32):
            return ctx.enter_context(nc.sbuf_tensor(name, shape, dt))

        def psum(name, shape, dt=F32):
            return ctx.enter_context(nc.psum_tensor(name, shape, dt))

        def sem(name):
            return ctx.enter_context(nc.semaphore(name))

        def signal(name, block, per):
            return Signal(sem(name), block, per)

        work_banks = [psum(f"work{i}", [P, HALF]) for i in range(2)]
        score_banks = [psum(f"scores{i}", [P, 2, HALF]) for i in range(2)]
        out_banks = [psum(f"pv{i}", [P, HALF]) for i in range(2)]

        ident = sb("ident", [P, P])
        ident16 = sb("ident16", [P, P], F16)
        identb = sb("identb", [P, P], BF16)
        mask = sb("mask", [P, P], BF16)
        tri = sb("tri", [P, T])
        before = sb("before", [P, TT, NE, NE])
        mhalf = sb("mhalf", [P, TT])
        eps = {n: sb(f"eps_{n}", [P, TT]) for n in ("ln", "xf")}
        eps_value = {"ln": LN_EPS, "xf": D * EPS_B}
        mark, exp_mark = (sb(n, [P, 1]) for n in ("mark", "exp_mark"))
        bf_rows = sb("bf_rows", [P, H])
        w_col = sb("w_col", [P, CT])
        kn_col = sb("kn_col", [P, CT])
        w8 = sb("w8", [P, HB, DB])

        proj = {m: sb(f"w_{m}", [P, 2, TAPS if m in "kv" else 1, C], F16) for m in "kvqg"}
        wf = sb("wf", [P, 2, H], F16)
        wo_a = sb("wo_a", [P, 2, CT, D], F16)
        wqkv = sb("wqkv", [P, 2, 3 * D], F16)
        wo_b = sb("wo_b", [P, D])
        gate_w = sb("gate_wT", [P, 2, NE], F16)
        up0, up1, up2, l1 = (sb(n, [P, 2, HID], F16) for n in ("e0_upT", "e1_w1T", "e1_w2T", "e2_l1T"))
        l2, l3 = (sb(n, [P, 2, 2, HID], F16) for n in ("e2_l2T", "e2_l3T"))
        e3d = sb("e3_downT", [P, 2, D], F16)
        e3u = sb("e3_upT", [P, 2, HID], F16)
        downs = [sb(f"down{e}T", [P, 2, 2, D], F16) for e in range(NE)]

        arena = sb("arena", [P, 6 * 2048])
        o_sb = sb("o_sb", [P, TT, H, DH + 1])

        def region(i):
            return arena[:, i * 2048:(i + 1) * 2048]

        def tokens(ap, c=C):
            return ap.rearrange("p (t c) -> p t c", t=TT)

        def channels(ap):
            return ap.rearrange("p (c t) -> p c t", c=CT)

        ks, qs, gs = tokens(region(0)), tokens(region(1)), tokens(region(2))
        ksq, qsq = tokens(o_sb[:].rearrange("p t h d -> p (t h d)")[:, 0:TT * C]), tokens(region(3))

        def pair(ap):
            parts = ap.bitcast(F16).rearrange("p (a n) -> p a n", a=2)
            return [channels(parts[:, a, :]) for a in range(2)]

        qT, kT = pair(region(4)), pair(region(5))
        y, osq, yT = ks, qs, kT
        x_load = sb("x_load", [P, TT, D])
        x_keep = sb("x_keep", [P, TT, D])
        xn = sb("xn", [P, TT, D])
        xh = sb("xh", [P, TAPS - 1 + T], F16)
        xl = sb("xl", [P, TAPS - 1 + T], F16)
        tanh_a = sb("tanh_a", [P, 2, HALF])
        vs = sb("vs", [P, TT, H, DH + 1])
        probs = [sb(f"probs{i}", [P, 2, 3 * P]) for i in range(2)]
        fz, fneg, fe, fd, fr, fw, fw2, fq, fmin, fl = (sb(f"f{i}", [P, TT, H]) for i in range(10))
        c_res = sb("c_res", [H, T])
        c_parts = sb("c_parts", [H, 3, T], BF16)
        dec_k = sb("dec_k", [6, H, T], BF16)
        dec_q = sb("dec_q", [6, H, T], BF16)
        c_dram = nc.dram_tensor("c_scratch", (2, H, 3, T), BF16, kind="Internal").ap()
        stats_a = sb("stats_a", [P, TT, 6])
        mv_a = sb("mv_a", [P, TT, 2])
        rs_a = sb("rs_a", [P, TT])
        t_a = sb("t_a", [P, TT])
        stats_o = sb("stats_o", [P, TT, 6])
        mv_o = sb("mv_o", [P, TT, 2])
        rs_o = sb("rs_o", [P, TT])
        t_o = sb("t_o", [P, TT])
        ss_qk, v_qk, a_qk, y_qk, r_qk = (sb(f"root_qk{i}", [P, 2, TT, H]) for i in range(5))
        sso, v_o, a_o, y_o, r_o = (sb(f"root_o{i}", [P, TT, H]) for i in range(5))
        x1 = sb("x1", [P, TT, D])

        x1_keep = sb("x1_keep", [P, TT, D])
        stats_b = sb("stats_b", [P, TT, 6])
        mv_b = sb("mv_b", [P, TT, 2])
        v_b, r_b = (sb(f"b{i}", [P, 2, TT]) for i in range(2))
        mhalf4 = sb("mhalf4", [P, 2, TT])
        flow_b = sb("flow_b", [P, 4, TT * D])
        z, h = (flow_b[:, i].rearrange("p (t d) -> p t d", t=TT) for i in range(2))
        qk = flow_b[:, 2:4].rearrange("p t (a h d) -> p t a h d", a=2, h=HB)
        gelu32 = [flow_b[:, 2 * i:2 * i + 2].rearrange("p a n -> p (a n)") for i in range(2)]
        wo_raw = flow_b[:].rearrange("p a (b d) -> p (a b) d", d=D)
        hT = sb("hT", [P, 2, T], F16)
        tanh_b = sb("tanh_b", [P, 2 * T])
        qk_sq = tanh_b[:].rearrange("p (t a h d) -> p t a h d", t=TT, a=2, h=HB)
        outT_a = tanh_b[0:DH + 1, :]
        ss_b, v_b2, a_b2, y_b2, rr_b = (sb(f"root_b{i}", [P, TT, 2 * HB]) for i in range(5))
        vb = sb("vb", [P, TT, HB, SLOT])
        q_pad = sb("q_pad", [P, TT * HB, SLOT], F16)
        k_pad = sb("k_pad", [P, TT * HB, SLOT], F16)
        qTb = sb("qTb", [P, 4, T], F16)
        kTb = sb("kTb", [P, 4, T], F16)
        rden = sb("rden", [P, TT, HB])
        ao = sb("ao", [P, TT, HB, DB])
        aT = sb("aT", [P, T])
        x2 = sb("x2", [P, TT, D])
        ss_f, t_f, rs_f = (sb(f"xf{i}", [P, TT]) for i in range(3))
        xf = sb("xf", [P, TT, D])
        x2_sq = ex_out = xf
        xfT = sb("xfT", [P, 2, T], F16)
        lg, ls, ex, pr, top = (sb(f"g{i}", [P, TT, NE]) for i in range(5))
        mx, es, er, tsum, trec = (sb(f"gs{i}", [P, TT]) for i in range(5))
        gt, ge, cnt = (sb(f"gg{i}", [P, TT, NE, NE]) for i in range(3))
        rank = sb("rank", [P, TT, NE])
        wts = sb("wts", [P, TT, NE])
        hid01 = sb("hid01", [P, 4 * T])
        h0, h1 = (hid01[:, 2 * i * T:2 * (i + 1) * T].bitcast(F16).rearrange("p (a c t) -> p a c t", a=2, c=2)
                  for i in range(2))
        outT_b = hid01[:].rearrange("p (g t) -> p g t", g=4)
        h2a, h2b, h3b = (sb(f"hid{i}", [P, 2, 2, T], F16) for i in range(3))
        h2c = h2a
        h3a = sb("h3a", [P, 2, 1, T], F16)
        stats_f = sb("stats_f", [P, TT, 6])
        mv_f = sb("mv_f", [P, TT, 2])
        rs_x, t_x = (sb(f"fx{i}", [P, TT]) for i in range(2))

        s_load = sem("weights_loaded")
        s_const = sem("constants_made")
        s_tr = sem("weights_transposed")
        s_trc = sem("transposed_copied")
        s_init = sem("buffers_cleared")
        pool_init = sem("pool_setup_step")
        dve_init = sem("dve_setup_step")

        x_loaded = signal("x_loaded", "X", 16)
        x_copied = signal("x_kept", "A", 16)
        a_stats = signal("a_stats", "X", 4)
        a_rstd = signal("a_rstd", "X", 2)
        xn_ready = signal("xn_ready", "X", TT)
        xh_ready = signal("xh_ready", "X", 1)
        gate_abs = signal("gate_abs", "X", 3)
        gate_exp = signal("gate_exp", "X", 1)
        gate_log = signal("gate_log", "X", 5 + len(SERIES) + 1)
        cum_split = signal("cum_split", "X", 5)
        cum_stored = signal("cum_stored", "X", 16)
        decay_loaded = signal("decay_loaded", "X", 32)
        tanh_kg = signal("tanh_kg", "A", 9)
        tanh_v = signal("tanh_v", "X", 3)
        q_squared = signal("q_squared", "A", 4)
        k_squared = signal("k_squared", "A", 4)
        q_summed = signal("q_summed", "A", 4)
        k_summed = signal("k_summed", "A", 4)
        qk_scale = signal("qk_scale", "A", 12)
        k_normed = signal("k_normed", "A", 2)
        q_normed = signal("q_normed", "A", 2)
        outT_a_ready = signal("outT_a_ready", "A", PAIRS)
        o_turned = signal("o_turned", "A", PAIRS)
        o_copied = signal("o_copied", "A", PAIRS)
        o_squared = signal("o_squared", "A", 3)
        o_summed = signal("o_summed", "A", 3)
        o_scale = signal("o_scale", "A", 12)
        o_normed = signal("o_normed", "A", TT)
        y_ready = signal("y_ready", "A", TT)
        o_stats = signal("o_stats", "A", 4)
        o_rstd = signal("o_rstd", "A", 2)
        o_ln_ready = signal("o_ln_ready", "A", 1)
        hi_a = signal("hi_a", "A", 12)
        x1_ready = signal("x1_ready", "A", 1)

        x1_copied = signal("x1_copied", "B", 1)
        b_stats = signal("b_stats", "A", 6)
        b_rstd = signal("b_rstd", "A", 1)
        z_ready = signal("z_ready", "B", TT)
        h_ready = signal("h_ready", "B", TT)
        hT_hi = signal("hT_hi", "B", 1)
        xfT_hi = signal("xfT_hi", "B", 1)
        hid_hi = signal("hid_hi", "B", 7)
        hid_lo = signal("hid_lo", "B", 7)
        qk_copied = signal("qk_copied", "B", TT)
        qk_squared = signal("qk_squared", "B", 1)
        qk_summed = signal("qk_summed", "B", 1)
        b_scale = signal("b_scale", "B", 11)
        qk_normed = signal("qk_normed", "B", 1)
        q_weighted = signal("q_weighted", "B", 1)
        k_hi, k_lo = signal("k_hi", "B", 2), signal("k_lo", "B", 1)
        q_hi, q_lo = signal("q_hi", "B", 2), signal("q_lo", "B", 1)
        pads_T = signal("pads_T", "B", 2)
        outT_b_ready = signal("outT_b_ready", "B", 2)
        den_ready = signal("den_ready", "B", TT)
        x2_head = signal("x2_head", "B", 1)
        x2_squared = signal("x2_squared", "B", 1)
        x2_summed = signal("x2_summed", "B", 1)
        x2_rms = signal("x2_rms", "B", 2)
        xf_ready = signal("xf_ready", "B", TT)
        route_max = signal("route_max", "B", 2)
        route_shift = signal("route_shift", "B", 1)
        route_exp = signal("route_exp", "B", 1)
        route_dve = signal("route_dve", "B", 5)
        route_cmp = signal("route_cmp", "B", 4)
        route_sel = signal("route_sel", "B", 1)
        route_recip = signal("route_recip", "B", 2)
        wts_ready = signal("wts_ready", "B", 1)
        tanh_b_ready = signal("tanh_b_ready", "B", 1)
        mixed = signal("mixed", "B", TT * (NE - 1))
        f_stats = signal("f_stats", "B", 4)
        f_rstd = signal("f_rstd", "B", 2)
        f_norm = signal("f_norm", "B", TT)
        out_ready = signal("out_ready", "B", 1)
        out_stored = signal("out_stored", "B", 16)

        work = Ring(2, WORK, rounds)
        work_filled = [sem(f"work_filled{i}") for i in range(4)]
        work_freed = [sem(f"work_freed{i}") for i in range(4)]
        pair_ring = Ring(2, ATTENTION, rounds)
        scores_ready = [sem(f"scores_ready{i}") for i in range(2)]
        probs_ready = [sem(f"probs_ready{i}") for i in range(2)]
        probs_used = [sem(f"probs_used{i}") for i in range(2)]

        spare = Ring(2, SPARE, rounds)
        spares_named = [name for _, name in SPARE]

        def place(seg, name):
            if name in spares_named:
                slot, before_it = spare.place(seg, name)
                return slot + 2, before_it
            return work.place(seg, name)

        def work_of(seg, name):
            slot, before_it = place(seg, name)
            return (work_banks + out_banks)[slot], slot, before_it

        def used(seg, name):
            slot, before_it = place(seg, name)
            return work_freed[slot], before_it + 1

        def wait_used(eng, seg, names):
            latest = {}
            for name in names:
                latest[place(seg, name)[0]] = name
            for name in latest.values():
                eng.wait_ge(*used(seg, name))

        def multiplied(seg, pair):
            slot, before_it = pair_ring.place(seg, pair)
            return probs_used[slot], before_it + 1

        def run(engine, *stages):
            def play(seg):
                for block, stage in stages:
                    if block in seg.offset:
                        stage(seg)

            play(Segment("first", None, {"X": 0}))
            play(Segment("second", None, {"X": 1, "A": 0}))
            play(Segment("third", None, {"X": 2, "A": 1, "B": 0}))
            with engine.Fori(1, rounds + 1) as i:
                play(Segment("loop", i, {"X": 2, "A": 1, "B": 0}))
            play(Segment("end", None, {"A": NB - 1, "B": NB - 2}))
            play(Segment("last", None, {"B": NB - 1}))

        spares = [a[:].rearrange("p t h d -> p (t h d)") for a in (o_sb, vs)]
        stage_conv = {"k": arena[:, 0:4096], "v": arena[:, 4096:8192]}
        stage_proj = {m: arena[:, 8192 + i * C:8192 + (i + 1) * C] for i, m in enumerate("kvqg")}
        fold = tanh_a[:].rearrange("p a c -> p (a c)")
        n1 = sb("n1w_col", [P, 1])
        n2 = sb("n2w_col", [P, 1])
        onw2 = sb("onw2", [P, 1])
        q8, k8 = sb("q8", [P, DB]), sb("k8", [P, DB])
        wf_raw = sb("wf_raw", [P, H])
        small = sb("small", [P, DB])

        at = [0]

        def source(name, rows, cols):
            n = -(-rows // P) * cols
            lo = at[0]
            at[0] += n
            ap = spares[lo // 2048][:, lo % 2048:lo % 2048 + n]
            return name, rows, cols, ap.rearrange("p (r c) -> p r c", c=cols)

        groups = [([source("wq", D, D), source("wk", D, D), source("wv", D, D)], n1, wqkv[:]),
                  ([source("wo", D, D)], None, wo_b[:]),
                  ([source("e0_up", HID, D)], n2, up0[:]),
                  ([source("e1_w1", HID, D)], n2, up1[:]),
                  ([source("e1_w2", HID, D)], n2, up2[:]),
                  ([source("e2_l1", HID, D)], n2, l1[:]),
                  ([source("e3_down", D, D)], n2, e3d[:]),
                  ([source("e3_up", HID, D)], None, e3u[:]),
                  ([source("gate_w", NE, D)], n2, gate_w[:])]
        at[0] = max(at[0], 2048)
        groups += [([source("e2_l2", HID, HID)], None, l2[:]),
                   ([source("e2_l3", HID, HID)], None, l3[:]),
                   ([source("e0_down", D, HID)], None, downs[0][:]),
                   ([source("e1_down", D, HID)], 0.5, downs[1][:]),
                   ([source("e2_l4", D, HID)], None, downs[2][:]),
                   ([source("e3_out", D, HID)], None, downs[3][:])]
        sources = [s for g in groups for s in g[0]]

        block = ctx.enter_context(nc.Block())

        def row(ap):
            return ap.rearrange("(o n) -> o n", o=1)

        setup_loads = (
            [(stage_proj[m], w[f"W{m}"]) for m in "kvqg"]
            + [(stage_conv[m], w[f"{m}conv_w"].rearrange("(o c) j -> o (c j)", o=1).partition_broadcast(P)) for m in "kv"]
            + [(wf_raw[:], w["Wf"]), (bf_rows[:], w["bf"].partition_broadcast(P)),
               (w_col[:], w["qnw"].rearrange("(c p) -> p c", p=P)), (kn_col[:], w["knw"].rearrange("(c p) -> p c", p=P)),
               (q8[:], w["qn_w"].partition_broadcast(P)), (k8[:], w["kn_w"].partition_broadcast(P)),
               (n1[:], w["n1_w"].rearrange("(p o) -> p o", o=1)), (n2[:], w["n2_w"].rearrange("(p o) -> p o", o=1)),
               (onw2[0:DH, :], w["onw"].rearrange("(p o) -> p o", o=1)),
               (onw2[DH:P, :], w["onw"].rearrange("(p o) -> p o", o=1)),
               (wo_raw[:], w["Wo"].rearrange("(c p) d -> p c d", p=P))]
            + [(ap if rows % P == 0 else ap[0:rows], w[name].rearrange("(r p) c -> p r c", p=min(P, rows)))
               for name, rows, cols, ap in sources])
        loads_total = 16 * len(setup_loads)

        @block.sync
        def _(sp):
            for dst, src in setup_loads:
                sp.dma_start(dst, src, allow_slow_non_contiguous=True).then_inc(s_load, 16)

            def batch(seg, block):
                b = seg.scaled(1, seg.offset[block])
                return b if seg.reg is None else sp.snap(b)

            def tokens_of(ap, b):
                ap = ap[b] if isinstance(b, int) else ap[bass.ds(b, 1)].rearrange("o t d -> (o t) d")
                return ap.rearrange("(t p) d -> p t d", p=P)

            def load_x(seg):
                b = batch(seg, "X")
                sp.wait_ge(xn_ready.sem, seg.of(xn_ready, 0))
                sp.dma_start(x_load[:], tokens_of(x_in, b)).then_inc(x_loaded.sem, 16)

            def load_residual(seg):
                b = batch(seg, "A")
                sp.wait_ge(x1_ready.sem, seg.of(x1_ready, 0))
                sp.dma_start(x_keep[:], tokens_of(x_in, b)).then_inc(x_copied.sem, 16)

            def move_cum(seg):
                sp.wait_ge(decay_loaded.sem, seg.of(decay_loaded, 0))
                sp.wait_ge(cum_split.sem, seg.of(cum_split, 5))
                sp.dma_start(c_dram[0], c_parts[:]).then_inc(cum_stored.sem, 16)
                sp.wait_ge(cum_stored.sem, seg.of(cum_stored, 16))
                if "A" in seg.offset:
                    sp.wait_ge(*multiplied(seg, f"A{PAIRS - 1}"))
                else:
                    sp.wait_ge(s_init, 1)
                src = c_dram[0].rearrange("h p t -> p h t")
                sp.dma_start(dec_q[0:3], src).then_inc(decay_loaded.sem, 16)
                sp.dma_start(dec_k[3:6], src).then_inc(decay_loaded.sem, 16)

            def store(seg):
                b = batch(seg, "B")
                sp.wait_ge(out_ready.sem, seg.of(out_ready, 1))
                sp.dma_start(tokens_of(out, b), x1_keep[:]).then_inc(out_stored.sem, 16)

            run(sp, ("X", load_x), ("A", load_residual), ("X", move_cum), ("B", store))
            sp.wait_ge(out_stored.sem, 16 * NB)

        O_PARTS = [(0, 4), (4, 6), (6, 8)]

        KG_UNITS = ["k00", "k01", "g00", "g01", "k10", "k11", "v11", "g10", "g11"]
        V_UNITS = ["v00", "v01", "v10"]

        LO_PARTS = ("e2a", "e3a", "e0", "e2b", "e2c", "e3b", "e1")

        @block.gpsimd
        def _(pool):
            steps = [0]

            def step(ins):
                steps[0] += 1
                ins.then_inc(pool_init, 1)
                pool.wait_ge(pool_init, steps[0])

            step(pool.memset(ident[:], 1.0))
            step(pool.affine_select(out=ident[:], in_=ident[:], compare_op=ALU.is_equal, fill=0.0, base=0,
                                    pattern=[[-1, P]], channel_multiplier=1))
            step(pool.tensor_copy(ident16[:], ident[:]))
            step(pool.tensor_copy(identb[:], ident[:]))
            step(pool.memset(tri[:], 1.0))
            step(pool.affine_select(out=tri[:], in_=tri[:], compare_op=ALU.is_ge, fill=0.0, base=0,
                                    pattern=[[1, T]], channel_multiplier=-1))
            step(pool.memset(mask[:], 0.0))
            step(pool.affine_select(out=mask[:], in_=mask[:], compare_op=ALU.is_ge, fill=MASKED, base=0,
                                    pattern=[[1, P]], channel_multiplier=-1))
            step(pool.memset(before[:], 1.0))
            step(pool.affine_select(out=before[:], in_=before[:], compare_op=ALU.is_gt, fill=0.0, base=0,
                                    pattern=[[0, TT], [1, NE], [-1, NE]], channel_multiplier=0))
            for name, tile in eps.items():
                step(pool.memset(tile[:], eps_value[name]))
            step(pool.memset(mhalf4[:], -0.5))
            pool.memset(mhalf[:], -0.5).then_inc(s_const, 1)
            step(pool.memset(dec_k[:], 1.0))
            step(pool.memset(dec_q[:], -1.0))
            step(pool.memset(xh[:, 0:TAPS - 1], 0.0))
            step(pool.memset(xl[:, 0:TAPS - 1], 0.0))
            step(pool.memset(q_pad[:], 0.0))
            step(pool.memset(k_pad[:], 0.0))
            step(pool.memset(vb[:], 0.0))
            step(pool.memset(vb[:, :, :, DB], 1.0))
            pool.wait_ge(s_trc, len(groups))
            pool.memset(vs[:, :, :, DH], 1.0).then_inc(s_init, 1)
            pool.wait_ge(s_init, 1)

            def flat(ap):
                return ap.rearrange("p t h -> p (t h)")

            def rsqrt(seg, done, n, dst, src, name, tmp):
                cols = src.shape[-1]
                pool.tensor_tensor(tmp, src, eps[name][:, 0:cols], ALU.add).then_inc(done.sem, 1)
                pool.wait_ge(done.sem, seg.of(done, n))
                pool.tensor_tensor(dst, tmp, mhalf[:, 0:cols], ALU.pow).then_inc(done.sem, 1)

            def rstd_a(seg):
                pool.wait_ge(a_stats.sem, seg.of(a_stats, 4))
                rsqrt(seg, a_rstd, 1, rs_a[:], mv_a[:, :, 1], "ln", t_a[:])

            def square_k(seg, t):
                for half in range(2):
                    lo = half * HALF
                    pool.wait_ge(*used(seg, f"k{t}{half}"))
                    pool.tensor_tensor(ksq[:, t, lo:lo + HALF], ks[:, t, lo:lo + HALF], ks[:, t, lo:lo + HALF],
                                       ALU.mult).then_inc(k_squared.sem, 1)

            def heads(ap):
                return ap.rearrange("p t (h d) -> p (t h) d", d=DH)

            def norm_qk(seg):
                wait_used(pool, seg, ["q10", "q11"])
                pool.wait_ge(qk_scale.sem, seg.of(qk_scale, 12))
                for n, (x_t, done) in enumerate(((ks, k_normed), (qs, q_normed))):
                    for half in range(2):
                        hh = slice(half * 8, half * 8 + 8)
                        heads = x_t.rearrange("p t (h d) -> p t h d", d=DH)[:, :, hh, :]
                        r = r_qk[:, n, :, hh].unsqueeze(3).broadcast_to([P, TT, H // 2, DH])
                        pool.tensor_tensor(heads, heads, r, ALU.mult).then_inc(done.sem, 1)

            def square_o(seg, part):
                first, end = O_PARTS[part]
                hh = slice(2 * first, 2 * end)
                if part == 0:
                    pool.wait_ge(*used(seg, "qT3"))
                pool.wait_ge(o_copied.sem, seg.of(o_copied, end))
                num = o_sb[:, :, hh, 0:DH]
                pool.tensor_tensor(osq.rearrange("p t (h d) -> p t h d", d=DH)[:, :, hh, :], num, num, ALU.mult)\
                    .then_inc(o_squared.sem, 1)

            def norm_o(seg):
                pool.wait_ge(o_scale.sem, seg.of(o_scale, 12))
                for t in range(TT):
                    pool.tensor_tensor(y[:, t].rearrange("p (h d) -> p h d", d=DH), o_sb[:, t, :, 0:DH],
                                       r_o[:, t].unsqueeze(2).broadcast_to([P, H, DH]), ALU.mult)\
                        .then_inc(o_normed.sem, 1)

            def rstd_o(seg):
                pool.wait_ge(o_stats.sem, seg.of(o_stats, 4))
                rsqrt(seg, o_rstd, 1, rs_o[:], mv_o[:, :, 1], "ln", t_o[:])

            def rstd_b(seg):
                pool.wait_ge(b_stats.sem, seg.of(b_stats, 6))
                pool.wait_ge(z_ready.sem, seg.scaled(TT, TT * seg.offset["A"]))
                pool.tensor_tensor(r_b[:], v_b[:], mhalf4[:], ALU.pow).then_inc(b_rstd.sem, 1)

            def norm_b(seg):
                f = "p t a h d -> p (t a h) d"
                pool.wait_ge(qk_copied.sem, seg.of(qk_copied, TT))
                pool.tensor_tensor(qk_sq[:], qk[:], qk[:], ALU.mult).then_inc(qk_squared.sem, 1)
                pool.wait_ge(b_scale.sem, seg.of(b_scale, 11))
                r = rr_b[:].rearrange("p t h -> p (t h)").unsqueeze(2).broadcast_to([P, TT * 2 * HB, DB])
                pool.tensor_tensor(qk[:].rearrange(f), qk[:].rearrange(f), r, ALU.mult).then_inc(qk_normed.sem, 1)
                pool.wait_ge(qk_normed.sem, seg.of(qk_normed, 1))
                wb = w8[:].rearrange("p h d -> p (h d)").unsqueeze(1).broadcast_to([P, TT, HB * DB])
                qq = qk[:].rearrange("p t a h d -> p t a (h d)")[:, :, 0, :]
                pool.tensor_tensor(qq, qq, wb, ALU.mult).then_inc(q_weighted.sem, 1)

            def square_x2(seg):
                wait_used(pool, seg, [f"wo{t}" for t in range(TT)])
                pool.wait_ge(x2_head.sem, seg.of(x2_head, 1))
                pool.tensor_tensor(x2_sq[:], x2[:], x2[:], ALU.mult).then_inc(x2_squared.sem, 1)
                pool.wait_ge(x2_summed.sem, seg.of(x2_summed, 1))
                rsqrt(seg, x2_rms, 1, rs_f[:], ss_f[:], "xf", t_f[:])

            def route(seg):
                pool.wait_ge(route_max.sem, seg.of(route_max, 2))
                pool.tensor_tensor(ls[:], lg[:], mx[:].unsqueeze(2).broadcast_to([P, TT, NE]),
                                   ALU.subtract).then_inc(route_shift.sem, 1)

            def rstd_f(seg):
                pool.wait_ge(f_stats.sem, seg.of(f_stats, 4))
                rsqrt(seg, f_rstd, 1, rs_x[:], mv_f[:, :, 1], "ln", t_x[:])

            run(pool, ("A", lambda s: square_k(s, 0)), ("X", rstd_a), ("B", norm_b), ("A", lambda s: square_k(s, 1)),
                ("A", norm_qk), ("B", square_x2), ("A", lambda s: square_o(s, 0)), ("B", route),
                ("A", lambda s: square_o(s, 1)), ("A", lambda s: square_o(s, 2)), ("A", norm_o),
                ("A", rstd_o), ("A", rstd_b), ("B", rstd_f))

        @block.scalar
        def _(act):
            act.wait_ge(s_init, 1)

            def filled(seg, name):
                bank, slot, n = work_of(seg, name)
                act.wait_ge(work_filled[slot], n + 1)
                return bank, slot

            def project_q(name):
                def stage(seg):
                    t, lo = int(name[1]), int(name[2]) * HALF
                    bank, slot = filled(seg, name)
                    if name == "q00":
                        act.wait_ge(o_summed.sem, seg.of(o_summed, 0))
                    act.activation(qsq[:, t, lo:lo + HALF], bank[:], ACT.Square).then_inc(q_squared.sem, 1)
                    act.activation(qs[:, t, lo:lo + HALF], bank[:], ACT.Copy).then_inc(work_freed[slot], 1)
                return "A", stage

            def tanh_kg_of(name):
                def stage(seg):
                    n = KG_UNITS.index(name)
                    bank, slot = filled(seg, name)
                    if n >= 2:
                        act.wait_ge(*used(seg, KG_UNITS[n - 2]))
                    act.activation(tanh_a[:, n % 2, :], bank[:], ACT.Tanh, scale=0.5).then_inc(tanh_kg.sem, 1)
                return "A", stage

            def tanh_of_v(seg, n):
                bank, _ = filled(seg, V_UNITS[n])
                if n >= 2:
                    act.wait_ge(*used(seg, V_UNITS[n - 2]))
                act.activation(tanh_a[:, 1 - n % 2, :], bank[:], ACT.Tanh, scale=0.5).then_inc(tanh_v.sem, 1)

            def copy_xT(seg):
                bank, _ = filled(seg, "xT")
                act.activation(xh[:, TAPS - 1:], bank[:, 0:T], ACT.Copy).then_inc(xh_ready.sem, 1)

            def gate(seg):
                act.wait_ge(gate_abs.sem, seg.of(gate_abs, 3))
                act.activation(fe[:], fneg[:], ACT.Exp).then_inc(gate_exp.sem, 1)

            def turned(seg, name, dst, units):
                for u in units:
                    bank, slot = filled(seg, f"{name}{u}")
                    if name != "qT":
                        act.activation(dst[0][:, 2 * u:2 * u + 2, :].rearrange("p c t -> p (c t)"), bank[:], ACT.Copy)\
                           .then_inc(hi_a.sem, 1)
                        continue
                    for i in range(2):
                        c = 2 * u + i
                        last = act.activation(dst[0][:, c, :], bank[:, i * T:(i + 1) * T], ACT.Copy,
                                              scale=w_col[:, c:c + 1])
                    last.then_inc(hi_a.sem, 1)

            def exps(seg, block, pairs):
                for p in pairs:
                    slot, n = pair_ring.place(seg, f"{block}{p}")
                    act.wait_ge(scores_ready[slot], n + 1)
                    act.wait_ge(probs_used[slot], n)
                    act.activation(probs[slot][:], score_banks[slot][:, :, 0:3 * P], ACT.Exp)\
                       .then_inc(probs_ready[slot], 1)

            def copy_outT_a(seg, p):
                act.wait_ge(*multiplied(seg, f"A{p}"))
                act.activation(outT_a, out_banks[0][0:DH + 1, :], ACT.Copy).then_inc(outT_a_ready.sem, 1)

            def attention_a(seg, steps):
                for p in steps:
                    if p < PAIRS:
                        exps(seg, "A", [p])
                    if p >= 1:
                        copy_outT_a(seg, p - 1)

            def copy_outT_b(seg, half):
                act.wait_ge(*multiplied(seg, f"B{4 * half + 3}"))
                act.activation(outT_b[:, 2 * half:2 * half + 2, :].rearrange("p g t -> p (g t)"), out_banks[half][:],
                               ACT.Copy).then_inc(outT_b_ready.sem, 1)

            def keep(seg):
                act.wait_ge(out_stored.sem, seg.of(out_stored, 0))
                act.wait_ge(x1_ready.sem, seg.scaled(1, seg.offset["B"] + 1))
                act.activation(x1_keep[:], x1[:], ACT.Copy).then_inc(x1_copied.sem, 1)
                act.wait_ge(z_ready.sem, seg.of(z_ready, TT))
                act.wait_ge(f_norm.sem, seg.of(f_norm, 0))
                act.activation(x2[:, :, 0:MUTE], z[:, :, 0:MUTE], ACT.Copy).then_inc(x2_head.sem, 1)

            def copy_hT(seg):
                bank, _ = filled(seg, "hT")
                act.activation(hT[:, 0], bank[:, 0:T], ACT.Copy).then_inc(hT_hi.sem, 1)

            def copy_qkv(t):
                def stage(seg):
                    bank, slot = filled(seg, f"qkv{t}")
                    if t == 0:
                        act.wait_ge(k_lo.sem, seg.of(k_lo, 0))
                        act.wait_ge(q_lo.sem, seg.of(q_lo, 0))
                    act.activation(qk[:, t].rearrange("p a h d -> p (a h d)"), bank[:, 0:2 * D], ACT.Copy)\
                       .then_inc(qk_copied.sem, 1)
                    act.activation(vb[:, t, :, 0:DB], bank[:, 2 * D:3 * D].rearrange("p (h d) -> p h d", d=DB),
                                   ACT.Copy).then_inc(work_freed[slot], 1)
                return "B", stage

            def fetch_exp(seg):
                act.activation(exp_mark[:], n1[:], ACT.Exp)

            def copy_pads(seg):
                for name, dst in (("kpT", kTb), ("qpT", qTb)):
                    bank, slot = filled(seg, name)
                    act.activation(dst[:].rearrange("p j t -> p (j t)"), bank[:].bitcast(F16), ACT.Copy)\
                       .then_inc(work_freed[slot], 1)

            def copy_aT(seg):
                bank, slot = filled(seg, "aT")
                act.activation(aT[:], bank[:, 0:T], ACT.Copy).then_inc(work_freed[slot], 1)

            def copy_xfT(seg):
                bank, _ = filled(seg, "xfT")
                act.activation(xfT[:, 0], bank[:, 0:T], ACT.Copy).then_inc(xfT_hi.sem, 1)

            def route(seg):
                act.wait_ge(route_shift.sem, seg.of(route_shift, 1))
                act.activation(ex[:], ls[:], ACT.Exp).then_inc(route_exp.sem, 1)

            gelus = ("e2a", "e3a", "e0", "e2b", "e2c", "e3b")

            def gelu(seg, name, dst):
                n, cols = gelus.index(name), dst.shape[2] * T
                bank, slot = filled(seg, name)
                if n >= 2:
                    act.wait_ge(hid_lo.sem, seg.of(hid_lo, LO_PARTS.index(gelus[n - 2]) + 1))
                act.activation(gelu32[n % 2][:, 0:cols], bank[:, 0:cols], ACT.Gelu).then_inc(hid_hi.sem, 1)
                act.activation(dst[:, 0].rearrange("p c t -> p (c t)"), bank[:, 0:cols], ACT.Gelu)\
                   .then_inc(work_freed[slot], 1)

            def tanh_e1(seg):
                bank, slot = filled(seg, "e1a")
                act.activation(tanh_b[:], bank[:], ACT.Tanh, scale=0.5).then_inc(tanh_b_ready.sem, 1)

            def hi_e1(seg):
                act.wait_ge(*used(seg, "e1b"))
                act.activation(h1[:, 0].rearrange("p c t -> p (c t)"), tanh_b[:], ACT.Copy).then_inc(hid_hi.sem, 1)

            def v_unit(n):
                return "X", lambda s: tanh_of_v(s, n)

            def gelu_of(name, dst):
                return "B", lambda s: gelu(s, name, dst)

            def turn(name, dst, *units):
                return "A", lambda s: turned(s, name, dst, units)

            def attend_b(*pairs):
                return "B", lambda s: exps(s, "B", pairs)

            def attend_a(*steps):
                return "A", lambda s: attention_a(s, steps)

            run(act, project_q("q00"), tanh_kg_of("k00"), ("B", copy_hT), project_q("q01"), tanh_kg_of("k01"),
                tanh_kg_of("g00"), copy_qkv(0), tanh_kg_of("g01"), copy_qkv(1), ("B", keep),
                tanh_kg_of("k10"), project_q("q10"), tanh_kg_of("k11"), project_q("q11"), ("B", fetch_exp), tanh_kg_of("v11"), tanh_kg_of("g10"),
                tanh_kg_of("g11"), ("B", copy_pads), ("X", copy_xT),
                attend_b(0, 1, 2, 3), turn("kT", kT, 0), attend_b(4), turn("kT", kT, 1), attend_b(5),
                ("B", lambda s: copy_outT_b(s, 0)), turn("kT", kT, 2), attend_b(6), turn("kT", kT, 3),
                ("X", gate), turn("qT", qT, 0), attend_b(7), turn("qT", qT, 1), ("B", lambda s: copy_outT_b(s, 1)),
                attend_a(0, 1), turn("qT", qT, 2), ("B", copy_aT), attend_a(2), turn("qT", qT, 3),
                attend_a(3, 4, 5), ("B", copy_xfT), attend_a(6, 7), ("B", route), gelu_of("e2a", h2a), attend_a(8),
                gelu_of("e3a", h3a), gelu_of("e0", h0), gelu_of("e2b", h2b), v_unit(0), v_unit(1), ("B", tanh_e1),
                v_unit(2), ("B", hi_e1), gelu_of("e2c", h2c), turn("yT", yT, 0, 1, 2, 3), gelu_of("e3b", h3b))

        @block.vector
        def _(dve):
            dve.wait_ge(s_load, loads_total)
            steps = [0]

            def step(ins):
                steps[0] += 1
                ins.then_inc(dve_init, 1)
                dve.wait_ge(dve_init, steps[0])

            def split(src, hi, lo):
                step(dve.tensor_copy(hi, src))
                step(dve.tensor_tensor(lo, src, hi, ALU.subtract))

            step(dve.scalar_tensor_tensor(out=w_col[:], in0=w_col[:], scalar=float(DH) * DH ** -0.5, in1=kn_col[:],
                                          op0=ALU.mult, op1=ALU.mult))
            for m in "kv":
                for j in range(TAPS):
                    taps = stage_conv[m].rearrange("p (c j) -> p c j", j=TAPS)[:, :, j]
                    step(dve.tensor_tensor(fold, stage_proj[m], taps, ALU.mult))
                    split(fold, proj[m][:, 0, j, :], proj[m][:, 1, j, :])
            for m in "qg":
                split(stage_proj[m], proj[m][:, 0, 0, :], proj[m][:, 1, 0, :])
            split(wf_raw[:], wf[:, 0, :], wf[:, 1, :])
            wo_flat = wo_raw[:].rearrange("p c d -> p (c d)")
            step(dve.tensor_scalar(wo_flat, wo_flat, onw2[:, 0:1], 0.5 * DH ** 0.5, ALU.mult, ALU.mult))
            split(wo_flat, wo_a[:, 0].rearrange("p c d -> p (c d)"), wo_a[:, 1].rearrange("p c d -> p (c d)"))
            step(dve.tensor_scalar(n2[:], n2[:], float(D) ** 0.5, None, ALU.mult))
            step(dve.tensor_tensor(small[:], q8[:], k8[:], ALU.mult))
            step(dve.tensor_scalar(w8[:], small[:].unsqueeze(1).broadcast_to([P, HB, DB]), float(DB) * DB ** -0.5, None,
                                   ALU.mult))
            for n, (srcs, scale, dst) in enumerate(groups):
                cols = sum(-(-r // P) * c if r >= P else r for _, r, c, _ in srcs)
                bank = work_banks[n % 2][:, 0:cols]
                dve.wait_ge(s_tr, n + 1)
                s = 1.0 if scale is None else scale if isinstance(scale, float) else scale[:, 0:1]
                if len(dst.shape) == 2:
                    dve.tensor_scalar(dst, bank, s, None, ALU.mult).then_inc(s_trc, 1)
                    continue
                hi, lo = (dst[:, a] if len(dst.shape) == 3 else dst[:, a].rearrange("p a b -> p (a b)")
                          for a in range(2))
                step(dve.tensor_scalar(hi, bank, s, None, ALU.mult))
                dve.scalar_tensor_tensor(out=lo, in0=bank, scalar=s, in1=hi, op0=ALU.mult, op1=ALU.subtract)\
                   .then_inc(s_trc, 1)
            dve.wait_ge(s_init, 1)

            def filled(seg, name):
                bank, slot, n = work_of(seg, name)
                dve.wait_ge(work_filled[slot], n + 1)
                return bank, slot

            def stats(seg, done, src, st, mv):
                for t in range(TT):
                    dve.bn_stats(st[:, t, :], src(t)).then_inc(done.sem, 1)
                dve.wait_ge(done.sem, seg.of(done, TT))
                dve.memset(mark[:], 0.0)
                for t in range(TT):
                    dve.bn_aggr(mv[:, t, :], st[:, t, :]).then_inc(done.sem, 1)

            def root(seg, done, n, dst, v, a, y):
                def link(ins, k, wait=True):
                    ins.then_inc(done.sem, 1)
                    if wait:
                        dve.wait_ge(done.sem, seg.of(done, k))

                dve.wait_ge(done.sem, seg.of(done, n))
                link(dve.tensor_scalar(y.bitcast(I32), v.bitcast(I32), -0.5, ROOT_SEED, ALU.mult, ALU.add), n + 1)
                for r in range(ROOT_ROUNDS):
                    k, last = n + 3 * r, r == ROOT_ROUNDS - 1
                    link(dve.tensor_tensor(a, y, y, ALU.mult), k + 2)
                    link(dve.scalar_tensor_tensor(out=a, in0=a, scalar=-0.5, in1=v, op0=ALU.mult, op1=ALU.mult), k + 3)
                    link(dve.scalar_tensor_tensor(out=dst if last else y, in0=a, scalar=1.5, in1=y, op0=ALU.add,
                                                  op1=ALU.mult), k + 4, not last)

            def stats_x(seg):
                dve.wait_ge(x_loaded.sem, seg.of(x_loaded, 16))
                stats(seg, a_stats, lambda t: x_load[:, t, :], stats_a, mv_a)

            def layernorm_x(seg):
                dve.wait_ge(a_rstd.sem, seg.of(a_rstd, 2))
                dve.wait_ge(a_stats.sem, seg.of(a_stats, 4))
                for t in range(TT):
                    dve.tensor_scalar(xn[:, t, :], x_load[:, t, :], mv_a[:, t, 0:1], rs_a[:, t:t + 1],
                                      ALU.subtract, ALU.mult).then_inc(xn_ready.sem, 1)

            def split_xT(seg):
                bank, slot = filled(seg, "xT")
                dve.wait_ge(xh_ready.sem, seg.of(xh_ready, 1))
                dve.tensor_tensor(xl[:, TAPS - 1:], bank[:, 0:T], xh[:, TAPS - 1:], ALU.subtract)\
                   .then_inc(work_freed[slot], 1)

            def gates(seg):
                bank, slot = filled(seg, "gate_logits")
                dve.tensor_tensor(fz[:], bank[:, 0:TT * H].rearrange("p (t h) -> p t h", t=TT),
                                  bf_rows[:].unsqueeze(1).broadcast_to([P, TT, H]), ALU.add)\
                   .then_inc(work_freed[slot], 1)
                dve.wait_ge(work_freed[slot], work_of(seg, "gate_logits")[2] + 1)
                dve.tensor_scalar(fneg[:], fz[:], -1.0, None, ALU.mult).then_inc(gate_abs.sem, 1)
                dve.tensor_scalar(fmin[:], fz[:], 0.0, None, ALU.min).then_inc(gate_abs.sem, 1)
                dve.wait_ge(gate_abs.sem, seg.of(gate_abs, 2))
                dve.tensor_tensor(fneg[:], fneg[:], fz[:], ALU.min).then_inc(gate_abs.sem, 1)

            def gates_log(seg):
                def link(n, ins):
                    ins.then_inc(gate_log.sem, 1)
                    dve.wait_ge(gate_log.sem, seg.of(gate_log, n))

                dve.wait_ge(gate_exp.sem, seg.of(gate_exp, 1))
                link(1, dve.tensor_scalar(fd[:], fe[:], 2.0, None, ALU.add))
                link(2, dve.reciprocal(fr[:], fd[:]))
                link(3, dve.tensor_tensor(fw[:], fe[:], fr[:], ALU.mult))
                link(4, dve.tensor_tensor(fw2[:], fw[:], fw[:], ALU.mult))
                link(5, dve.tensor_scalar(fq[:], fw2[:], SERIES[0], None, ALU.mult))
                n = 5
                for c in SERIES[1:]:
                    n += 1
                    link(n, dve.scalar_tensor_tensor(out=fq[:], in0=fq[:], scalar=c, in1=fw2[:], op0=ALU.add,
                                                     op1=ALU.mult))
                link(n + 1, dve.scalar_tensor_tensor(out=fq[:], in0=fq[:], scalar=1.0, in1=fw[:], op0=ALU.add,
                                                     op1=ALU.mult))
                dve.scalar_tensor_tensor(out=fl[:], in0=fq[:], scalar=-2.0, in1=fmin[:], op0=ALU.mult,
                                         op1=ALU.add).then_inc(gate_log.sem, 1)

            def split_cum(seg):
                bank, slot = filled(seg, "cum")
                cum = bank[0:H, 0:T]
                dve.wait_ge(cum_stored.sem, seg.of(cum_stored, 0))
                dve.tensor_copy(c_parts[:, 0, :], cum).then_inc(cum_split.sem, 1)
                dve.wait_ge(cum_split.sem, seg.of(cum_split, 1))
                dve.tensor_tensor(c_res[:], cum, c_parts[:, 0, :], ALU.subtract).then_inc(work_freed[slot], 1)
                dve.wait_ge(work_freed[slot], work_of(seg, "cum")[2] + 1)
                dve.tensor_copy(c_parts[:, 1, :], c_res[:]).then_inc(cum_split.sem, 1)
                dve.wait_ge(cum_split.sem, seg.of(cum_split, 2))
                dve.tensor_tensor(c_res[:], c_res[:], c_parts[:, 1, :], ALU.subtract).then_inc(cum_split.sem, 1)
                dve.wait_ge(cum_split.sem, seg.of(cum_split, 3))
                dve.tensor_copy(c_parts[:, 2, :], c_res[:]).then_inc(cum_split.sem, 2)

            def by_head(ap):
                return ap.rearrange("p (h d) -> p h d", d=DH)

            def silu(seg, name, th, th_ready, dst):
                bank, slot = filled(seg, name)
                dve.wait_ge(*th_ready)
                src = bank[:]
                if len(dst.shape) == 3:
                    th, src = by_head(th), by_head(src)
                dve.scalar_tensor_tensor(out=dst, in0=th, scalar=1.0, in1=src, op0=ALU.add, op1=ALU.mult)\
                   .then_inc(work_freed[slot], 1)

            def silu_kg(name):
                m, t, lo, n = name[0], int(name[1]), int(name[2]) * HALF, KG_UNITS.index(name)
                return "A", lambda s: silu(s, name, tanh_a[:, n % 2, :], (tanh_kg.sem, s.of(tanh_kg, n + 1)),
                                           {"k": ks, "g": gs}[m][:, t, lo:lo + HALF])

            def silu_v11(seg):
                n = KG_UNITS.index("v11")
                silu(seg, "v11", tanh_a[:, n % 2, :], (tanh_kg.sem, seg.of(tanh_kg, n + 1)), vs[:, 1, 8:16, 0:DH])

            def silu_v(n):
                t, half = divmod(n, 2)
                return "X", lambda s: silu(s, V_UNITS[n], tanh_a[:, 1 - n % 2, :], (tanh_v.sem, s.of(tanh_v, n + 1)),
                                           vs[:, t, half * 8:half * 8 + 8, 0:DH])

            def sum_qk(seg, t, m):
                for half in range(2):
                    lo, hh = half * HALF, slice(half * 8, half * 8 + 8)
                    squared, src, at_row = {"k": (k_squared, ksq, 0), "q": (q_squared, qsq, 1)}[m]
                    dve.wait_ge(squared.sem, seg.of(squared, 2 * t + half + 1))
                    dve.tensor_reduce(ss_qk[:, at_row, t, hh], by_head(src[:, t, lo:lo + HALF]), X, ALU.add)\
                       .then_inc((k_summed, q_summed)[at_row].sem, 1)

            def root_qk(seg):
                for n, (summed, eps_of) in enumerate(((k_summed, 4 * DH * EPS_A), (q_summed, DH * EPS_A))):
                    dve.wait_ge(summed.sem, seg.of(summed, 4))
                    dve.tensor_scalar(v_qk[:, n], ss_qk[:, n], eps_of, None, ALU.add).then_inc(qk_scale.sem, 1)
                flat = [ap[:].rearrange("p a t h -> p (a t h)") for ap in (r_qk, v_qk, a_qk, y_qk)]
                root(seg, qk_scale, 2, *flat)

            def split_turned(seg, name, dst, units):
                first = {"kT": 0, "qT": 4, "yT": 8}[name]
                for u in units:
                    bank, slot = filled(seg, f"{name}{u}")
                    dve.wait_ge(hi_a.sem, seg.of(hi_a, first + u + 1))
                    if name != "qT":
                        hi, lo = (part[:, 2 * u:2 * u + 2, :].rearrange("p c t -> p (c t)") for part in dst)
                        dve.tensor_tensor(lo, bank[:], hi, ALU.subtract).then_inc(work_freed[slot], 1)
                        continue
                    for i in range(2):
                        c = 2 * u + i
                        last = dve.scalar_tensor_tensor(out=dst[1][:, c, :], in0=bank[:, i * T:(i + 1) * T],
                                                        scalar=w_col[:, c:c + 1], in1=dst[0][:, c, :],
                                                        op0=ALU.mult, op1=ALU.subtract)
                    last.then_inc(work_freed[slot], 1)

            def copy_o(seg, pairs):
                for p in pairs:
                    dve.wait_ge(o_turned.sem, seg.of(o_turned, p + 1))
                    src = out_banks[1][:, 0:4 * (DH + 1)].rearrange("p (t h d) -> p t (h d)", t=TT, h=2)
                    dst = o_sb[:, :, 2 * p:2 * p + 2, :].rearrange("p t h d -> p t (h d)")
                    dve.tensor_copy(dst, src).then_inc(o_copied.sem, 1)

            def sum_o(seg, part):
                hh = slice(2 * O_PARTS[part][0], 2 * O_PARTS[part][1])
                dve.wait_ge(o_squared.sem, seg.of(o_squared, part + 1))
                for_heads = osq.rearrange("p t (h d) -> p t h d", d=DH)[:, :, hh, :]
                dve.tensor_reduce(sso[:, :, hh], for_heads, X, ALU.add).then_inc(o_summed.sem, 1)

            def root_o(seg):
                den = o_sb[:, :, :, DH]
                dve.wait_ge(o_copied.sem, seg.of(o_copied, PAIRS))
                dve.wait_ge(o_summed.sem, seg.of(o_summed, 3))
                dve.tensor_tensor(a_o[:], den, den, ALU.mult).then_inc(o_scale.sem, 1)
                dve.wait_ge(o_scale.sem, seg.of(o_scale, 1))
                dve.scalar_tensor_tensor(out=v_o[:], in0=a_o[:], scalar=4 * DH * EPS_A, in1=sso[:], op0=ALU.mult,
                                         op1=ALU.add).then_inc(o_scale.sem, 1)
                root(seg, o_scale, 2, *[ap[:].rearrange("p t h -> p (t h)") for ap in (r_o, v_o, a_o, y_o)])

            def gate_o(seg):
                wait_used(dve, seg, ["g10", "g11"])
                for t in range(TT):
                    dve.wait_ge(o_normed.sem, seg.of(o_normed, t + 1))
                    dve.tensor_tensor(y[:, t], y[:, t], gs[:, t], ALU.mult).then_inc(y_ready.sem, 1)

            def stats_of_o(seg):
                bank, slot = filled(seg, "attn_out")
                stats(seg, o_stats, lambda t: bank[:, t * D:(t + 1) * D], stats_o, mv_o)

            def layernorm_o(seg):
                bank, slot = filled(seg, "attn_out")
                dve.wait_ge(o_rstd.sem, seg.of(o_rstd, 2))
                dve.wait_ge(o_stats.sem, seg.of(o_stats, 4))
                dve.wait_ge(x1_copied.sem, seg.scaled(1, seg.offset["A"]))
                for t, done in enumerate((o_ln_ready.sem, work_freed[slot])):
                    dve.tensor_scalar(x1[:, t, :], bank[:, t * D:(t + 1) * D], mv_o[:, t, 0:1], rs_o[:, t:t + 1],
                                      ALU.subtract, ALU.mult).then_inc(done, 1)
                dve.wait_ge(o_ln_ready.sem, seg.of(o_ln_ready, 1))
                dve.wait_ge(*used(seg, "attn_out"))
                dve.wait_ge(x_copied.sem, seg.of(x_copied, 16))
                dve.tensor_tensor(x1[:], x_keep[:], x1[:], ALU.add).then_inc(x1_ready.sem, 1)

            def stats_of_b(seg):
                dve.wait_ge(x1_ready.sem, seg.of(x1_ready, 1))
                stats(seg, b_stats, lambda t: x1[:, t, :], stats_b, mv_b)
                dve.wait_ge(b_stats.sem, seg.of(b_stats, 4))
                dve.tensor_scalar(v_b[:, 0, :], mv_b[:, :, 1], LN_EPS, None, ALU.add).then_inc(b_stats.sem, 1)
                dve.tensor_scalar(v_b[:, 1, :], mv_b[:, :, 1], 1.0 + EPS_B, EPS_B * LN_EPS, ALU.mult, ALU.add)\
                   .then_inc(b_stats.sem, 1)

            def layernorm_b(seg):
                dve.wait_ge(b_rstd.sem, seg.of(b_rstd, 1))
                dve.wait_ge(x2_head.sem, seg.scaled(1, seg.offset["A"]))
                for dst, a, done in ((h, 1, h_ready), (z, 0, z_ready)):
                    for t in range(TT):
                        dve.tensor_scalar(dst[:, t, :], x1[:, t, :], mv_b[:, t, 0:1], r_b[:, a, t:t + 1],
                                          ALU.subtract, ALU.mult).then_inc(done.sem, 1)

            def split_hT(seg):
                bank, slot = filled(seg, "hT")
                dve.wait_ge(hT_hi.sem, seg.of(hT_hi, 1))
                dve.tensor_tensor(hT[:, 1], bank[:, 0:T], hT[:, 0], ALU.subtract).then_inc(work_freed[slot], 1)

            def root_b(seg):
                dve.wait_ge(qk_squared.sem, seg.of(qk_squared, 1))
                dve.tensor_reduce(ss_b[:].rearrange("p t h -> p (t h)"),
                                  qk_sq[:].rearrange("p t a h d -> p (t a h) d"), X, ALU.add)\
                   .then_inc(qk_summed.sem, 1)
                dve.wait_ge(qk_summed.sem, seg.of(qk_summed, 1))
                dve.tensor_scalar(v_b2[:], ss_b[:], DB * EPS_B, None, ALU.add).then_inc(b_scale.sem, 1)
                root(seg, b_scale, 1, *[ap[:].rearrange("p t h -> p (t h)") for ap in (rr_b, v_b2, a_b2, y_b2)])

            def pads(seg):
                def head_rows(a):
                    return qk[:, :, a].rearrange("p t h d -> p t h d")

                def pad(ap, part):
                    return ap[:].rearrange("p (t h) s -> p t h s", t=TT)[:, :, :, part * DB:(part + 1) * DB]

                dve.wait_ge(qk_normed.sem, seg.of(qk_normed, 1))
                dve.tensor_copy(pad(k_pad, 0), head_rows(1)).then_inc(k_hi.sem, 1)
                dve.tensor_copy(pad(k_pad, 2), head_rows(1)).then_inc(k_hi.sem, 1)
                dve.wait_ge(k_hi.sem, seg.of(k_hi, 1))
                dve.tensor_tensor(pad(k_pad, 1), head_rows(1), pad(k_pad, 0), ALU.subtract).then_inc(k_lo.sem, 1)
                dve.wait_ge(q_weighted.sem, seg.of(q_weighted, 1))
                dve.tensor_copy(pad(q_pad, 0), head_rows(0)).then_inc(q_hi.sem, 1)
                dve.tensor_copy(pad(q_pad, 1), head_rows(0)).then_inc(q_hi.sem, 1)
                dve.wait_ge(q_hi.sem, seg.of(q_hi, 1))
                dve.tensor_tensor(pad(q_pad, 2), head_rows(0), pad(q_pad, 0), ALU.subtract).then_inc(q_lo.sem, 1)

            def outputs_b(seg):
                for t in range(TT):
                    bank, slot = filled(seg, f"oB{t}")
                    o = bank[:].rearrange("p (h s) -> p h s", h=HB)
                    dve.reciprocal(rden[:, t], o[:, :, DB]).then_inc(den_ready.sem, 1)
                    dve.wait_ge(den_ready.sem, seg.of(den_ready, t + 1))
                    dve.tensor_tensor(ao[:, t], o[:, :, 0:DB], rden[:, t].unsqueeze(2).broadcast_to([P, HB, DB]),
                                      ALU.mult).then_inc(work_freed[slot], 1)

            def residual_b(seg):
                for t in range(TT):
                    bank, slot = filled(seg, f"wo{t}")
                    dve.wait_ge(f_norm.sem, seg.of(f_norm, 0))
                    dve.wait_ge(z_ready.sem, seg.of(z_ready, TT))
                    dve.tensor_tensor(x2[:, t, MUTE:], bank[:, 0:D - MUTE], z[:, t, MUTE:], ALU.add)\
                       .then_inc(work_freed[slot], 1)

            def normalize_b(seg):
                dve.wait_ge(x2_squared.sem, seg.of(x2_squared, 1))
                dve.tensor_reduce(ss_f[:], x2_sq[:], X, ALU.add).then_inc(x2_summed.sem, 1)
                dve.wait_ge(x2_rms.sem, seg.of(x2_rms, 2))
                for t in range(TT):
                    dve.tensor_scalar(xf[:, t, :], x2[:, t, :], rs_f[:, t:t + 1], None, ALU.mult)\
                       .then_inc(xf_ready.sem, 1)

            def split_xfT(seg):
                bank, slot = filled(seg, "xfT")
                dve.wait_ge(xfT_hi.sem, seg.of(xfT_hi, 1))
                dve.tensor_tensor(xfT[:, 1], bank[:, 0:T], xfT[:, 0], ALU.subtract).then_inc(work_freed[slot], 1)

            def route(seg):
                bank, slot = filled(seg, "route")
                big = float(np.finfo(np.float32).max)
                dve.tensor_scalar(lg[:], bank[:, 0:TT * NE].rearrange("p (t e) -> p t e", t=TT), -big, big,
                                  ALU.max, ALU.min).then_inc(work_freed[slot], 1)
                dve.wait_ge(work_freed[slot], work_of(seg, "route")[2] + 1)
                dve.tensor_reduce(mx[:], lg[:], X, ALU.max).then_inc(route_max.sem, 2)

            def route_weights(seg):
                dve.wait_ge(route_exp.sem, seg.of(route_exp, 1))
                dve.tensor_reduce(es[:], ex[:], X, ALU.add).then_inc(route_dve.sem, 1)
                dve.wait_ge(route_dve.sem, seg.of(route_dve, 1))
                dve.reciprocal(er[:], es[:]).then_inc(route_dve.sem, 1)
                dve.wait_ge(route_dve.sem, seg.of(route_dve, 2))
                dve.tensor_tensor(pr[:], ex[:], er[:].unsqueeze(2).broadcast_to([P, TT, NE]), ALU.mult)\
                   .then_inc(route_dve.sem, 1)
                dve.wait_ge(route_dve.sem, seg.of(route_dve, 3))
                pj = pr[:].unsqueeze(2).broadcast_to([P, TT, NE, NE])
                pi = pr[:].unsqueeze(3).broadcast_to([P, TT, NE, NE])
                dve.tensor_tensor(gt[:], pj, pi, ALU.is_gt).then_inc(route_cmp.sem, 1)
                dve.tensor_tensor(ge[:], pj, pi, ALU.is_equal).then_inc(route_cmp.sem, 1)
                dve.wait_ge(route_cmp.sem, seg.of(route_cmp, 2))
                dve.tensor_tensor(ge[:], ge[:], before[:], ALU.mult).then_inc(route_cmp.sem, 1)
                dve.wait_ge(route_cmp.sem, seg.of(route_cmp, 3))
                dve.tensor_tensor(cnt[:], gt[:], ge[:], ALU.add).then_inc(route_cmp.sem, 1)
                dve.wait_ge(route_cmp.sem, seg.of(route_cmp, 4))
                dve.tensor_reduce(rank[:], cnt[:], X, ALU.add).then_inc(route_dve.sem, 1)
                dve.wait_ge(route_dve.sem, seg.of(route_dve, 4))
                dve.scalar_tensor_tensor(out=top[:], in0=rank[:], scalar=1.5, in1=pr[:], op0=ALU.is_lt,
                                         op1=ALU.mult).then_inc(route_sel.sem, 1)
                dve.wait_ge(route_sel.sem, seg.of(route_sel, 1))
                dve.tensor_reduce(tsum[:], top[:], X, ALU.add).then_inc(route_dve.sem, 1)
                dve.wait_ge(route_dve.sem, seg.of(route_dve, 5))
                dve.tensor_scalar(trec[:], tsum[:], 1e-8, None, ALU.add).then_inc(route_recip.sem, 1)
                dve.wait_ge(route_recip.sem, seg.of(route_recip, 1))
                dve.reciprocal(tsum[:], trec[:]).then_inc(route_recip.sem, 1)
                dve.wait_ge(route_recip.sem, seg.of(route_recip, 2))
                dve.tensor_tensor(wts[:], top[:], tsum[:].unsqueeze(2).broadcast_to([P, TT, NE]), ALU.mult)\
                   .then_inc(wts_ready.sem, 1)

            def lo_part(seg, dst, src, hi_ready):
                cols = dst.shape[2] * T
                dve.wait_ge(*hi_ready)
                dve.tensor_tensor(dst[:, 1].rearrange("p c t -> p (c t)"), src[:, 0:cols],
                                  dst[:, 0].rearrange("p c t -> p (c t)"), ALU.subtract).then_inc(hid_lo.sem, 1)

            gelus = ("e2a", "e3a", "e0", "e2b", "e2c", "e3b")

            def gelu_lo(name, dst):
                return "B", lambda s: lo_part(s, dst, gelu32[gelus.index(name) % 2], used(s, name))

            def swiglu(seg):
                bank, slot = filled(seg, "e1a")
                dve.wait_ge(tanh_b_ready.sem, seg.of(tanh_b_ready, 1))
                dve.scalar_tensor_tensor(out=tanh_b[:], in0=tanh_b[:], scalar=1.0, in1=bank[:], op0=ALU.add,
                                         op1=ALU.mult).then_inc(work_freed[slot], 1)
                bank, slot = filled(seg, "e1b")
                dve.wait_ge(*used(seg, "e1a"))
                dve.tensor_tensor(tanh_b[:], tanh_b[:], bank[:], ALU.mult).then_inc(work_freed[slot], 1)

            def swiglu_lo(seg):
                dve.wait_ge(*used(seg, "e1b"))
                lo_part(seg, h1, tanh_b, (hid_hi.sem, seg.of(hid_hi, 5)))

            def mix(seg, experts):
                if experts[0] == 0:
                    dve.wait_ge(wts_ready.sem, seg.of(wts_ready, 1))
                banks = [(filled(seg, f"down{t}") if experts[0] == 0 else work_of(seg, f"down{t}"))
                         for t in range(TT)]
                for e in experts:
                    for t in range(TT):
                        bank, slot = banks[t][:2]
                        if e > 0:
                            dve.wait_ge(mixed.sem, seg.of(mixed, (e - 1) * TT + t + 1))
                        acc = x2[:, t, MUTE:]
                        dve.scalar_tensor_tensor(out=acc, in0=bank[:, e * P:e * P + D - MUTE],
                                                 scalar=wts[:, t, e:e + 1], in1=acc, op0=ALU.mult,
                                                 op1=ALU.add)\
                           .then_inc(mixed.sem if e < NE - 1 else work_freed[slot], 1)

            def stats_of_out(seg):
                wait_used(dve, seg, [f"down{t}" for t in range(TT)])
                stats(seg, f_stats, lambda t: x2[:, t, :], stats_f, mv_f)

            def finish(seg):
                dve.wait_ge(f_rstd.sem, seg.of(f_rstd, 2))
                dve.wait_ge(f_stats.sem, seg.of(f_stats, 4))
                for t in range(TT):
                    dve.tensor_scalar(ex_out[:, t, :], x2[:, t, :], mv_f[:, t, 0:1], rs_x[:, t:t + 1],
                                      ALU.subtract, ALU.mult).then_inc(f_norm.sem, 1)
                dve.wait_ge(f_norm.sem, seg.of(f_norm, TT))
                dve.wait_ge(x1_copied.sem, seg.of(x1_copied, 1))
                dve.tensor_tensor(x1_keep[:], ex_out[:], x1_keep[:], ALU.add).then_inc(out_ready.sem, 1)

            def turn(name, dst, *units):
                return "A", lambda s: split_turned(s, name, dst, units)

            def copy(*pairs):
                return "A", lambda s: copy_o(s, pairs)

            run(dve, silu_kg("k00"), ("B", split_hT), ("X", stats_x), silu_kg("k01"),
                silu_kg("g00"), silu_kg("g01"), ("X", layernorm_x),
                ("A", lambda s: sum_qk(s, 0, "k")), ("A", lambda s: sum_qk(s, 0, "q")), silu_kg("k10"),
                ("B", root_b), silu_kg("k11"), ("B", pads), ("A", silu_v11), silu_kg("g10"),
                silu_kg("g11"), ("A", lambda s: sum_qk(s, 1, "q")), ("A", lambda s: sum_qk(s, 1, "k")),
                ("A", root_qk), ("X", split_xT), ("X", gates), turn("kT", kT, 0, 1, 2, 3), turn("qT", qT, 0, 1), ("B", outputs_b),
                turn("qT", qT, 2), copy(0), turn("qT", qT, 3), copy(1), ("B", residual_b),
                ("X", gates_log), copy(2), ("B", normalize_b), copy(3), ("X", split_cum), ("B", split_xfT), copy(4), ("B", route),
                ("A", lambda s: sum_o(s, 0)), copy(5, 6), ("B", route_weights), ("A", lambda s: sum_o(s, 1)),
                gelu_lo("e2a", h2a), copy(7),
                gelu_lo("e3a", h3a), gelu_lo("e0", h0), ("A", lambda s: sum_o(s, 2)), ("A", root_o),
                gelu_lo("e2b", h2b), silu_v(0), silu_v(1), ("B", swiglu), ("A", gate_o), silu_v(2), gelu_lo("e2c", h2c),
                turn("yT", yT, 0, 1, 2, 3), gelu_lo("e3b", h3b), ("B", swiglu_lo),
                ("A", stats_of_o), ("B", lambda s: mix(s, (0, 1))), ("A", layernorm_o), ("A", stats_of_b),
                ("B", lambda s: mix(s, (2, 3))), ("B", stats_of_out), ("A", layernorm_b), ("B", finish))

        @block.tensor
        def _(pe):
            pe.wait_ge(s_load, loads_total)
            pe.wait_ge(s_const, 1)
            for n, (srcs, _, _) in enumerate(groups):
                if n >= 2:
                    pe.wait_ge(s_trc, n - 1)
                bank, at_col = work_banks[n % 2], 0
                for _, rows, cols, src in srcs:
                    for c in range(cols // P):
                        for r in range(-(-rows // P)):
                            m = min(P, rows)
                            last = pe.transpose(bank[:, at_col:at_col + m], src[0:m, r, c * P:(c + 1) * P],
                                                ident[0:m, 0:m])
                            at_col += m
                last.then_inc(s_tr, 1)
            pe.wait_ge(s_init, 1)
            taken = {}

            def take(seg, name):
                ring = spare if name in spares_named else work
                order, n = ring.order[seg.name], taken.get((ring, seg.name), 0)
                assert order[n] == name, (seg.name, name, order[n])
                taken[ring, seg.name] = n + 1
                bank, slot, n = work_of(seg, name)
                pe.wait_ge(work_freed[slot], n)
                return bank, work_filled[slot]

            def turn(seg, name, src):
                bank, full = take(seg, name)
                for t in range(TT):
                    last = pe.transpose(bank[:, t * P:(t + 1) * P], src[:, t], ident[:])
                last.then_inc(full, 1)

            def turn_x(seg):
                pe.wait_ge(xn_ready.sem, seg.of(xn_ready, TT))
                turn(seg, "xT", xn)

            def three(out_ap, lhs, rhs, taps, start=True):
                n, total = 0, 3 * len(taps)
                for j in taps:
                    for a, b in ((0, 0), (0, 1), (1, 0)):
                        last = pe.matmul(out_ap, lhs(a, j), rhs(b, j), start=start and n == 0, stop=n == total - 1)
                        n += 1
                return last

            def x_cols(t, shift):
                return lambda a, j: (xh, xl)[a][:, t * P + shift + j:t * P + shift + j + P]

            def gate_logits(seg):
                bank, full = take(seg, "gate_logits")
                pe.wait_ge(xh_ready.sem, seg.of(xh_ready, 1))
                pe.wait_ge(*used(seg, "xT"))
                for t in range(TT):
                    last = three(bank[:, t * H:(t + 1) * H], x_cols(t, TAPS - 1), lambda b, j: wf[:, b, :], [0])
                last.then_inc(full, 1)

            def project(seg, names):
                for name in names:
                    m, t, lo = name[0], int(name[1]), int(name[2]) * HALF
                    bank, full = take(seg, name)
                    taps = list(range(TAPS)) if m in "kv" else [0]
                    three(bank[:], x_cols(t, 0 if m in "kv" else TAPS - 1),
                          lambda b, j: proj[m][:, b, j, lo:lo + HALF], taps).then_inc(full, 1)

            PARTS = ((0, 0), (1, 0), (0, 1))

            def cumulate(seg):
                bank, full = take(seg, "cum")
                pe.wait_ge(gate_log.sem, seg.of(gate_log, gate_log.per))
                pe.matmul(bank[0:H, 0:T], fl[:, 0, :], tri[:], start=True, stop=False)
                pe.matmul(bank[0:H, P:T], fl[:, 1, :], tri[:, 0:P], start=False, stop=True).then_inc(full, 1)

            def turn_heads(seg, name, src, units):
                for u in units:
                    bank, full = take(seg, f"{name}{u}")
                    for i in range(2):
                        for t in range(TT):
                            c = 2 * u + i
                            last = pe.transpose(bank[:, i * T + t * P:i * T + (t + 1) * P],
                                                src[:, t, c * P:(c + 1) * P], ident[:])
                    last.then_inc(full, 1)

            def turn_k(seg, units):
                pe.wait_ge(k_normed.sem, seg.of(k_normed, units[-1] // 2 + 1))
                turn_heads(seg, "kT", ks, units)

            def turn_q(seg, units):
                pe.wait_ge(q_normed.sem, seg.of(q_normed, units[-1] // 2 + 1))
                turn_heads(seg, "qT", qs, units)

            BLOCKS = ((slice(0, T), 0, slice(0, T)), (slice(T, T + P), 1, slice(P, T)))

            def scores_a(seg, p):
                slot, n = pair_ring.place(seg, f"A{p}")
                pe.wait_ge(probs_ready[slot], n)
                for i in range(2):
                    head, rows = 2 * p + i, slice(i * DH, (i + 1) * DH)
                    for cols, s, toks in BLOCKS:
                        dst = score_banks[slot][:, i, cols]
                        keys = slice(s * P, (s + 1) * P)
                        pe.matmul(dst, dec_k[:, head, keys], dec_q[:, head, toks], start=True, stop=False)
                        pe.matmul(score_banks[slot][:, i, cols.start:cols.start + P], identb[:], mask[:],
                                  start=False, stop=False)
                        for a, b in PARTS:
                            last = pe.matmul(dst, kT[a][rows, p, keys], qT[b][rows, p, toks], start=False,
                                             stop=(a, b) == PARTS[-1])
                return last.then_inc(scores_ready[slot], 1)

            def values(dst, pr, i, v):
                pe.matmul(dst, v(0), pr[:, i, 0:T], start=True, stop=False)
                return pe.matmul(dst[:, P:T], v(1), pr[:, i, T:T + P], start=False, stop=True)

            def values_a(seg, p):
                slot, n = pair_ring.place(seg, f"A{p}")
                pe.wait_ge(probs_ready[slot], n + 1)
                if p > 0:
                    pe.wait_ge(outT_a_ready.sem, seg.of(outT_a_ready, p))
                for i in range(2):
                    last = values(out_banks[0][0:DH + 1, i * T:(i + 1) * T], probs[slot], i,
                                  lambda s: vs[:, s, 2 * p + i, :])
                last.then_inc(probs_used[slot], 1)

            def turn_values(seg, p):
                pe.wait_ge(outT_a_ready.sem, seg.of(outT_a_ready, p + 1))
                if p > 0:
                    pe.wait_ge(o_copied.sem, seg.of(o_copied, p))
                bank = out_banks[1][:, 0:4 * (DH + 1)].rearrange("p (t h d) -> p t h d", t=TT, h=2)
                for t in range(TT):
                    for i in range(2):
                        last = pe.transpose(bank[:, t, i, :], outT_a[:, i * T + t * P:i * T + (t + 1) * P],
                                            ident[0:DH + 1, 0:DH + 1])
                last.then_inc(o_turned.sem, 1)

            def attention_a(seg, steps):
                if steps[0] == 0:
                    pe.wait_ge(decay_loaded.sem, seg.scaled(32, 32 * (seg.offset["A"] + 1)))
                for p in steps:
                    if p < PAIRS:
                        if p % 2 == 0:
                            wait_used(pe, seg, [f"{m}T{p // 2}" for m in "kq"])
                        scores_a(seg, p)
                    if p >= 2:
                        turn_values(seg, p - 2)
                    if 1 <= p <= PAIRS:
                        values_a(seg, p - 1)

            def turn_y(seg, units):
                pe.wait_ge(y_ready.sem, seg.of(y_ready, TT))
                turn_heads(seg, "yT", y, units)

            def output_a(seg):
                bank, full = take(seg, "attn_out")
                wait_used(pe, seg, [f"yT{u}" for u in range(4)])
                for t in range(TT):
                    for c in range(CT):
                        for a, b in PARTS:
                            last = pe.matmul(bank[:, t * D:(t + 1) * D], yT[a][:, c, t * P:(t + 1) * P],
                                             wo_a[:, b, c, :], start=c == 0 and (a, b) == PARTS[0],
                                             stop=c == CT - 1 and (a, b) == PARTS[-1])
                last.then_inc(full, 1)

            def turn_h(seg):
                pe.wait_ge(h_ready.sem, seg.of(h_ready, TT))
                turn(seg, "hT", h)

            def qkv_b(t):
                def stage(seg):
                    bank, full = take(seg, f"qkv{t}")
                    pe.wait_ge(*used(seg, "hT"))
                    for a, b in PARTS:
                        last = pe.matmul(bank[:, 0:3 * D], hT[:, a, t * P:(t + 1) * P], wqkv[:, b],
                                         start=(a, b) == PARTS[0], stop=(a, b) == PARTS[-1])
                    last.then_inc(full, 1)
                return "B", stage

            def turn_pads(seg):
                for name, src, ready in (("kpT", k_pad, k_lo), ("qpT", q_pad, q_lo)):
                    pe.wait_ge(ready.sem, seg.of(ready, 1))
                    bank, full = take(seg, name)
                    dst = bank[:].bitcast(F16)
                    for j in range(4):
                        for t in range(TT):
                            lo = t * HB + 4 * j
                            last = pe.transpose(dst[:, j * T + t * P:j * T + (t + 1) * P],
                                                src[:, lo:lo + 4, :].rearrange("p h s -> p (h s)"), ident16[:])
                    last.then_inc(full, 1)

            def scores_b(seg, p):
                slot, n = pair_ring.place(seg, f"B{p}")
                pe.wait_ge(probs_ready[slot], n)
                for i in range(2):
                    j, r = divmod(2 * p + i, 4)
                    rows = slice(r * SLOT, r * SLOT + 3 * DB)
                    for cols, s, toks in BLOCKS:
                        pe.matmul(score_banks[slot][:, i, cols], kTb[rows, j, s * P:(s + 1) * P], qTb[rows, j, toks],
                                  start=True, stop=False)
                        last = pe.matmul(score_banks[slot][:, i, cols.start:cols.start + P], identb[:], mask[:],
                                         start=False, stop=True)
                last.then_inc(scores_ready[slot], 1)

            def values_b(seg, p):
                slot, n = pair_ring.place(seg, f"B{p}")
                if p == 0:
                    wait_used(pe, seg, [n for n in ("g10", "g11") if n in spare.order[seg.name]])
                    pe.wait_ge(o_copied.sem, seg.scaled(PAIRS, PAIRS * (seg.offset["B"] + 1)))
                pe.wait_ge(probs_ready[slot], n + 1)
                for i in range(2):
                    head = 2 * p + i
                    g, j = divmod(head, 4)
                    dst = out_banks[g // 2][j * SLOT:(j + 1) * SLOT, (g % 2) * T:(g % 2 + 1) * T]
                    last = values(dst, probs[slot], i, lambda s: vb[:, s, head, :])
                last.then_inc(probs_used[slot], 1)

            def turn_values_b(seg):
                for t in range(TT):
                    bank, full = take(seg, f"oB{t}")
                    pe.wait_ge(outT_b_ready.sem, seg.of(outT_b_ready, 2))
                    for g in range(4):
                        last = pe.transpose(bank[:, g * P:(g + 1) * P], outT_b[:, g, t * P:(t + 1) * P], ident[:])
                    last.then_inc(full, 1)

            def attention_b(seg, steps):
                if steps[0] == 0:
                    wait_used(pe, seg, ["qpT", "kpT"])
                for p in steps:
                    if p < PAIRS:
                        scores_b(seg, p)
                    if p >= 1:
                        values_b(seg, p - 1)

            def turn_out(seg):
                wait_used(pe, seg, ["oB0", "oB1"])
                turn(seg, "aT", ao[:].rearrange("p t h d -> p t (h d)"))

            def output_b(seg):
                for t in range(TT):
                    bank, full = take(seg, f"wo{t}")
                    pe.wait_ge(*used(seg, "aT"))
                    pe.matmul(bank[:, 0:D - MUTE], aT[:, t * P:(t + 1) * P], wo_b[:, MUTE:], start=True, stop=True)\
                      .then_inc(full, 1)

            def layer(seg, name, weights, inputs, cols=HID):
                bank, full = take(seg, name)
                steps = [(k, a, b) for k in range(len(weights)) for a, b in PARTS]
                for m in range(cols // P):
                    for k, a, b in steps:
                        last = pe.matmul(bank[:, m * T:(m + 1) * T], weights[k][a][:, m * P:(m + 1) * P],
                                         inputs[k][b], start=(k, a, b) == steps[0], stop=(k, a, b) == steps[-1])
                last.then_inc(full, 1)

            def flat_pair(wt):
                return [[wt[:, 0], wt[:, 1]]]

            def tiled_pair(wt):
                return [[wt[:, a, k] for a in range(2)] for k in range(wt.shape[2])]

            def wait_lo(seg, name):
                pe.wait_ge(hid_lo.sem, seg.of(hid_lo, LO_PARTS.index(name) + 1))

            def turn_xf(seg):
                pe.wait_ge(xf_ready.sem, seg.of(xf_ready, TT))
                turn(seg, "xfT", xf)

            def route(seg):
                bank, full = take(seg, "route")
                pe.wait_ge(*used(seg, "xfT"))
                for t in range(TT):
                    for a, b in PARTS:
                        last = pe.matmul(bank[:, t * NE:(t + 1) * NE], xfT[:, a, t * P:(t + 1) * P], gate_w[:, b],
                                         start=(a, b) == PARTS[0], stop=(a, b) == PARTS[-1])
                last.then_inc(full, 1)

            def on_x(name, weights, cols=HID):
                return "B", lambda s: layer(s, name, flat_pair(weights), flat_pair(xfT), cols)

            def deeper(name, weights, before_it, inputs):
                def stage(seg):
                    wait_lo(seg, before_it)
                    layer(seg, name, tiled_pair(weights) if len(weights.shape) == 4 else flat_pair(weights),
                          tiled_pair(inputs))
                return "B", stage

            def experts_down(seg):
                wait_lo(seg, LO_PARTS[-1])
                steps = [(k, a, b) for k in range(2) for a, b in PARTS]
                for t in range(TT):
                    bank, full = take(seg, f"down{t}")
                    for e, hid in enumerate((h0, h1, h2c, h3b)):
                        for k, a, b in steps:
                            last = pe.matmul(bank[:, e * P:e * P + D - MUTE], hid[:, a, k, t * P:(t + 1) * P],
                                             downs[e][:, b, k, MUTE:], start=(k, a, b) == steps[0],
                                             stop=(k, a, b) == steps[-1])
                    last.then_inc(full, 1)

            def k_unit(*units):
                return "A", lambda s: turn_k(s, units)

            def q_unit(*units):
                return "A", lambda s: turn_q(s, units)

            def attend_a(*steps):
                return "A", lambda s: attention_a(s, steps)

            def attend_b(*steps):
                return "B", lambda s: attention_b(s, steps)

            def project_a(*names):
                return "A", lambda s: project(s, names)

            def project_v(n):
                def stage(seg):
                    if "A" in seg.offset:
                        pe.wait_ge(o_copied.sem, seg.of(o_copied, PAIRS))
                    project(seg, [V_UNITS[n]])
                return "X", stage

            def y_unit(*units):
                return "A", lambda s: turn_y(s, units)

            run(pe, project_a("q00", "k00"), ("B", turn_h), project_a("q01", "k01", "g00"), qkv_b(0),
                project_a("g01"), qkv_b(1),
                project_a("k10", "q10", "k11", "q11", "v11", "g10", "g11"), ("B", turn_pads), ("X", turn_x),
                attend_b(0, 1, 2, 3), ("X", gate_logits),
                k_unit(0), attend_b(4),
                k_unit(1), attend_b(5), k_unit(2), attend_b(6), k_unit(3), q_unit(0), attend_b(7), q_unit(1),
                attend_b(8), attend_a(0), ("B", turn_values_b), attend_a(1), q_unit(2), ("B", turn_out), attend_a(2),
                q_unit(3),
                attend_a(3), ("B", output_b), attend_a(4, 5), ("X", cumulate), ("B", turn_xf),
                attend_a(6), ("B", route), attend_a(7), on_x("e2a", l1), attend_a(8), on_x("e3a", e3d, P),
                attend_a(9), on_x("e0", up0), deeper("e2b", l2, "e2a", h2a), project_v(0), project_v(1),
                on_x("e1a", up1), on_x("e1b", up2), project_v(2), deeper("e2c", l3, "e2b", h2b),
                y_unit(0, 1, 2, 3), deeper("e3b", e3u, "e3a", h3a), ("A", output_a),
                ("B", experts_down))


_NAMES = ["x", "Wq", "Wk", "Wv", "Wo", "Wf", "bf", "Wg", "qnw", "knw", "onw", "kconv_w", "vconv_w"]
_FFN = ["n1_w", "n2_w", "wq", "wk", "wv", "wo", "qn_w", "kn_w", "gate_w", "e0_up", "e0_down", "e1_w1", "e1_w2",
        "e1_down", "e2_l1", "e2_l2", "e2_l3", "e2_l4", "e3_down", "e3_up", "e3_out"]


def kernel(**inputs):
    import numpy as _np
    import concourse.bacc as _bacc
    from concourse import mybir as _mybir
    from concourse.bass_utils import run_bass_kernel_spmd as _run

    nc = _bacc.Bacc("TRN2", target_bir_lowering=False, num_devices=1)
    arrays, args = {}, {}
    for prefix, names in (("L0_attn_", _NAMES), ("L0_ffn_", _FFN)):
        for name in names:
            a = _np.ascontiguousarray(inputs[prefix + name])
            arrays[f"in_{prefix}{name}"] = a
            args[name] = nc.dram_tensor(f"in_{prefix}{name}", a.shape, _mybir.dt.from_np(a.dtype),
                                        kind="ExternalInput").ap()
    x = args.pop("x")
    out = nc.dram_tensor("out_0", tuple(x.shape), F32, kind="ExternalOutput").ap()
    build(nc, x, args, out)
    r = _run(nc, [arrays], core_ids=[0])
    return r.results[0]["out_0"]
```
